# Optimizing a Trainium2 kernel written in Bass

```python
import numpy as np
import jax
import jax.numpy as jnp

def _softmax(x, axis=-1):
    return jax.nn.softmax(x, axis=axis)

def _gelu(x):
    return jax.nn.gelu(x, approximate=True)

def _silu(x):
    return jax.nn.silu(x)

def _sigmoid(x):
    return jax.nn.sigmoid(x)

def _layernorm(x, axis=-1, eps=1e-05):
    m = jnp.mean(x, axis=axis, keepdims=True)
    v = jnp.var(x, axis=axis, keepdims=True)
    return (x - m) / jnp.sqrt(v + eps)

def _scatter_add(tgt, idx, src, axis=0):
    return tgt.at[idx].add(src)

def _segment_sum(src, seg, n):
    return jax.ops.segment_sum(src, seg, n)
kernel_name = 'mk_metaformer_d2_conv_nchw256_r2_cfa984'

def setup_inputs(seed: int=0):
    np.random.seed(seed)
    _w = jnp.asarray

    def _rec_inputs():
        import jax
        import jax.numpy as jnp
        _gk = jax.random.key(seed)
        x = -0.000125 + 0.9999 * jax.random.normal(jax.random.fold_in(_gk, 1), (8, 128, 64, 64), jnp.float32)
        return x
    x = _rec_inputs()

    def _L0_conv_setup():
        import jax, jax.numpy as jnp
        import numpy as np
        B, C, H, W = (8, 128, 64, 64)
        K = 3
        GC = 16
        G = C // GC
        RED = 4
        CR = C // RED
        PAD = (K - 1) // 2

        def _forward(x, w1, b1, wd, bd, w2, b2):
            y = jnp.einsum('oc,bchw->bohw', w1, x) + b1[None, :, None, None]
            y = jax.lax.conv_general_dilated(y, wd, window_strides=(1, 1), padding=[(PAD, PAD), (PAD, PAD)], feature_group_count=CR, dimension_numbers=('NCHW', 'OIHW', 'NCHW')) + bd[None, :, None, None]
            w = jnp.einsum('oc,bchw->bohw', w2, y) + b2[None, :, None, None]
            w = w.reshape(B, G, K, K, H, W)
            xr = x.reshape(B, G, GC, H, W)
            xp = jnp.pad(xr, ((0, 0), (0, 0), (0, 0), (PAD, PAD), (PAD, PAD)))
            out = jnp.zeros((B, G, GC, H, W), dtype=x.dtype)
            for kh in range(K):
                for kw in range(K):
                    out = out + xp[:, :, :, kh:kh + H, kw:kw + W] * w[:, :, kh, kw][:, :, None, :, :]
            return out.reshape(B, C, H, W)
        key = jax.random.key(seed)
        ks = jax.random.split(key, 8)
        s = 0.05
        return {'x': jax.random.normal(ks[0], (B, C, H, W), dtype=jnp.float32), 'w1': jax.random.normal(ks[1], (CR, C), dtype=jnp.float32) * s, 'b1': jax.random.normal(ks[2], (CR,), dtype=jnp.float32) * s, 'wd': jax.random.normal(ks[3], (CR, 1, K, K), dtype=jnp.float32) * s, 'bd': jax.random.normal(ks[4], (CR,), dtype=jnp.float32) * s, 'w2': jax.random.normal(ks[5], (K * K * G, CR), dtype=jnp.float32) * s, 'b2': jax.random.normal(ks[6], (K * K * G,), dtype=jnp.float32) * s}
    _L0_conv_all = _L0_conv_setup()
    _L0_conv_in = {k: v for k, v in _L0_conv_all.items() if k in ('w1', 'b1', 'wd', 'bd', 'w2', 'b2')}
    del _L0_conv_all

    def _L0_ffn_setup():
        import jax, jax.numpy as jnp
        import numpy as np
        B, N, D = (16, 2048, 128)
        NUM_EXPERTS, TOP_K, HEADS = (4, 2, 4)
        N_EDGES = 524288
        LN_EPS = 1e-05

        def _layernorm(x, g, b):
            mu = x.mean(-1, keepdims=True)
            var = ((x - mu) ** 2).mean(-1, keepdims=True)
            return (x - mu) * jax.lax.rsqrt(var + LN_EPS) * g + b

        def _forward(x, edge_index, W_gat, att_src, att_dst, b_gat, ln_gamma, ln_beta, W1, b1, W2, b2):
            Bc, Nc, Dc = x.shape
            M = Bc * Nc
            x_flat = x.reshape(M, Dc)
            h = (x_flat @ W_gat).reshape(M, HEADS, NUM_EXPERTS)
            loops = jnp.arange(M, dtype=edge_index.dtype)
            src = jnp.concatenate([edge_index[0], loops])
            dst = jnp.concatenate([edge_index[1], loops])
            a_src = (h * att_src).sum(-1)
            a_dst = (h * att_dst).sum(-1)
            e = jax.nn.leaky_relu(a_src[src] + a_dst[dst], negative_slope=0.2)
            e_max = jax.ops.segment_max(e, dst, num_segments=M)
            ee = jnp.exp(e - e_max[dst])
            denom = jax.ops.segment_sum(ee, dst, num_segments=M)
            alpha = ee / (denom[dst] + 1e-16)
            msg = h[src] * alpha[:, :, None]
            agg = jax.ops.segment_sum(msg, dst, num_segments=M).reshape(M, HEADS * NUM_EXPERTS) + b_gat
            scores = _layernorm(agg, ln_gamma, ln_beta).reshape(M, HEADS, NUM_EXPERTS).mean(1)
            scores = scores.reshape(Bc, Nc, NUM_EXPERTS)
            topk_s, topk_i = jax.lax.top_k(scores, TOP_K)
            w = jax.nn.softmax(topk_s, axis=-1)
            out = jnp.zeros_like(x)
            for ei in range(NUM_EXPERTS):
                g = jnp.where(topk_i == ei, w, 0.0).sum(-1)
                hh = jax.nn.gelu(x @ W1[ei] + b1[ei], approximate=False)
                out = out + g[..., None] * (hh @ W2[ei] + b2[ei])
            return out
        key = jax.random.key(seed)
        ks = jax.random.split(key, 8)
        s = 0.05
        return {'x': jax.random.normal(ks[0], (B, N, D), jnp.float32), 'W_gat': jax.random.normal(ks[1], (D, HEADS * NUM_EXPERTS), jnp.float32) * s, 'att_src': jax.random.normal(ks[2], (HEADS, NUM_EXPERTS), jnp.float32) * s, 'att_dst': jax.random.normal(ks[3], (HEADS, NUM_EXPERTS), jnp.float32) * s, 'b_gat': jnp.zeros((HEADS * NUM_EXPERTS,), jnp.float32), 'ln_gamma': jnp.ones((HEADS * NUM_EXPERTS,), jnp.float32), 'ln_beta': jnp.zeros((HEADS * NUM_EXPERTS,), jnp.float32), 'W1': jax.random.normal(ks[4], (NUM_EXPERTS, D, 2 * D), jnp.float32) * s, 'b1': jnp.zeros((NUM_EXPERTS, 2 * D), jnp.float32), 'W2': jax.random.normal(ks[5], (NUM_EXPERTS, 2 * D, D), jnp.float32) * s, 'b2': jnp.zeros((NUM_EXPERTS, D), jnp.float32), 'edge_index': jax.random.randint(ks[6], (2, N_EDGES), 0, B * N, jnp.int32)}
    _L0_ffn_all = _L0_ffn_setup()
    _L0_ffn_in = {k: v for k, v in _L0_ffn_all.items() if k in ('W_gat', 'att_src', 'att_dst', 'b_gat', 'ln_gamma', 'ln_beta', 'W1', 'b1', 'W2', 'b2', 'edge_index')}
    del _L0_ffn_all

    def _L1_conv_setup():
        import jax, jax.numpy as jnp
        import numpy as np
        B0, CIN, Hh, Ww = (8, 128, 48, 48)
        SPLIT = 8
        DM = CIN // SPLIT
        EXPAND = 2
        DIN = EXPAND * DM
        DSTATE = 32
        DCONV = 3
        HEADDIM = 8
        NH = DIN // HEADDIM
        DOUT = 128
        CHUNK = 32
        D_IN_PROJ = 2 * DIN + 2 * DSTATE + NH
        CONV_CH = DIN + 2 * DSTATE

        def _layernorm(x, w, b, eps=1e-05):
            mu = jnp.mean(x, -1, keepdims=True)
            xc = x - mu
            var = jnp.mean(xc * xc, -1, keepdims=True)
            return xc * jax.lax.rsqrt(var + eps) * w + b

        def _ssd(x, A, Bm, Cm, chunk):
            b, l, h, p = x.shape
            n = Bm.shape[-1]
            nc = l // chunk
            xc = x.reshape(b, nc, chunk, h, p)
            Ac = A.reshape(b, nc, chunk, h).transpose(0, 3, 1, 2)
            Bc = Bm.reshape(b, nc, chunk, n)
            Cc = Cm.reshape(b, nc, chunk, n)
            ac = jnp.cumsum(Ac, -1)
            seg = ac[..., :, None] - ac[..., None, :]
            mask = jnp.tril(jnp.ones((chunk, chunk), bool))
            L = jnp.where(mask, jnp.exp(jnp.where(mask, seg, 0.0)), 0.0)
            Yd = jnp.einsum('bcln,bcsn,bhcls,bcshp->bclhp', Cc, Bc, L, xc)
            decay_states = jnp.exp(ac[..., -1:] - ac)
            states = jnp.einsum('bcln,bhcl,bclhp->bchpn', Bc, decay_states, xc)
            chunk_decay = jnp.exp(ac[..., -1])

            def step(carry, inp):
                s, d = inp
                return (carry * d[..., None, None] + s, carry)
            states_t = jnp.moveaxis(states, 1, 0)
            dec_t = jnp.moveaxis(chunk_decay, 2, 0)
            _, prev = jax.lax.scan(step, jnp.zeros_like(states_t[0]), (states_t, dec_t))
            prev = jnp.moveaxis(prev, 0, 1)
            Yo = jnp.einsum('bcln,bchpn,bhcl->bclhp', Cc, prev, jnp.exp(ac))
            return (Yd + Yo).reshape(b, l, h, p)

        def _mamba2(u, W_in, conv_w, conv_b, dt_bias, A_log, D, rms_w, W_out):
            b, l, _ = u.shape
            zxbcdt = u @ W_in
            z = zxbcdt[..., :DIN]
            xBC = zxbcdt[..., DIN:DIN + CONV_CH]
            dt = jax.nn.softplus(zxbcdt[..., -NH:] + dt_bias)
            conv = jax.lax.conv_general_dilated(xBC.transpose(0, 2, 1), conv_w, (1,), [(DCONV - 1, 0)], dimension_numbers=('NCH', 'OIH', 'NCH'), feature_group_count=CONV_CH)
            xBC = jax.nn.silu(conv + conv_b[None, :, None]).transpose(0, 2, 1)
            xs = xBC[..., :DIN].reshape(b, l, NH, HEADDIM)
            Bm = xBC[..., DIN:DIN + DSTATE]
            Cm = xBC[..., DIN + DSTATE:]
            A = -jnp.exp(A_log)
            y = _ssd(xs * dt[..., None], dt * A, Bm, Cm, CHUNK)
            y = y + xs * D[None, None, :, None]
            y = y.reshape(b, l, DIN) * jax.nn.silu(z)
            y = y * jax.lax.rsqrt(jnp.mean(y * y, -1, keepdims=True) + 1e-05) * rms_w
            return y @ W_out
        key = jax.random.key(seed)
        ks = jax.random.split(key, 10)
        x = jax.random.normal(ks[0], (B0, CIN, Hh, Ww), jnp.float32)
        inp = {'x': x, 'ln_w': jnp.ones((CIN,), jnp.float32), 'ln_b': jnp.zeros((CIN,), jnp.float32), 'skip_scale': jnp.ones((1,), jnp.float32), 'proj_w': jax.random.normal(ks[1], (CIN, DOUT), jnp.float32) / np.sqrt(CIN), 'proj_b': jnp.zeros((DOUT,), jnp.float32), 'W_in': jax.random.normal(ks[2], (DM, D_IN_PROJ), jnp.float32) / np.sqrt(DM), 'conv_w': jax.random.normal(ks[3], (CONV_CH, 1, DCONV), jnp.float32) * 0.3, 'conv_b': jnp.zeros((CONV_CH,), jnp.float32), 'dt_bias': jax.random.normal(ks[4], (NH,), jnp.float32) * 0.5, 'A_log': jnp.log(jnp.arange(1.0, NH + 1.0, dtype=jnp.float32)), 'D': jax.random.normal(ks[5], (NH,), jnp.float32) * 0.5, 'rms_w': jnp.ones((DIN,), jnp.float32), 'W_out': jax.random.normal(ks[6], (DIN, DM), jnp.float32) / np.sqrt(DIN)}
        return inp
    _L1_conv_all = _L1_conv_setup()
    _L1_conv_in = {k: v for k, v in _L1_conv_all.items() if k in ('ln_w', 'ln_b', 'skip_scale', 'proj_w', 'proj_b', 'W_in', 'conv_w', 'conv_b', 'dt_bias', 'A_log', 'D', 'rms_w', 'W_out')}
    del _L1_conv_all

    def _L1_ffn_setup():
        import jax, jax.numpy as jnp
        import numpy as np
        B, N, D = (16, 2048, 128)
        NUM_EXPERTS, TOP_K, HEADS = (4, 2, 4)
        N_EDGES = 524288
        LN_EPS = 1e-05

        def _layernorm(x, g, b):
            mu = x.mean(-1, keepdims=True)
            var = ((x - mu) ** 2).mean(-1, keepdims=True)
            return (x - mu) * jax.lax.rsqrt(var + LN_EPS) * g + b

        def _forward(x, edge_index, W_gat, att_src, att_dst, b_gat, ln_gamma, ln_beta, W1, b1, W2, b2):
            Bc, Nc, Dc = x.shape
            M = Bc * Nc
            x_flat = x.reshape(M, Dc)
            h = (x_flat @ W_gat).reshape(M, HEADS, NUM_EXPERTS)
            loops = jnp.arange(M, dtype=edge_index.dtype)
            src = jnp.concatenate([edge_index[0], loops])
            dst = jnp.concatenate([edge_index[1], loops])
            a_src = (h * att_src).sum(-1)
            a_dst = (h * att_dst).sum(-1)
            e = jax.nn.leaky_relu(a_src[src] + a_dst[dst], negative_slope=0.2)
            e_max = jax.ops.segment_max(e, dst, num_segments=M)
            ee = jnp.exp(e - e_max[dst])
            denom = jax.ops.segment_sum(ee, dst, num_segments=M)
            alpha = ee / (denom[dst] + 1e-16)
            msg = h[src] * alpha[:, :, None]
            agg = jax.ops.segment_sum(msg, dst, num_segments=M).reshape(M, HEADS * NUM_EXPERTS) + b_gat
            scores = _layernorm(agg, ln_gamma, ln_beta).reshape(M, HEADS, NUM_EXPERTS).mean(1)
            scores = scores.reshape(Bc, Nc, NUM_EXPERTS)
            topk_s, topk_i = jax.lax.top_k(scores, TOP_K)
            w = jax.nn.softmax(topk_s, axis=-1)
            out = jnp.zeros_like(x)
            for ei in range(NUM_EXPERTS):
                g = jnp.where(topk_i == ei, w, 0.0).sum(-1)
                hh = jax.nn.gelu(x @ W1[ei] + b1[ei], approximate=False)
                out = out + g[..., None] * (hh @ W2[ei] + b2[ei])
            return out
        key = jax.random.key(seed)
        ks = jax.random.split(key, 8)
        s = 0.05
        return {'x': jax.random.normal(ks[0], (B, N, D), jnp.float32), 'W_gat': jax.random.normal(ks[1], (D, HEADS * NUM_EXPERTS), jnp.float32) * s, 'att_src': jax.random.normal(ks[2], (HEADS, NUM_EXPERTS), jnp.float32) * s, 'att_dst': jax.random.normal(ks[3], (HEADS, NUM_EXPERTS), jnp.float32) * s, 'b_gat': jnp.zeros((HEADS * NUM_EXPERTS,), jnp.float32), 'ln_gamma': jnp.ones((HEADS * NUM_EXPERTS,), jnp.float32), 'ln_beta': jnp.zeros((HEADS * NUM_EXPERTS,), jnp.float32), 'W1': jax.random.normal(ks[4], (NUM_EXPERTS, D, 2 * D), jnp.float32) * s, 'b1': jnp.zeros((NUM_EXPERTS, 2 * D), jnp.float32), 'W2': jax.random.normal(ks[5], (NUM_EXPERTS, 2 * D, D), jnp.float32) * s, 'b2': jnp.zeros((NUM_EXPERTS, D), jnp.float32), 'edge_index': jax.random.randint(ks[6], (2, N_EDGES), 0, B * N, jnp.int32)}
    _L1_ffn_all = _L1_ffn_setup()
    _L1_ffn_in = {k: v for k, v in _L1_ffn_all.items() if k in ('W_gat', 'att_src', 'att_dst', 'b_gat', 'ln_gamma', 'ln_beta', 'W1', 'b1', 'W2', 'b2', 'edge_index')}
    del _L1_ffn_all
    return {'x': x, 'L0_conv_w1': _L0_conv_in['w1'], 'L0_conv_b1': _L0_conv_in['b1'], 'L0_conv_wd': _L0_conv_in['wd'], 'L0_conv_bd': _L0_conv_in['bd'], 'L0_conv_w2': _L0_conv_in['w2'], 'L0_conv_b2': _L0_conv_in['b2'], 'L0_ffn_W_gat': _L0_ffn_in['W_gat'], 'L0_ffn_att_src': _L0_ffn_in['att_src'], 'L0_ffn_att_dst': _L0_ffn_in['att_dst'], 'L0_ffn_b_gat': _L0_ffn_in['b_gat'], 'L0_ffn_ln_gamma': _L0_ffn_in['ln_gamma'], 'L0_ffn_ln_beta': _L0_ffn_in['ln_beta'], 'L0_ffn_W1': _L0_ffn_in['W1'], 'L0_ffn_b1': _L0_ffn_in['b1'], 'L0_ffn_W2': _L0_ffn_in['W2'], 'L0_ffn_b2': _L0_ffn_in['b2'], 'L0_ffn_edge_index': _L0_ffn_in['edge_index'], 'L1_conv_ln_w': _L1_conv_in['ln_w'], 'L1_conv_ln_b': _L1_conv_in['ln_b'], 'L1_conv_skip_scale': _L1_conv_in['skip_scale'], 'L1_conv_proj_w': _L1_conv_in['proj_w'], 'L1_conv_proj_b': _L1_conv_in['proj_b'], 'L1_conv_W_in': _L1_conv_in['W_in'], 'L1_conv_conv_w': _L1_conv_in['conv_w'], 'L1_conv_conv_b': _L1_conv_in['conv_b'], 'L1_conv_dt_bias': _L1_conv_in['dt_bias'], 'L1_conv_A_log': _L1_conv_in['A_log'], 'L1_conv_D': _L1_conv_in['D'], 'L1_conv_rms_w': _L1_conv_in['rms_w'], 'L1_conv_W_out': _L1_conv_in['W_out'], 'L1_ffn_W_gat': _L1_ffn_in['W_gat'], 'L1_ffn_att_src': _L1_ffn_in['att_src'], 'L1_ffn_att_dst': _L1_ffn_in['att_dst'], 'L1_ffn_b_gat': _L1_ffn_in['b_gat'], 'L1_ffn_ln_gamma': _L1_ffn_in['ln_gamma'], 'L1_ffn_ln_beta': _L1_ffn_in['ln_beta'], 'L1_ffn_W1': _L1_ffn_in['W1'], 'L1_ffn_b1': _L1_ffn_in['b1'], 'L1_ffn_W2': _L1_ffn_in['W2'], 'L1_ffn_b2': _L1_ffn_in['b2'], 'L1_ffn_edge_index': _L1_ffn_in['edge_index']}

def reference(x, L0_conv_w1, L0_conv_b1, L0_conv_wd, L0_conv_bd, L0_conv_w2, L0_conv_b2, L0_ffn_W_gat, L0_ffn_att_src, L0_ffn_att_dst, L0_ffn_b_gat, L0_ffn_ln_gamma, L0_ffn_ln_beta, L0_ffn_W1, L0_ffn_b1, L0_ffn_W2, L0_ffn_b2, L0_ffn_edge_index, L1_conv_ln_w, L1_conv_ln_b, L1_conv_skip_scale, L1_conv_proj_w, L1_conv_proj_b, L1_conv_W_in, L1_conv_conv_w, L1_conv_conv_b, L1_conv_dt_bias, L1_conv_A_log, L1_conv_D, L1_conv_rms_w, L1_conv_W_out, L1_ffn_W_gat, L1_ffn_att_src, L1_ffn_att_dst, L1_ffn_b_gat, L1_ffn_ln_gamma, L1_ffn_ln_beta, L1_ffn_W1, L1_ffn_b1, L1_ffn_W2, L1_ffn_b2, L1_ffn_edge_index):
    import jax
    import jax.numpy as jnp

    def _L0_conv_ref(x, w1, b1, wd, bd, w2, b2):
        import jax, jax.numpy as jnp
        import numpy as np
        B, C, H, W = (8, 128, 64, 64)
        K = 3
        GC = 16
        G = C // GC
        RED = 4
        CR = C // RED
        PAD = (K - 1) // 2

        def _forward(x, w1, b1, wd, bd, w2, b2):
            y = jnp.einsum('oc,bchw->bohw', w1, x) + b1[None, :, None, None]
            y = jax.lax.conv_general_dilated(y, wd, window_strides=(1, 1), padding=[(PAD, PAD), (PAD, PAD)], feature_group_count=CR, dimension_numbers=('NCHW', 'OIHW', 'NCHW')) + bd[None, :, None, None]
            w = jnp.einsum('oc,bchw->bohw', w2, y) + b2[None, :, None, None]
            w = w.reshape(B, G, K, K, H, W)
            xr = x.reshape(B, G, GC, H, W)
            xp = jnp.pad(xr, ((0, 0), (0, 0), (0, 0), (PAD, PAD), (PAD, PAD)))
            out = jnp.zeros((B, G, GC, H, W), dtype=x.dtype)
            for kh in range(K):
                for kw in range(K):
                    out = out + xp[:, :, :, kh:kh + H, kw:kw + W] * w[:, :, kh, kw][:, :, None, :, :]
            return out.reshape(B, C, H, W)
        return _forward(x, w1, b1, wd, bd, w2, b2)

    def _L0_ffn_ref(x, W_gat, att_src, att_dst, b_gat, ln_gamma, ln_beta, W1, b1, W2, b2, edge_index):
        import jax, jax.numpy as jnp
        import numpy as np
        B, N, D = (16, 2048, 128)
        NUM_EXPERTS, TOP_K, HEADS = (4, 2, 4)
        N_EDGES = 524288
        LN_EPS = 1e-05

        def _layernorm(x, g, b):
            mu = x.mean(-1, keepdims=True)
            var = ((x - mu) ** 2).mean(-1, keepdims=True)
            return (x - mu) * jax.lax.rsqrt(var + LN_EPS) * g + b

        def _forward(x, edge_index, W_gat, att_src, att_dst, b_gat, ln_gamma, ln_beta, W1, b1, W2, b2):
            Bc, Nc, Dc = x.shape
            M = Bc * Nc
            x_flat = x.reshape(M, Dc)
            h = (x_flat @ W_gat).reshape(M, HEADS, NUM_EXPERTS)
            loops = jnp.arange(M, dtype=edge_index.dtype)
            src = jnp.concatenate([edge_index[0], loops])
            dst = jnp.concatenate([edge_index[1], loops])
            a_src = (h * att_src).sum(-1)
            a_dst = (h * att_dst).sum(-1)
            e = jax.nn.leaky_relu(a_src[src] + a_dst[dst], negative_slope=0.2)
            e_max = jax.ops.segment_max(e, dst, num_segments=M)
            ee = jnp.exp(e - e_max[dst])
            denom = jax.ops.segment_sum(ee, dst, num_segments=M)
            alpha = ee / (denom[dst] + 1e-16)
            msg = h[src] * alpha[:, :, None]
            agg = jax.ops.segment_sum(msg, dst, num_segments=M).reshape(M, HEADS * NUM_EXPERTS) + b_gat
            scores = _layernorm(agg, ln_gamma, ln_beta).reshape(M, HEADS, NUM_EXPERTS).mean(1)
            scores = scores.reshape(Bc, Nc, NUM_EXPERTS)
            topk_s, topk_i = jax.lax.top_k(scores, TOP_K)
            w = jax.nn.softmax(topk_s, axis=-1)
            out = jnp.zeros_like(x)
            for ei in range(NUM_EXPERTS):
                g = jnp.where(topk_i == ei, w, 0.0).sum(-1)
                hh = jax.nn.gelu(x @ W1[ei] + b1[ei], approximate=False)
                out = out + g[..., None] * (hh @ W2[ei] + b2[ei])
            return out
        return _forward(x, edge_index, W_gat, att_src, att_dst, b_gat, ln_gamma, ln_beta, W1, b1, W2, b2)

    def _L1_conv_ref(x, ln_w, ln_b, skip_scale, proj_w, proj_b, W_in, conv_w, conv_b, dt_bias, A_log, D, rms_w, W_out):
        import jax, jax.numpy as jnp
        import numpy as np
        B0, CIN, Hh, Ww = (8, 128, 48, 48)
        SPLIT = 8
        DM = CIN // SPLIT
        EXPAND = 2
        DIN = EXPAND * DM
        DSTATE = 32
        DCONV = 3
        HEADDIM = 8
        NH = DIN // HEADDIM
        DOUT = 128
        CHUNK = 32
        D_IN_PROJ = 2 * DIN + 2 * DSTATE + NH
        CONV_CH = DIN + 2 * DSTATE

        def _layernorm(x, w, b, eps=1e-05):
            mu = jnp.mean(x, -1, keepdims=True)
            xc = x - mu
            var = jnp.mean(xc * xc, -1, keepdims=True)
            return xc * jax.lax.rsqrt(var + eps) * w + b

        def _ssd(x, A, Bm, Cm, chunk):
            b, l, h, p = x.shape
            n = Bm.shape[-1]
            nc = l // chunk
            xc = x.reshape(b, nc, chunk, h, p)
            Ac = A.reshape(b, nc, chunk, h).transpose(0, 3, 1, 2)
            Bc = Bm.reshape(b, nc, chunk, n)
            Cc = Cm.reshape(b, nc, chunk, n)
            ac = jnp.cumsum(Ac, -1)
            seg = ac[..., :, None] - ac[..., None, :]
            mask = jnp.tril(jnp.ones((chunk, chunk), bool))
            L = jnp.where(mask, jnp.exp(jnp.where(mask, seg, 0.0)), 0.0)
            Yd = jnp.einsum('bcln,bcsn,bhcls,bcshp->bclhp', Cc, Bc, L, xc)
            decay_states = jnp.exp(ac[..., -1:] - ac)
            states = jnp.einsum('bcln,bhcl,bclhp->bchpn', Bc, decay_states, xc)
            chunk_decay = jnp.exp(ac[..., -1])

            def step(carry, inp):
                s, d = inp
                return (carry * d[..., None, None] + s, carry)
            states_t = jnp.moveaxis(states, 1, 0)
            dec_t = jnp.moveaxis(chunk_decay, 2, 0)
            _, prev = jax.lax.scan(step, jnp.zeros_like(states_t[0]), (states_t, dec_t))
            prev = jnp.moveaxis(prev, 0, 1)
            Yo = jnp.einsum('bcln,bchpn,bhcl->bclhp', Cc, prev, jnp.exp(ac))
            return (Yd + Yo).reshape(b, l, h, p)

        def _mamba2(u, W_in, conv_w, conv_b, dt_bias, A_log, D, rms_w, W_out):
            b, l, _ = u.shape
            zxbcdt = u @ W_in
            z = zxbcdt[..., :DIN]
            xBC = zxbcdt[..., DIN:DIN + CONV_CH]
            dt = jax.nn.softplus(zxbcdt[..., -NH:] + dt_bias)
            conv = jax.lax.conv_general_dilated(xBC.transpose(0, 2, 1), conv_w, (1,), [(DCONV - 1, 0)], dimension_numbers=('NCH', 'OIH', 'NCH'), feature_group_count=CONV_CH)
            xBC = jax.nn.silu(conv + conv_b[None, :, None]).transpose(0, 2, 1)
            xs = xBC[..., :DIN].reshape(b, l, NH, HEADDIM)
            Bm = xBC[..., DIN:DIN + DSTATE]
            Cm = xBC[..., DIN + DSTATE:]
            A = -jnp.exp(A_log)
            y = _ssd(xs * dt[..., None], dt * A, Bm, Cm, CHUNK)
            y = y + xs * D[None, None, :, None]
            y = y.reshape(b, l, DIN) * jax.nn.silu(z)
            y = y * jax.lax.rsqrt(jnp.mean(y * y, -1, keepdims=True) + 1e-05) * rms_w
            return y @ W_out
        Bn, C, h, w = x.shape
        L = h * w
        xf = x.reshape(Bn, C, L).transpose(0, 2, 1)
        xn = _layernorm(xf, ln_w, ln_b)
        d = C // SPLIT
        xs = jnp.moveaxis(xn.reshape(Bn, L, SPLIT, d), 2, 0)
        xs = xs.reshape(SPLIT * Bn, L, d)
        ym = _mamba2(xs, W_in, conv_w, conv_b, dt_bias, A_log, D, rms_w, W_out)
        ym = ym + skip_scale * xs
        ym = jnp.moveaxis(ym.reshape(SPLIT, Bn, L, d), 0, 2).reshape(Bn, L, C)
        ym = _layernorm(ym, ln_w, ln_b)
        out = ym @ proj_w + proj_b
        return out.transpose(0, 2, 1).reshape(Bn, DOUT, h, w)

    def _L1_ffn_ref(x, W_gat, att_src, att_dst, b_gat, ln_gamma, ln_beta, W1, b1, W2, b2, edge_index):
        import jax, jax.numpy as jnp
        import numpy as np
        B, N, D = (16, 2048, 128)
        NUM_EXPERTS, TOP_K, HEADS = (4, 2, 4)
        N_EDGES = 524288
        LN_EPS = 1e-05

        def _layernorm(x, g, b):
            mu = x.mean(-1, keepdims=True)
            var = ((x - mu) ** 2).mean(-1, keepdims=True)
            return (x - mu) * jax.lax.rsqrt(var + LN_EPS) * g + b

        def _forward(x, edge_index, W_gat, att_src, att_dst, b_gat, ln_gamma, ln_beta, W1, b1, W2, b2):
            Bc, Nc, Dc = x.shape
            M = Bc * Nc
            x_flat = x.reshape(M, Dc)
            h = (x_flat @ W_gat).reshape(M, HEADS, NUM_EXPERTS)
            loops = jnp.arange(M, dtype=edge_index.dtype)
            src = jnp.concatenate([edge_index[0], loops])
            dst = jnp.concatenate([edge_index[1], loops])
            a_src = (h * att_src).sum(-1)
            a_dst = (h * att_dst).sum(-1)
            e = jax.nn.leaky_relu(a_src[src] + a_dst[dst], negative_slope=0.2)
            e_max = jax.ops.segment_max(e, dst, num_segments=M)
            ee = jnp.exp(e - e_max[dst])
            denom = jax.ops.segment_sum(ee, dst, num_segments=M)
            alpha = ee / (denom[dst] + 1e-16)
            msg = h[src] * alpha[:, :, None]
            agg = jax.ops.segment_sum(msg, dst, num_segments=M).reshape(M, HEADS * NUM_EXPERTS) + b_gat
            scores = _layernorm(agg, ln_gamma, ln_beta).reshape(M, HEADS, NUM_EXPERTS).mean(1)
            scores = scores.reshape(Bc, Nc, NUM_EXPERTS)
            topk_s, topk_i = jax.lax.top_k(scores, TOP_K)
            w = jax.nn.softmax(topk_s, axis=-1)
            out = jnp.zeros_like(x)
            for ei in range(NUM_EXPERTS):
                g = jnp.where(topk_i == ei, w, 0.0).sum(-1)
                hh = jax.nn.gelu(x @ W1[ei] + b1[ei], approximate=False)
                out = out + g[..., None] * (hh @ W2[ei] + b2[ei])
            return out
        return _forward(x, edge_index, W_gat, att_src, att_dst, b_gat, ln_gamma, ln_beta, W1, b1, W2, b2)

    def _gn(v, G=32, eps=1e-05):
        B_, C_, H_, W_ = v.shape
        g = v.reshape(B_, G, C_ // G, H_, W_)
        m = jnp.mean(g, axis=(2, 3, 4), keepdims=True)
        s = jnp.var(g, axis=(2, 3, 4), keepdims=True)
        return ((g - m) / jnp.sqrt(s + eps)).reshape(v.shape)

    def _ln_c(v, eps=1e-06):
        m = jnp.mean(v, axis=1, keepdims=True)
        s = jnp.var(v, axis=1, keepdims=True)
        return (v - m) / jnp.sqrt(s + eps)

    def _ln_t(v, eps=1e-05):
        m = jnp.mean(v, axis=-1, keepdims=True)
        s = jnp.var(v, axis=-1, keepdims=True)
        return (v - m) / jnp.sqrt(s + eps)

    def _to_tokens(v):
        B_, C_, H_, W_ = v.shape
        return v.reshape(B_, C_, H_ * W_).transpose(0, 2, 1)

    def _from_tokens(t, like):
        B_, C_, H_, W_ = like.shape
        return t.transpose(0, 2, 1).reshape(B_, C_, H_, W_)
    x = x + _L0_conv_ref(_ln_c(x), L0_conv_w1, L0_conv_b1, L0_conv_wd, L0_conv_bd, L0_conv_w2, L0_conv_b2)
    t = _to_tokens(x)
    t = t + _L0_ffn_ref(_ln_t(t), L0_ffn_W_gat, L0_ffn_att_src, L0_ffn_att_dst, L0_ffn_b_gat, L0_ffn_ln_gamma, L0_ffn_ln_beta, L0_ffn_W1, L0_ffn_b1, L0_ffn_W2, L0_ffn_b2, L0_ffn_edge_index)
    x = _from_tokens(t, x)
    x = x + _L1_conv_ref(_ln_c(x), L1_conv_ln_w, L1_conv_ln_b, L1_conv_skip_scale, L1_conv_proj_w, L1_conv_proj_b, L1_conv_W_in, L1_conv_conv_w, L1_conv_conv_b, L1_conv_dt_bias, L1_conv_A_log, L1_conv_D, L1_conv_rms_w, L1_conv_W_out)
    t = _to_tokens(x)
    t = t + _L1_ffn_ref(_ln_t(t), L1_ffn_W_gat, L1_ffn_att_src, L1_ffn_att_dst, L1_ffn_b_gat, L1_ffn_ln_gamma, L1_ffn_ln_beta, L1_ffn_W1, L1_ffn_b1, L1_ffn_W2, L1_ffn_b2, L1_ffn_edge_index)
    x = _from_tokens(t, x)
    return x

_drawn_inputs = setup_inputs


def setup_inputs(seed=0):
    import zlib

    import numpy as np

    out = dict(_drawn_inputs(seed))
    spreads = {'L0_ffn_b_gat': (0.0, 0.1),
     'L0_ffn_ln_gamma': (1.0, 0.2),
     'L0_ffn_ln_beta': (0.0, 0.1),
     'L0_ffn_b1': (0.0, 0.1),
     'L0_ffn_b2': (0.0, 0.1),
     'L1_conv_ln_w': (1.0, 0.2),
     'L1_conv_ln_b': (0.0, 0.1),
     'L1_conv_proj_b': (0.0, 0.1),
     'L1_conv_conv_b': (0.0, 0.1),
     'L1_conv_rms_w': (1.0, 0.2),
     'L1_ffn_b_gat': (0.0, 0.1),
     'L1_ffn_ln_gamma': (1.0, 0.2),
     'L1_ffn_ln_beta': (0.0, 0.274),
     'L1_ffn_b1': (0.0, 0.35),
     'L1_ffn_b2': (0.0, 0.1)}
    factors = {'L0_conv_b1': 4.559, 'L1_ffn_att_src': 4.001, 'L1_ffn_att_dst': 16.839}
    for name, (base, spread) in spreads.items():
        noise = np.random.default_rng([zlib.crc32(name.encode()), seed]).standard_normal(out[name].shape)
        drawn = base * np.exp(spread * noise) if base else spread * noise
        out[name] = jnp.asarray(drawn.astype(out[name].dtype))
    for name, factor in factors.items():
        out[name] = (out[name] * factor).astype(out[name].dtype)
    return out
```

```python
import numpy as np
import concourse.bass as bass
from concourse import mybir
from contextlib import ExitStack

f32=mybir.dt.float32; u32=mybir.dt.uint32; i32=mybir.dt.int32; bf16=mybir.dt.bfloat16
ALU=mybir.AluOpType; ACT=mybir.ActivationFunctionType; AX=mybir.AxisListType
P=128; NODES=32768; B=8; TOK=4096; T=512; TILES=NODES//T; TPI=TOK//T
W=64; ROWS=T//W
LEAD=2

class Flag:
    def __init__(self, sem): self.sem=sem
    def start(self, eng): eng.sem_inc(self.sem, LEAD)
    def of(self, eng, i): eng.wait_ge(self.sem, i+LEAD+1)
    def before(self, eng, i, buffers): eng.wait_ge(self.sem, i+LEAD+1-buffers)

class Room:
    def __init__(self, nc, ctx, tag): self.nc,self.ctx,self.tag=nc,ctx,tag; self.sems=[]
    def sb(self,n,s,d=f32): return self.ctx.enter_context(self.nc.sbuf_tensor(f"{self.tag}_{n}",s,d))
    def pb(self,n,s,d=f32): return self.ctx.enter_context(self.nc.psum_tensor(f"{self.tag}_{n}",s,d))
    def sem(self,n): return self.nc.alloc_semaphore(f"{self.tag}_{n}")
    def flags(self,names): return [Flag(self.sem(n)) for n in names.split()]
    def pair(self,n): return [self.sem(f"{n}0"),self.sem(f"{n}1")]

def landed(eng, sems, i, par):
    eng.wait_ge(sems[par], (i-par)*8+16)
class Stores:
    def __init__(self, room, name): self.sems=room.pair(name); self.done,=room.flags(name+"_done")
    def start(self, eng): self.done.start(eng)
    def landed(self, eng, i, par):
        landed(eng,self.sems,i,par)
        eng.sem_inc(self.done.sem,1)

class Rows:
    def __init__(self, room, name, half):
        self.half=half; self.sems=[[room.sem(f"{name}{par}{k}") for k in range(2)] for par in range(2)]
    def of(self, k, par): return self.sems[par][k%2]
    def wait(self, eng, turns, par):
        for s in self.sems[par]: eng.wait_ge(s, turns*(8*self.half))

def paired(eng, n, body, peel=False):
    if peel: body(0,0); body(1,1)
    with eng.Fori(1 if peel else 0,n//2) as t:
        body(t*2,0); body(t*2+1,1)

def skewed(eng, n, ahead, body):
    ahead(0,0)
    with eng.Fori(0,n//2-1) as t:
        ahead(t*2+1,1); body(t*2,0); ahead(t*2+2,0); body(t*2+1,1)
    ahead(n-1,1); body(n-2,0); body(n-1,1)

class Norm:
    def __init__(self, nc, room, name, mean_w, eps, source, arrived, dest, dest_free):
        self.nc,self.eps,self.mean_w=nc,eps,mean_w
        self.source,self.arrived,self.dest,self.dest_free=source,arrived,dest,dest_free
        self.cen=room.sb(name+"_cen",[P,2,T]); self.sq=room.sb(name+"_sq",[P,2,T]); self.log=room.sb(name+"_log",[P,2,T]); self.rstd=room.sb(name+"_rstd",[P,2,T]); self.logged,=room.flags(name+"_logged")
        self.mean=room.pb(name+"_mean",[P,T]); self.var=room.pb(name+"_var",[P,T])
        self.averaged,self.centred,self.squared,self.spread,self.scaled,self.normed=room.flags(
            " ".join(name+"_"+s for s in ("averaged","centred","squared","spread","scaled","normed")))
    def pe_start(self,pe): self.averaged.start(pe); self.spread.start(pe)
    def dve_start(self,dve): self.centred.start(dve); self.normed.start(dve)
    def act_start(self,act): self.squared.start(act); self.scaled.start(act); self.logged.start(act)
    def pe_mean(self,pe,i,par):
        self.arrived(pe,i,par)
        self.centred.before(pe,i,1)
        self.nc.tensor.matmul(self.mean[:,:],self.mean_w,self.source(i,par),start=True,stop=True).then_inc(self.averaged.sem,1)
    def pe_var(self,pe,i,par):
        self.squared.of(pe,i)
        self.logged.before(pe,i,1)
        self.nc.tensor.matmul(self.var[:,:],self.mean_w,self.sq[:,par,:],start=True,stop=True).then_inc(self.spread.sem,1)
    def dve_centre(self,dve,i,par):
        self.averaged.of(dve,i)
        self.normed.before(dve,i,2)
        self.squared.before(dve,i,2)
        self.nc.vector.tensor_tensor(self.cen[:,par,:],self.source(i,par),self.mean[:,:],ALU.subtract).then_inc(self.centred.sem,1)
    def act_square(self,act,i,par):
        self.centred.of(act,i)
        self.spread.before(act,i,2)
        self.nc.scalar.activation(self.sq[:,par,:],self.cen[:,par,:],ACT.Square).then_inc(self.squared.sem,1)
    def act_root(self,act,i,par):
        self.spread.of(act,i)
        self.normed.before(act,i,2)
        self.nc.scalar.activation(self.log[:,par,:],self.var[:,:],ACT.Ln,bias=self.eps).then_inc(self.logged.sem,1)
        self.logged.of(act,i)
        self.nc.scalar.activation(self.rstd[:,par,:],self.log[:,par,:],ACT.Exp,scale=-0.5).then_inc(self.scaled.sem,1)
    def dve_scale(self,dve,i,par):
        self.scaled.of(dve,i)
        self.dest_free(dve,i,par)
        self.nc.vector.tensor_tensor(self.dest(i,par),self.cen[:,par,:],self.rstd[:,par,:],ALU.mult).then_inc(self.normed.sem,1)

def lagged(eng, n, stages, base=0, last_first=False):
    depth=len(stages); k0=(depth-1)+(depth-1)%2
    order=list(enumerate(stages))[::-1 if last_first else 1]
    def step(k, par):
        for j,stage in order:
            if isinstance(k,int) and not 0<=k-j<n: continue
            i=k-j if isinstance(base,int) and base==0 else base+(k-j)
            stage(i,(par-j)%2)
    for k in range(k0): step(k,k%2)
    with eng.Fori(0,(n-k0)//2) as t:
        step(t*2+k0,0); step(t*2+k0+1,1)
    for k in range(n,n+depth-1): step(k,k%2)

E=524288; LO=128; HI=256; COLS=E//P; S=4; SRING=8; SLOTS=4; SHALF=64; FIRST_TURNS=20

def sort_edges(nc, edges, placed_dram, start_dram, deg_dram, beside, tag='s'):
    TURNS=COLS//SRING; GROUPS=COLS//S
    with ExitStack() as ctx:
        ctx.enter_context(nc.cleanup_on_exit())
        sb=lambda n,s,d: ctx.enter_context(nc.sbuf_tensor(tag+n,s,d))
        pb=lambda n,s,d: ctx.enter_context(nc.psum_tensor(tag+n,s,d))
        sem=lambda n: nc.alloc_semaphore(tag+n)
        ei=sb("s_ei",[P,2,COLS],i32)
        rec=sb("s_rec",[P,COLS,3],i32)
        part=sb("s_part",[P,COLS],i32)
        lo=sb("s_lo",[P,COLS],f32); hi=sb("s_hi",[P,COLS],f32)
        iota_i=sb("s_iotai",[P,HI],i32); iota=sb("s_iota",[P,HI],bf16)
        pid_i=sb("s_pidi",[P,P],i32); ident=sb("s_ident",[P,P],bf16); identf=sb("s_identf",[P,P],f32)
        tri=sb("s_tri",[P,P],f32); zeros=sb("s_zeros",[P,2*HI],bf16)
        hots=sb("s_hots",[P,S,SLOTS,LO+HI],bf16); olo=hots[:,:,:,0:LO]; ohi=hots[:,:,:,LO:LO+HI]; dist=sb("s_dist",[P,2,LO+HI],bf16)
        oloT=sb("s_oloT",[P,S,P],bf16); oloTf=sb("s_oloTf",[P,2,S,P],f32)
        same=sb("s_same",[P,2,S,P],bf16)
        cnt=sb("s_cnt",[P,S,HI],f32)
        deg=sb("s_deg",[P,HI],f32); incl=sb("s_incl",[P,HI],f32); start=sb("s_start",[P,HI],f32)
        base=sb("s_base",[P,S,HI],f32); zf=sb("s_zf",[P,HI],f32); zcol=sb("s_zcol",[P,1],f32)
        prod=sb("s_prod",[P,S,HI],f32); posf=sb("s_posf",[P,SRING],f32)
        neg=sb("s_neg",[P,4,P],bf16)
        cntP=pb("s_cntP",[P,S,HI],f32)
        TP=pb("s_TP",[P,S,P],bf16); AP_=pb("s_AP",[P,S,P],f32); PP=pb("s_PP",[P,S,HI],f32)
        edges_in=sem("edges_in"); iotas=sem("iotas"); consts=sem("consts"); prep=sem("prep")
        hot_c=sem("hot_c"); hot_a=sem("hot_a"); measured=sem("measured"); keyed=sem("keyed"); counted=sem("counted"); zeroed=sem("zeroed")
        tot=sem("tot"); offs=sem("offs"); based=sem("based"); tables_out=sem("tables_out"); seeded=sem("seeded"); seedcopied=sem("seedcopied")
        hot=sem("hot"); turned=sem("turned"); turnedc=sem("turnedc"); turnedf=sem("turnedf"); pairs=sem("pairs"); masked=sem("masked"); ranks=sem("ranks"); updated=sem("updated"); cnt_copied=sem("cnt_copied"); placed=sem("placed"); posready=sem("posready"); gate=sem("gate"); reccop=sem("reccop")
        chunk_out=sem("chunk_out"); chunks=sem("chunks")
        beside_sync,beside_pool=beside(Room(nc,ctx,tag),chunks)
        block=ctx.enter_context(nc.Block())

        @block.sync
        def _(sp):
            sp.dma_start(ei[:,:,:], edges.rearrange("a (p c) -> p a c", p=P)).then_inc(edges_in,16)
            if beside_sync: beside_sync(sp)
            sp.wait_ge(based,1)
            sp.dma_start(start_dram, start[:,:]).then_inc(tables_out,16)
            sp.dma_start(deg_dram, deg[:,:]).then_inc(tables_out,16)
            sp.wait_ge(tables_out,32)
            with sp.Fori(0,COLS//SHALF) as k:
                sp.wait_ge(posready,k*(SHALF//S)+SHALF//S)
                sp.dma_start(placed_dram[:,bass.ds(k*SHALF,SHALF),:],rec[:,bass.ds(k*SHALF,SHALF),:]).then_inc(chunk_out,16)
                sp.wait_ge(chunk_out,k*16+16)
                sp.sem_inc(chunks,1)

        @block.gpsimd
        def _(pool):
            pool.iota(iota_i[:,:], pattern=[[1,HI]], base=0, channel_multiplier=0).then_inc(iotas,1)
            pool.iota(pid_i[:,:], pattern=[[1,P]], base=0, channel_multiplier=-1).then_inc(iotas,1)
            beside_pool(pool)

        def onehots(dve,c,slot,par,done):
            nc.vector.tensor_scalar(olo[:,slot,par,:], iota[:,0:LO], lo[:,bass.ds(c,1)], None, ALU.is_equal)
            nc.vector.tensor_scalar(ohi[:,slot,par,:], iota[:,:], hi[:,bass.ds(c,1)], None, ALU.is_equal).then_inc(done,1)

        @block.vector
        def _(dve):
            dve.wait_ge(iotas,2)
            nc.vector.tensor_copy(iota[:,:],iota_i[:,:])
            nc.vector.tensor_scalar(ident[:,:],pid_i[:,:],0,None,ALU.is_equal)
            nc.vector.tensor_scalar(identf[:,:],pid_i[:,:],0,None,ALU.is_equal)
            nc.vector.tensor_scalar(tri[:,:],pid_i[:,:],0,None,ALU.is_gt)
            for s in range(4): nc.vector.tensor_scalar(neg[:,s,:],pid_i[:,:],0,-1.0,ALU.is_le,ALU.mult)
            nc.vector.memset(zf[:,:],0.0)
            nc.vector.memset(zcol[:,:],0.0)
            nc.vector.memset(zeros[:,:],0.0).then_inc(consts,1)
            dve.wait_ge(edges_in,16)
            nc.vector.tensor_copy(rec[:,:,0],ei[:,0,:])
            nc.vector.tensor_copy(rec[:,:,1],ei[:,1,:])
            nc.vector.tensor_single_scalar(part[:,:],ei[:,1,:],8,ALU.logical_shift_right).then_inc(prep,1)
            dve.wait_ge(prep,1)
            nc.vector.tensor_copy(lo[:,:],part[:,:]).then_inc(prep,1)
            dve.wait_ge(prep,2)
            nc.vector.tensor_single_scalar(part[:,:],ei[:,1,:],HI-1,ALU.bitwise_and).then_inc(prep,1)
            dve.wait_ge(prep,3)
            nc.vector.tensor_copy(hi[:,:],part[:,:]).then_inc(prep,1)
            dve.wait_ge(prep,4)
            dve.wait_ge(consts,1)
            dve.sem_inc(keyed,1)
            def count(i,par):
                if not isinstance(i,int): dve.wait_ge(counted,i-1)
                for s in range(S-1): onehots(dve,i*S+s,s,par,hot_c)
            paired(dve,2*TURNS,count,peel=True)
            dve.wait_ge(counted,TURNS*2)
            nc.vector.tensor_copy(cnt[:,:,:],cntP[:,:,:]).then_inc(tot,1)
            dve.wait_ge(tot,1)
            nc.vector.tensor_tensor(deg[:,:],cnt[:,0,:],cnt[:,1,:],ALU.add).then_inc(tot,1)
            for s in range(2,S):
                dve.wait_ge(tot,s)
                nc.vector.tensor_tensor(deg[:,:],deg[:,:],cnt[:,s,:],ALU.add).then_inc(tot,1)
            dve.wait_ge(tot,S)
            nc.vector.tensor_tensor_scan(incl[:,:],deg[:,:],zf[:,:],0.0,ALU.add,ALU.add).then_inc(tot,1)
            dve.wait_ge(offs,1)
            dve.wait_ge(tot,S+1)
            nc.vector.scalar_tensor_tensor(start[:,:],incl[:,:],PP[:,0,0:1],deg[:,:],ALU.add,ALU.subtract).then_inc(based,1)
            dve.wait_ge(based,1)
            nc.vector.tensor_copy(base[:,0,:],start[:,:]).then_inc(based,1)
            for s in range(1,S):
                dve.wait_ge(based,s+1)
                nc.vector.tensor_tensor(base[:,s,:],base[:,s-1,:],cnt[:,s-1,:],ALU.add).then_inc(based,1)
            def hots_of(g,slot):
                for s in range(S): onehots(dve,g*S+s,s,slot,hot)
            for g in range(3): hots_of(g,g)
            def group(g,slot,next_hots=True):
                par=slot%2
                def places(h):
                    dve.wait_ge(ranks,g*2+h+1)
                    for s in (2*h,2*h+1):
                        nc.vector.tensor_tensor_reduce(out=prod[:,s,:],in0=PP[:,s,:],in1=ohi[:,s,slot,:],scale=1.0,scalar=0.0,op0=ALU.mult,op1=ALU.add,accum_out=posf[:,par*S+s:par*S+s+1]).then_inc(placed,1)
                places(0)
                places(1)
                if next_hots:
                    if not (isinstance(g,int) and g==0): dve.wait_ge(updated,g*2)
                    hots_of(g+3,(slot+3)%SLOTS)
                dve.wait_ge(placed,g*S+S)
                nc.vector.tensor_copy(rec[:,bass.ds(g*S,S),2],posf[:,par*S:par*S+S]).then_inc(posready,1)
            for j in range(SLOTS): group(j,j)
            with dve.Fori(1,GROUPS//SLOTS-1) as u:
                for j in range(SLOTS): group(u*SLOTS+j,j)
            for j in range(SLOTS): group(GROUPS-SLOTS+j,j,next_hots=j<1)

        @block.scalar
        def _(act):
            def copy_cnt(h):
                nc.scalar.copy(cnt[:,2*h:2*h+2,:],cntP[:,2*h:2*h+2,:]).then_inc(cnt_copied,1)
            def copy_turned(par):
                nc.scalar.copy(oloT[:,:,:],TP[:,:,:]).then_inc(turnedc,1)
                nc.scalar.copy(oloTf[:,par,:,:],TP[:,:,:]).then_inc(turnedf,1)
            def mask(g,par):
                act.wait_ge(pairs,g+1)
                nc.scalar.activation(same[:,par,:,:],AP_[:,:,:],ACT.Relu).then_inc(masked,1)
            act.wait_ge(keyed,1)
            def count(i,par):
                c=i*S+(S-1)
                nc.scalar.activation(dist[:,par,0:LO],iota[:,0:LO],ACT.Square,scale=-1.0,bias=lo[:,bass.ds(c,1)])
                nc.scalar.activation(dist[:,par,LO:LO+HI],iota[:,:],ACT.Square,scale=-1.0,bias=hi[:,bass.ds(c,1)]).then_inc(measured,1)
                act.wait_ge(measured,i+1)
                if not isinstance(i,int): act.wait_ge(counted,i-1)
                nc.scalar.activation(hots[:,S-1,par,:],dist[:,par,:],ACT.Relu,scale=-1.0,bias=1.0).then_inc(hot_a,1)
            paired(act,2*TURNS,count,peel=True)
            for h in range(2):
                act.wait_ge(seeded,h+1)
                copy_cnt(h)
            act.wait_ge(turned,1)
            copy_turned(0)
            mask(0,0)
            def group(g,par):
                act.wait_ge(turned,g+2)
                act.wait_ge(pairs,g+1)
                copy_turned(1-par)
                act.wait_ge(updated,g*2+1)
                copy_cnt(0)
                mask(g+1,1-par)
                act.wait_ge(updated,g*2+2)
                copy_cnt(1)
            with act.Fori(0,TURNS-1) as t:
                group(t*2,0)
                group(t*2+1,1)
            group(GROUPS-2,0)

        @block.tensor
        def _(pe):
            pe.wait_ge(consts,1)
            for b in range(2):
                nc.tensor.matmul(cntP[:,2*b:2*b+2,:],zeros[:,0:P],zeros[:,:],start=True,stop=False,skip_group_check=True)
            def count(i,par):
                for s in range(S):
                    if s<S-1: pe.wait_ge(hot_c,i*(S-1)+s+1)
                    else: pe.wait_ge(hot_a,i+1)
                    last=nc.tensor.matmul(cntP[:,s,:],olo[:,s,par,:],ohi[:,s,par,:],start=False,stop=False,skip_group_check=True)
                last.then_inc(counted,1)
            paired(pe,2*TURNS,count)
            pe.wait_ge(tot,S+1)
            nc.tensor.matmul(PP[:,0,0:1],tri[:,:],incl[:,HI-1:HI],start=True,stop=True).then_inc(offs,1)
            pe.wait_ge(based,S+1)
            for b in range(2):
                nc.tensor.matmul(cntP[:,2*b:2*b+2,:],identf[:,:],base[:,2*b:2*b+2,:],start=True,stop=False,skip_group_check=True).then_inc(seeded,1)
            def turn_hots(g,slot):
                pe.wait_ge(hot,g*S+S)
                if not (isinstance(g,int) and g==0): pe.wait_ge(turnedf,g)
                for s in range(S):
                    last=nc.tensor.transpose(TP[:,s,:],olo[:,s,slot,:],ident[:,:])
                last.then_inc(turned,1)
            def pair_up(g):
                pe.wait_ge(turnedc,g+1)
                nc.tensor.matmul(AP_[:,:,:],ident[:,:],neg[:,:,:],start=True,stop=False,skip_group_check=True)
                for s in range(S):
                    last=nc.tensor.matmul(AP_[:,s,:],oloT[:,s,:],oloT[:,s,:],start=False,stop=True,skip_group_check=True)
                last.then_inc(pairs,1)
            turn_hots(0,0)
            pair_up(0)
            def look_up(g,slot,h,first):
                par=slot%2
                pe.wait_ge(cnt_copied,g*2+h+1)
                pe.wait_ge(turnedf,g+1)
                if not first: pe.wait_ge(placed,g*S-S+2*h+2)
                for s in (2*h,2*h+1):
                    nc.tensor.matmul(PP[:,s,:],oloTf[:,par,s,:],cnt[:,s,:],start=(s==2*h),stop=False,skip_group_check=True)
                pe.wait_ge(masked,g+1)
                for s in (2*h,2*h+1):
                    last=nc.tensor.matmul(PP[:,s,:],same[:,par,s,:],ohi[:,s,slot,:],start=False,stop=True,skip_group_check=True)
                last.then_inc(ranks,1)
                for s in (2*h,2*h+1):
                    last=nc.tensor.matmul(cntP[:,s,:],olo[:,s,slot,:],ohi[:,s,slot,:],start=False,stop=False,skip_group_check=True)
                last.then_inc(updated,1)
            def group(g,slot,first=False,nxt=True):
                if nxt: turn_hots(g+1,(slot+1)%SLOTS)
                look_up(g,slot,0,first)
                if nxt: pair_up(g+1)
                look_up(g,slot,1,first)
            for j in range(SLOTS): group(j,j,first=j==0)
            with pe.Fori(1,GROUPS//SLOTS-1) as u:
                for j in range(SLOTS): group(u*SLOTS+j,j)
            for j in range(SLOTS): group(GROUPS-SLOTS+j,j,nxt=j<3)

class Scatter:
    def __init__(self, nc, room, placed, rec, t0, t1, chunks=None):
        self.nc,self.placed,self.rec,self.t0,self.t1,self.chunks=nc,placed,rec,t0,t1,chunks
        self.ring=room.sb("ring",[P,2,SHALF,3],i32)
        self.ring_in=room.pair("ring_in"); self.sent=Rows(room,"sent",SHALF); self.gate=room.sem("sgate")
    def load(self, pool, i, par):
        if self.chunks is not None: pool.wait_ge(self.chunks,i+(self.t0*2+1))
        pool.dma_start(self.ring[:,par,:,:],self.placed[:,bass.ds((i+self.t0*2)*SHALF,SHALF),:]).then_inc(self.ring_in[par],16)
    def send(self, pool, par, lo, hi):
        for k in range(lo,hi):
            pool.indirect_dma_start(self.rec,bass.IndirectOffsetOnAxis(ap=self.ring[:,par,k,2:3],axis=0),self.ring[:,par,k,0:2],None).then_inc(self.sent.of(k,par),16)
    def pool(self, pool):
        def half(t,par,first=False,last=False):
            pool.wait_ge(self.ring_in[par],t*16+16)
            pool.sem_inc(self.gate,1)
            self.send(pool,par,0,SHALF//2)
            if not last:
                if not first: self.sent.wait(pool,t+par,1-par)
                self.load(pool,t*2+(par+1),1-par)
            self.send(pool,par,SHALF//2,SHALF)
        n=self.t1-self.t0
        self.load(pool,0,0)
        half(0,0,first=True)
        with pool.Fori(0,n-1) as t:
            half(t,1); half(t+1,0)
        half(n-1,1,last=True)
        for par in range(2): self.sent.wait(pool,n,par)


RED=32; GK=72; PADW=W+2
def involution(nc, x, w1, b1, wd, w2, bd, b2, pick, ones, x_out, beside=None, tag="c"):
    with ExitStack() as ctx:
        ctx.enter_context(nc.cleanup_on_exit())
        r=Room(nc,ctx,tag)
        img=[r.sb(f"img{k}",[P,TOK]) for k in range(2)]
        xn=[r.sb(f"xn{k}",[P,PADW,PADW]) for k in range(2)]
        y=[r.sb(f"y{k}",[96,PADW,PADW]) for k in range(2)]
        mw=r.sb("mw",[P,P]); w1s=r.sb("w1",[P,96]); b1s=r.sb("b1",[96,1]); wds=r.sb("wd",[96,3]); w2s=r.sb("w2",[96,GK])
        bds=r.sb("bd",[RED,1]); b2s=r.sb("b2",[GK,1]); picks=r.sb("pick",[GK,9,P]); wk=r.sb("wk",[96,3,GK]); bias=r.sb("bias",[GK,1]); eps=r.sb("eps",[P,1])
        kern=r.sb("kern",[GK,2,T]); prod=r.sb("prod",[P,3,T]); acc=r.sb("acc",[P,2,T])
        yP=r.pb("yP",[96,T]); kP=r.pb("kP",[GK,T]); eP=[r.pb(f"eP{k}",[P,T]) for k in range(3)]
        w_in=r.sem("w_in"); w_ready=r.sem("w_ready"); folded=r.sem("folded")
        img_in=r.pair("img_in"); out=Stores(r,"out")
        squeezed,padded,kernels,biased,added=r.flags("squeezed padded kernels biased added")
        spreadk=r.sem("spread_k"); times=r.sem("times"); summed=r.sem("summed"); image_used=r.sem("image_used"); edges=r.sem("edges")
        pars=[0]
        def src(i,par): return None
        block=ctx.enter_context(nc.Block())
        class N2(Norm): pass
        nm=N2(nc,r,"n",mw[:,:],eps[:,0:1],None,None,None,None)
        def images(eng, body):
            with eng.Fori(0,B//2) as t:
                for ip in range(2): body(t*2+ip, ip)
        @block.sync
        def _(sp):
            for d,s in ((mw[:,:],ones),(w1s[:,:],w1),(b1s[:,:],b1),(wds[:,:],wd),(w2s[:,:],w2),(bds[:,:],bd),(b2s[:,:],b2),(picks[:,:,:],pick)):
                sp.dma_start(d,s).then_inc(w_in,16)
            out.start(sp)
            def load(b,ip): sp.dma_start(img[ip][:,:],x[:,bass.ds(b*TOK,TOK)]).then_inc(img_in[ip],16)
            load(0,0); load(1,1)
            def stores(b,ip):
                def store(j,par):
                    i=b*TPI+j
                    sp.wait_ge(summed,i*9+9)
                    sp.dma_start(x_out[:,bass.ds(i*T,T)],acc[:,par,:]).then_inc(out.sems[par],16)
                    out.landed(sp,i,par)
                paired(sp,TPI,store)
            with sp.Fori(0,B//2-1) as t:
                for ip in range(2):
                    stores(t*2+ip,ip)
                    sp.wait_ge(image_used,t*2+ip+1)
                    load(t*2+ip+2,ip)
            for ip in range(2): stores(B-2+ip,ip)
        def bind(ip):
            nm.source=lambda i,par: img[ip][:,bass.ds(cur['j']*T,T)]
        cur={}
        def tiles(eng,b,ip,ahead,body):
            def call(f,j,par):
                cur['j']=j
                bind(ip)
                nm.arrived=lambda e,i,p: None
                nm.dest=lambda i,p: xn[ip][:,bass.ds(cur['j']*ROWS+1,ROWS),1:W+1]
                nm.dest_free=lambda e,i,p: None
                f(b*TPI+j,j,par,ip)
            if ahead is None:
                with eng.Fori(0,TPI//2) as jj:
                    call(body,jj*2,0); call(body,jj*2+1,1)
                return
            call(ahead,0,0)
            with eng.Fori(0,TPI//2-1) as jj:
                call(ahead,jj*2+1,1); call(body,jj*2,0); call(ahead,jj*2+2,0); call(body,jj*2+1,1)
            call(ahead,TPI-1,1); call(body,TPI-2,0); call(body,TPI-1,1)
        @block.tensor
        def _(pe):
            nm.pe_start(pe); squeezed.start(pe); kernels.start(pe)
            pe.wait_ge(w_in,16*8)
            nc.tensor.matmul(kP[:,0:1],w2s[0:RED,:],bds[:,:],start=True,stop=True).then_inc(folded,1)
            pe.wait_ge(w_ready,1)
            pe.wait_ge(edges,1)
            def image(b,ip):
                pe.wait_ge(img_in[ip],(b-ip)*8+16)
                def var_and_squeeze(i,j,par,ip):
                    nm.pe_var(pe,i,par)
                    nm.normed.of(pe,i)
                    padded.before(pe,i,1)
                    nc.tensor.matmul(yP[:,:],w1s[:,:],xn[ip][:,bass.ds(j*ROWS+1,ROWS),1:W+1],start=True,stop=True).then_inc(squeezed.sem,1)
                tiles(pe,b,ip,lambda i,j,par,ip: nm.pe_mean(pe,i,par),var_and_squeeze)
                padded.of(pe,b*TPI+TPI-1)
                def kernel_of(i,j,par,ip):
                    biased.before(pe,i,1)
                    for kh in range(3):
                        last=nc.tensor.matmul(kP[:,:],wk[:,kh,:],y[ip][:,bass.ds(j*ROWS+kh,ROWS),1:W+1],start=(kh==0),stop=(kh==2))
                    last.then_inc(kernels.sem,1)
                def spread(i,j,par,ip):
                    biased.of(pe,i)
                    for k in range(9):
                        pe.wait_ge(times,i*9+k+1)
                        nc.tensor.matmul(eP[k%3][:,:],picks[:,k,:],kern[:,par,:],start=True,stop=True).then_inc(spreadk,1)
                tiles(pe,b,ip,kernel_of,spread)
            images(pe,image)
        @block.scalar
        def _(act):
            nc.scalar.preload_act_table_set("natural_log_exp_and_others")
            nm.act_start(act); padded.start(act); biased.start(act)
            act.wait_ge(w_ready,1)
            def image(b,ip):
                def root_and_pad(i,j,par,ip):
                    nm.act_root(act,i,par)
                    squeezed.of(act,i)
                    for kw in range(3):
                        q=slice(RED*kw,RED*kw+RED)
                        last=nc.scalar.activation(y[ip][q,bass.ds(j*ROWS+1,ROWS),2-kw:2-kw+W],yP[q,:].rearrange("p (a b) -> p a b",b=W),ACT.Identity,bias=b1s[q,0:1])
                    last.then_inc(padded.sem,1)
                tiles(act,b,ip,lambda i,j,par,ip: nm.act_square(act,i,par),root_and_pad)
                def add_bias(i,j,par,ip):
                    kernels.of(act,i)
                    added.before(act,i,2)
                    nc.scalar.activation(kern[:,par,:],kP[:,:],ACT.Identity,bias=bias[:,0:1]).then_inc(biased.sem,1)
                tiles(act,b,ip,None,add_bias)
            images(act,image)
        @block.vector
        def _(dve):
            nm.dve_start(dve); added.start(dve)
            dve.sem_inc(times,3)
            nc.vector.memset(eps[:,:],1e-6)
            for k in range(2):
                nc.vector.memset(xn[k][:,:,:],0.0)
                nc.vector.memset(y[k][:,:,:],0.0).then_inc(edges,1) if k else nc.vector.memset(y[k][:,:,:],0.0)
            dve.wait_ge(w_in,16*8)
            for kh in range(3):
                nc.vector.tensor_scalar(wk[:,kh,:],w2s[:,:],wds[:,kh:kh+1],None,ALU.mult)
            dve.wait_ge(folded,1)
            nc.vector.tensor_tensor(bias[:,:],kP[:,0:1],b2s[:,:],ALU.add).then_inc(w_ready,1)
            def image(b,ip):
                dve.wait_ge(img_in[ip],(b-ip)*8+16)
                dve.wait_ge(edges,1)
                tiles(dve,b,ip,lambda i,j,par,ip: nm.dve_centre(dve,i,par),lambda i,j,par,ip: nm.dve_scale(dve,i,par))
                def weigh(i,j,par,ip):
                    out.done.before(dve,i,2)
                    for k in range(9):
                        kh,kw=k//3,k%3
                        dve.wait_ge(spreadk,i*9+k+1)
                        if k: dve.wait_ge(summed,i*9+k)
                        nc.vector.tensor_tensor(prod[:,k%3,:].rearrange("p (a b) -> p a b",b=W),eP[k%3][:,:].rearrange("p (a b) -> p a b",b=W),xn[ip][:,bass.ds(j*ROWS+kh,ROWS),kw:kw+W],ALU.mult).then_inc(times,1)
                        before=img[ip][:,bass.ds(j*T,T)] if k==0 else acc[:,par,:]
                        dve.wait_ge(times,i*9+k+4)
                        last=nc.vector.tensor_tensor(acc[:,par,:],before,prod[:,k%3,:],ALU.add)
                        last.then_inc(summed,1)
                    dve.wait_ge(summed,i*9+9)
                    nc.vector.sem_inc(added.sem,1)
                tiles(dve,b,ip,None,weigh)
                dve.sem_inc(image_used,1)
            images(dve,image)
        if beside:
            block.gpsimd(beside(r))


HW=24
def heads(nc, x, wg, att, ones, xn_out, table, tag="h"):
    with ExitStack() as ctx:
        ctx.enter_context(nc.cleanup_on_exit())
        r=Room(nc,ctx,tag)
        xt=r.sb("x",[P,2,T]); xn=r.sb("xn",[P,2,T]); mw=r.sb("mw",[P,P]); w=r.sb("w",[P,HW]); at=r.sb("att",[P,32]); prod=r.sb("prod",[P,2,16])
        hp=[r.pb(f"hp{k}",[P,4,HW]) for k in range(2)]; hs=r.sb("hs",[P,2,4,HW])
        eps=r.sb("eps",[P,1]); w_in=r.sem("w_in"); w_prod=r.sem("w_prod"); w_ready=r.sem("w_ready")
        rows,copied=r.flags("rows copied")
        x_in=r.pair("x_in"); xn_stores=Stores(r,"xn_out"); t_stores=Stores(r,"t_out")
        def dest_free(dve,i,par):
            xn_stores.done.before(dve,i,2)
            rows.before(dve,i,2)
        nm=Norm(nc,r,"n",mw[:,:],eps[:,0:1],lambda i,par:xt[:,par,:],lambda e,i,par: landed(e,x_in,i,par),lambda i,par:xn[:,par,:],dest_free)
        block=ctx.enter_context(nc.Block())
        @block.sync
        def _(sp):
            sp.dma_start(mw[:,:],ones).then_inc(w_in,16)
            sp.dma_start(w[:,0:16],wg).then_inc(w_in,16)
            sp.dma_start(at[:,:],att.partition_broadcast(P)).then_inc(w_in,16)
            def load(i,par):
                nm.centred.before(sp,i,2)
                sp.dma_start(xt[:,par,:],x[:,bass.ds(i*T,T)]).then_inc(x_in[par],16)
            paired(sp,TILES,load)
        @block.tensor
        def _(pe):
            nm.pe_start(pe); rows.start(pe)
            pe.wait_ge(w_in,48)
            pe.wait_ge(w_ready,3)
            def body(i,par):
                nm.pe_var(pe,i,par)
                nm.normed.of(pe,i)
                copied.before(pe,i,2)
                for q in range(4):
                    last=nc.tensor.matmul(hp[par][:,q,:],xn[:,par,q*P:(q+1)*P],w[:,:],start=True,stop=True,skip_group_check=True)
                last.then_inc(rows.sem,1)
            skewed(pe,TILES,lambda i,par: nm.pe_mean(pe,i,par),body)
        @block.vector
        def _(dve):
            nm.dve_start(dve)
            nc.vector.memset(eps[:,:],1e-5).then_inc(w_ready,1)
            dve.wait_ge(w_in,48)
            for k in range(2):
                nc.vector.tensor_tensor(prod[:,k,:],w[:,0:16],at[:,16*k:16*k+16],ALU.mult).then_inc(w_prod,1)
            dve.wait_ge(w_prod,2)
            for k in range(2):
                nc.vector.tensor_reduce(w[:,16+4*k:20+4*k],prod[:,k,:].rearrange("p (h e) -> p h e",e=4),AX.X,ALU.add).then_inc(w_ready,1)
            skewed(dve,TILES,lambda i,par: nm.dve_centre(dve,i,par),lambda i,par: nm.dve_scale(dve,i,par))
        @block.scalar
        def _(act):
            nc.scalar.preload_act_table_set("natural_log_exp_and_others")
            nm.act_start(act); copied.start(act)
            act.wait_ge(w_ready,1)
            def body(i,par):
                nm.act_root(act,i,par)
                rows.of(act,i)
                t_stores.done.before(act,i,2)
                nc.scalar.copy(hs[:,par,:,:],hp[par][:,:,:]).then_inc(copied.sem,1)
            skewed(act,TILES,lambda i,par: nm.act_square(act,i,par),body)
        @block.gpsimd
        def _(pool):
            def body(i,par):
                nm.normed.of(pool,i)
                pool.dma_start(xn_out[:,bass.ds(i*T,T)],xn[:,par,:]).then_inc(xn_stores.sems[par],16)
                copied.of(pool,i)
                pool.dma_start(table[bass.ds(i*T,T),:].rearrange("(q p) f -> p q f",p=P),hs[:,par,:,:]).then_inc(t_stores.sems[par],16)
                xn_stores.landed(pool,i,par)
                t_stores.landed(pool,i,par)
            xn_stores.start(pool); t_stores.start(pool)
            paired(pool,TILES,body)


E=524288; COLS=E//P; HI=256; HW=24; GHALF=16; RING=16; HALF=8; C=128; NF=20; FAR=1e30
class Gather:
    def __init__(self, nc, room, rec, table, rows, zero_edges, zero_row):
        self.nc,self.table,self.rows,self.zero_edges,self.zero_row=nc,table,rows,zero_edges,zero_row
        self.rec=rec.rearrange("(p c) f -> p c f",p=P)
        self.ring=room.sb("ring",[P,2,GHALF,2],i32); self.got=room.sb("got",[P,2,GHALF,HW]); self.zero=room.sb("zero",[P,1024])
        self.ring_in,self.stored=room.pair("ring_in"),room.pair("stored"); self.gathered=Rows(room,"gathered",GHALF)
        self.zeroed=room.sem("zeroed"); self.zeros_out=room.sem("zeros_out"); self.gate=room.sem("gather_gate")
    def load(self,sp,i,par): sp.dma_start(self.ring[:,par,:,:],self.rec[:,bass.ds(i*GHALF,GHALF),:]).then_inc(self.ring_in[par],16)
    def store(self,sp,t,par):
        i=t*2+par
        self.gathered.wait(sp,t+1,par)
        sp.dma_start(self.rows[:,bass.ds(i*GHALF,GHALF),:],self.got[:,par,:,:]).then_inc(self.stored[par],16)
    def sync(self,sp):
        self.load(sp,0,0); self.load(sp,1,1)
        sp.wait_ge(self.zeroed,1)
        edz=self.zero_edges.rearrange("(p n) f -> p (n f)",p=P); n=E*8//(P*1024)
        with sp.Fori(0,n) as i:
            sp.dma_start(edz[:,bass.ds(i*1024,1024)],self.zero[:,:]).then_inc(self.zeros_out,16)
        sp.dma_start(self.zero_row,self.zero[0:1,0:NF]).then_inc(self.zeros_out,16)
        with sp.Fori(0,COLS//(2*GHALF)-1) as t:
            for par in range(2):
                self.store(sp,t,par)
                self.load(sp,t*2+par+2,par)
        for par in range(2): self.store(sp,COLS//(2*GHALF)-1,par)
        for par in range(2): sp.wait_ge(self.stored[par],8*COLS//GHALF)
        sp.wait_ge(self.zeros_out,16*(n+1))
    def fetch(self,pool,i,par,first):
        pool.wait_ge(self.ring_in[par],(i-par)*8+16)
        pool.sem_inc(self.gate,1)
        if not first:
            pool.wait_ge(self.stored[par],(i-par)*8)
            pool.sem_inc(self.gate,1)
        for k in range(GHALF):
            pool.indirect_dma_start(self.got[:,par,k,:],None,self.table,bass.IndirectOffsetOnAxis(ap=self.ring[:,par,k,0:1],axis=0)).then_inc(self.gathered.of(k,par),16)
    def pool(self,pool):
        self.nc.gpsimd.memset(self.zero[:,:],0.0).then_inc(self.zeroed,1)
        self.fetch(pool,0,0,True); self.fetch(pool,1,1,True)
        with pool.Fori(1,COLS//(2*GHALF)) as t:
            for par in range(2): self.fetch(pool,t*2+par,par,False)

def edge_arrays(nc, tag):
    dram=lambda n,s: nc.dram_tensor(f"{tag}_{n}",s,f32).ap()
    return dict(rows=dram("rows",[P,COLS,HW]),mx=dram("mx",[E,4]),ed=dram("ed",[E+P,8]),ss=dram("ss",[E,NF]),ct=dram("ct",[P+1,NF]),nr=dram("nr",[NODES,8]))
def gather_of(nc, room, rec, table, d): return Gather(nc,room,rec,table,d["rows"],d["ed"][0:E,:],d["ct"][P:P+1,:])
def gather_alone(nc, rec, table, d, tag="ga"):
    with ExitStack() as ctx:
        ctx.enter_context(nc.cleanup_on_exit())
        g=gather_of(nc,Room(nc,ctx,tag),rec,table,d)
        block=ctx.enter_context(nc.Block())
        block.sync(g.sync); block.gpsimd(g.pool)

def attention(nc, rec, start, deg, table, bgat, gamma, beta, eye, gates, d, tag="g"):
    rows_d,mx_d,ed_d,ss_d,ct_d,nr_d=[d[k] for k in ("rows","mx","ed","ss","ct","nr")]
    with ExitStack() as ctx0:
        ctx0.enter_context(nc.cleanup_on_exit())
        r0=Room(nc,ctx0,tag)
        cont=r0.sb("cont",[P,COLS]); meta=r0.sb("meta",[P,3,NF]); ident=r0.sb("eye",[P,P])
        rowsP=r0.pb("rowsP",[NF,4,P]); colP=r0.pb("colP",[P,NF])
        joins=r0.sb("joins",[NF,3,P]); first=r0.sb("first",[P,1],u32)
        with ExitStack() as ctx:
            ctx.enter_context(nc.cleanup_on_exit())
            r=Room(nc,ctx,tag+"1")
            recs=r.sb("recs",[P,COLS,2],i32); brk=r.sb("brk",[P,COLS]); asrc=r.sb("asrc",[P,COLS,4]); zero=r.sb("zero",[P,1])
            got=r.sb("got",[P,2,C,HW])
            last=r.sb("last",[P,4]); lrow=r.sb("lrow",[4,5,P]); carry=r.sb("carry",[P,4])
            rec_in=r.sem("rec_in"); a_copied=r.sem("a_copied"); rows_in=r.pair("rows_in")
            step=r.sem("step"); pe_done=r.sem("pe_done"); mx_out=r.sem("mx_out"); scanned=r.sem("scanned"); meta_ready=r.sem("meta_ready")
            N=COLS//C
            block=ctx.enter_context(nc.Block())
            @block.sync
            def _(sp):
                sp.dma_start(recs[:,:,:],rec.rearrange("(p c) f -> p c f",p=P)).then_inc(rec_in,16)
                sp.dma_start(ident[:,:],eye).then_inc(rec_in,16)
                def load(i,par):
                    sp.wait_ge(a_copied,i+1)
                    sp.dma_start(got[:,par,:,:],rows_d[:,bass.ds(i*C,C),:]).then_inc(rows_in[par],16)
                paired(sp,N,load)
                sp.wait_ge(scanned,1)
                sp.dma_start(mx_d.rearrange("(p c) f -> p c f",p=P),asrc[:,:,:]).then_inc(mx_out,16)
                sp.wait_ge(mx_out,16)
            @block.scalar
            def _(act):
                act.sem_inc(a_copied,2)
                def keep(i,par):
                    landed(act,rows_in,i,par)
                    nc.scalar.copy(asrc[:,bass.ds(i*C,C),:],got[:,par,:,16:20]).then_inc(a_copied,1)
                paired(act,N,keep)
            @block.vector
            def _(dve):
                n=[0]
                def do(ins):
                    n[0]+=1; ins.then_inc(step,1); dve.wait_ge(step,n[0])
                dve.wait_ge(rec_in,32)
                nc.vector.memset(cont[:,0:1],1.0)
                do(nc.vector.tensor_tensor(cont[:,1:COLS],recs[:,1:COLS,1],recs[:,0:COLS-1,1],ALU.is_equal))
                do(nc.vector.tensor_scalar(brk[:,:],cont[:,:],-1.0,FAR,ALU.add,ALU.mult))
                nc.vector.tensor_copy(meta[:,0,:],recs[:,0:1,1].broadcast_to([P,NF]))
                nc.vector.tensor_copy(first[:,:],recs[:,0:1,1])
                nc.vector.tensor_copy(meta[:,1,:],recs[:,COLS-1:COLS,1].broadcast_to([P,NF]))
                do(nc.vector.tensor_reduce(last[:,0:1],cont[:,1:COLS],AX.X,ALU.min))
                do(nc.vector.tensor_copy(meta[:,2,:],last[:,0:1].broadcast_to([P,NF])))
                dve.wait_ge(a_copied,N+2)
                for h in range(4):
                    nc.vector.tensor_tensor_scan(asrc[:,:,h],brk[:,:],asrc[:,:,h],-FAR,ALU.add,ALU.max)
                do(nc.vector.memset(zero[:,0:1],0.0))
                nc.vector.tensor_copy(last[:,:],asrc[:,COLS-1,:]).then_inc(meta_ready,1)
                dve.wait_ge(pe_done,1)
                nc.vector.memset(joins[:,:,:],0.0).then_inc(meta_ready,1)
                dve.wait_ge(meta_ready,2)
                do(nc.vector.tensor_copy(joins[:,2,:],rowsP[:,1,:]))
                do(nc.vector.tensor_tensor(joins[:,0,1:P],rowsP[:,0,1:P],joins[:,2,0:P-1],ALU.is_equal))
                do(nc.vector.tensor_tensor(joins[:,1,1:P],joins[:,0,1:P],rowsP[:,2,0:P-1],ALU.mult))
                do(nc.vector.tensor_scalar(lrow[:,0,:],joins[0:4,1,:],-1.0,FAR,ALU.add,ALU.mult))
                do(nc.vector.tensor_scalar(lrow[:,1,:],joins[0:4,0,:],-1.0,FAR,ALU.add,ALU.mult))
                do(nc.vector.tensor_tensor(lrow[:,2,1:P],rowsP[0:4,3,0:P-1],joins[0:4,0,1:P],ALU.mult))
                do(nc.vector.tensor_tensor(lrow[:,1,1:P],lrow[:,1,1:P],lrow[:,2,1:P],ALU.add))
                do(nc.vector.tensor_tensor_scan(lrow[:,4,:],lrow[:,0,:],lrow[:,1,:],-FAR,ALU.add,ALU.max))
                nc.vector.sem_inc(meta_ready,1)
                dve.wait_ge(pe_done,2)
                do(nc.vector.tensor_copy(carry[:,:],colP[:,0:4]))
                for h in range(4):
                    nc.vector.tensor_tensor_scan(asrc[:,:,h],brk[:,:],asrc[:,:,h],carry[:,h:h+1],ALU.add,ALU.max)
                do(nc.vector.memset(zero[:,0:1],0.0))
                do(nc.vector.memset(cont[:,0:1],0.0))
                dve.sem_inc(scanned,1)
            @block.tensor
            def _(pe):
                pe.wait_ge(rec_in,32)
                pe.wait_ge(meta_ready,1)
                for k in range(3):
                    nc.tensor.matmul(rowsP[:,k,:],meta[:,k,:],ident[:,:],start=True,stop=True,skip_group_check=True)
                nc.tensor.matmul(rowsP[0:4,3,:],last[:,:],ident[:,:],start=True,stop=True,skip_group_check=True).then_inc(pe_done,1)
                pe.wait_ge(meta_ready,3)
                nc.tensor.matmul(colP[:,0:4],lrow[:,4,:],ident[0:4,0:4],start=True,stop=True).then_inc(pe_done,1)
        nodes=r0.sb("nodes",[P,HI,HW]); endr=r0.sb("endr",[P,HI],u32); stf=r0.sb("stf",[P,HI]); has=r0.sb("has",[P,HI]); nrow=r0.sb("nrow",[P,HI,8])
        rowfirst=r0.sb("rowfirst",[P,8])
        bc=lambda a,w: a.unsqueeze(2).broadcast_to([P,HI,w])
        def fetch_by_node(tg, prepare, jobs, finish, act_part=None):
            with ExitStack() as ctx:
                ctx.enter_context(nc.cleanup_on_exit())
                r=Room(nc,ctx,tag+tg)
                W_=max(j[3] for j in jobs)
                idx=r.sb("idx",[P,RING],u32); got=[r.sb(f"got{n}",[P,RING,j[3]]) for n,j in enumerate(jobs)]
                ready=r.sem("ready"); gate=r.sem("gate"); copied=r.sem("copied"); sg=r.pair("sg")
                N=HI//HALF
                prep=prepare(r)
                block=ctx.enter_context(nc.Block())
                if "sync" in prep: block.sync(prep["sync"])
                if "tensor" in prep: block.tensor(prep["tensor"])
                @block.gpsimd
                def _(pool):
                    if "pool" in prep: prep["pool"](pool)
                    for n,(ix,tb,o,w) in enumerate(jobs):
                        def fetch(i,par):
                            pool.wait_ge(ready,i+1+n*N)
                            pool.sem_inc(gate,1)
                            pool.wait_ge(copied,i+1+n*N)
                            pool.sem_inc(gate,1)
                            for k in range(par*HALF,par*HALF+HALF):
                                pool.indirect_dma_start(got[n][:,k,:],None,tb,bass.IndirectOffsetOnAxis(ap=idx[:,k:k+1],axis=0)).then_inc(sg[par],16)
                        paired(pool,N,fetch)
                    if "pool_after" in prep: prep["pool_after"](pool)
                @block.vector
                def _(dve):
                    prep["vector"](dve)
                    for n,(ix,tb,o,w) in enumerate(jobs):
                        def index(i,par):
                            if not (isinstance(i,int) and n==0): dve.wait_ge(sg[par],(i-par)*8*HALF+n*N*8*HALF)
                            nc.vector.tensor_copy(idx[:,par*HALF:par*HALF+HALF],ix[:,bass.ds(i*HALF,HALF)]).then_inc(ready,1)
                        paired(dve,N,index,peel=True)
                    dve.wait_ge(copied,2+N*len(jobs))
                    finish(dve,r,prep)
                @block.scalar
                def _(act):
                    act.sem_inc(copied,2)
                    for n,(ix,tb,o,w) in enumerate(jobs):
                        def keep(i,par):
                            act.wait_ge(sg[par],((i-par)*8+16+n*N*8)*HALF)
                            nc.scalar.copy(o[:,bass.ds(i*HALF,HALF),:],got[n][:,par*HALF:par*HALF+HALF,:]).then_inc(copied,1)
                        paired(act,N,keep)
                    if "scalar" in prep: prep["scalar"](act)
        def steps(dve,sem,n):
            def do(ins):
                n[0]+=1; ins.then_inc(sem,1); dve.wait_ge(sem,n[0])
            return do
        with ExitStack() as ctxm:
            ctxm.enter_context(nc.cleanup_on_exit())
            rm=Room(nc,ctxm,tag+"m")
            top=rm.sb("top",[P,HI,4]); degf=rm.sb("degf",[P,HI]); sidx=rm.sb("sidx",[P,HI],u32); pid=rm.sb("pid",[P,1],i32); pidf=rm.sb("pidf",[P,1]); tmp=rm.sb("tmp",[P,HI]); tmp4=rm.sb("tmp4",[P,HI,4])
            n=[0]
            def prepare(r):
                n_in=r.sem("n_in"); iot=r.sem("iot"); step=r.sem("step"); nrow_ready=r.sem("nrow_ready"); nr_out=r.sem("nr_out"); ring=r.sem("ring")
                rr=r.sb("rr",[P,RING,8]); ri=r.sb("ri",[P,RING],u32); sc=r.pair("sc"); g2=r.sem("g2"); f1=r.sem("f1")
                def sync(sp):
                    sp.dma_start(nodes[:,:,:],table.rearrange("(p n) f -> p n f",p=P)).then_inc(n_in,16)
                    sp.dma_start(stf[:,:],start).then_inc(n_in,16)
                    sp.dma_start(degf[:,:],deg).then_inc(n_in,16)
                    sp.wait_ge(nrow_ready,1)
                    sp.dma_start(nr_d.rearrange("(p n) f -> p n f",p=P),nrow[:,:,:]).then_inc(nr_out,16)
                def pool(p):
                    p.iota(pid[:,:],pattern=[[0,1]],base=E,channel_multiplier=1).then_inc(iot,1)
                def vector(dve):
                    do=steps(dve,step,n)
                    dve.wait_ge(n_in,48); dve.wait_ge(iot,1)
                    do(nc.vector.tensor_copy(pidf[:,:],pid[:,:]))
                    do(nc.vector.tensor_scalar(has[:,:],degf[:,:],0.0,None,ALU.is_gt))
                    do(nc.vector.scalar_tensor_tensor(tmp[:,:],stf[:,:],-1.0,degf[:,:],ALU.add,ALU.add))
                    do(nc.vector.tensor_scalar(endr[:,:],tmp[:,:],0.0,None,ALU.max))
                    do(nc.vector.tensor_scalar(tmp[:,:],has[:,:],-1.0,-1.0,ALU.mult,ALU.subtract))
                    do(nc.vector.tensor_scalar(tmp[:,:],tmp[:,:],pidf[:,0:1],None,ALU.mult))
                    do(nc.vector.tensor_tensor(degf[:,:],stf[:,:],has[:,:],ALU.mult))
                    do(nc.vector.tensor_tensor(sidx[:,:],tmp[:,:],degf[:,:],ALU.add))
                def pool_after(p):
                    def send(i,par):
                        p.wait_ge(ring,i+1)
                        p.sem_inc(g2,1)
                        for k in range(par*HALF,par*HALF+HALF):
                            p.indirect_dma_start(ed_d,bass.IndirectOffsetOnAxis(ap=ri[:,k:k+1],axis=0),rr[:,k,:],None).then_inc(sc[par],16)
                    paired(p,HI//HALF,send)
                    p.wait_ge(nr_out,16)
                    p.sem_inc(g2,1)
                    p.indirect_dma_start(rowfirst[:,:],None,nr_d,bass.IndirectOffsetOnAxis(ap=first[:,:],axis=0)).then_inc(f1,16)
                    for k in range(2): p.wait_ge(sc[k],8*HI)
                    p.wait_ge(f1,16)
                return dict(sync=sync,pool=pool,vector=vector,pool_after=pool_after,step=step,nrow_ready=nrow_ready,ring=ring,rr=rr,ri=ri,sc=sc)
            def finish(dve,r,prep):
                do=steps(dve,prep["step"],n)
                do(nc.vector.tensor_tensor(top[:,:,:],top[:,:,:],bc(has[:,:],4),ALU.mult))
                do(nc.vector.tensor_scalar(tmp[:,:],has[:,:],-1.0,FAR,ALU.add,ALU.mult))
                do(nc.vector.tensor_tensor(top[:,:,:],top[:,:,:],bc(tmp[:,:],4),ALU.add))
                do(nc.vector.tensor_tensor(top[:,:,:],top[:,:,:],nodes[:,:,16:20],ALU.max))
                do(nc.vector.tensor_tensor(top[:,:,:],top[:,:,:],nodes[:,:,20:24],ALU.add))
                do(nc.vector.tensor_copy(nrow[:,:,0:4],nodes[:,:,20:24]))
                do(nc.vector.scalar_tensor_tensor(nrow[:,:,4:8],top[:,:,:],0.2,top[:,:,:],ALU.mult,ALU.max))
                dve.sem_inc(prep["nrow_ready"],1)
                def fill(i,par):
                    if not isinstance(i,int): dve.wait_ge(prep["sc"][par],(i-par)*8*HALF)
                    nc.vector.tensor_copy(prep["ri"][:,par*HALF:par*HALF+HALF],sidx[:,bass.ds(i*HALF,HALF)])
                    nc.vector.tensor_copy(prep["rr"][:,par*HALF:par*HALF+HALF,:],nrow[:,bass.ds(i*HALF,HALF),:]).then_inc(prep["ring"],1)
                paired(dve,HI//HALF,fill,peel=True)
            fetch_by_node("2",prepare,[(endr,mx_d,top,4)],finish)
        with ExitStack() as ctx:
            ctx.enter_context(nc.cleanup_on_exit())
            r=Room(nc,ctx,tag+"3")
            gs=r.sb("gs",[P,2,C,HW]); ed=r.sb("ed",[P,2,C,8]); pr=r.sb("pr",[P,2,C,8]); z=r.sb("z",[P,2,C,4]); wt=r.sb("wt",[P,2,C,4]); wh=r.sb("wh",[P,2,C,NF]); zc=r.sb("zc",[P,8]); lrow=r.sb("lrow",[NF,2,P]); carry=r.sb("carry",[P,NF]); last=r.sb("last",[P,NF])
            g_in=r.pair("g_in"); e_in=r.pair("e_in"); out=Stores(r,"out"); zs=r.sem("zs"); step=r.sem("step"); done=r.sem("done"); pe_done=r.sem("pe_done"); ct_out=r.sem("ct_out"); carried=r.sem("carried")
            shaped,shifted,weighed,spread,summed,known=r.flags("shaped shifted weighed spread summed known")
            N=COLS//C
            edr=ed_d[0:E,:].rearrange("(p c) f -> p c f",p=P); ssr=ss_d.rearrange("(p c) f -> p c f",p=P)
            block=ctx.enter_context(nc.Block())
            @block.sync
            def _(sp):
                def load(i,par):
                    spread.before(sp,i,2)
                    sp.dma_start(gs[:,par,:,:],rows_d[:,bass.ds(i*C,C),:]).then_inc(g_in[par],16)
                    sp.dma_start(ed[:,par,:,:],edr[:,bass.ds(i*C,C),:]).then_inc(e_in[par],16)
                paired(sp,N,load)
                sp.wait_ge(carried,1)
                sp.dma_start(ct_d[0:P,:],carry[:,:]).then_inc(ct_out,16)
                sp.wait_ge(ct_out,16)
            @block.vector
            def _(dve):
                for f in (shaped,shifted,spread,summed,known): f.start(dve)
                nc.vector.memset(zc[:,:],0.0).then_inc(zs,1)
                dve.wait_ge(zs,1)
                def tile(i,par,begin=False):
                    landed(dve,e_in,i,par)
                    if begin:
                        nc.vector.tensor_copy(ed[:,0,0,:],rowfirst[:,:]).then_inc(zs,1)
                        dve.wait_ge(zs,2)
                    else: known.of(dve,i-1)
                    for f in range(8):
                        ins=nc.vector.tensor_tensor_scan(pr[:,par,:,f],cont[:,bass.ds(i*C,C)],ed[:,par,:,f],0.0 if begin else pr[:,1-par,C-1,f:f+1],ALU.mult,ALU.add)
                    ins.then_inc(known.sem,1)
                    known.of(dve,i)
                    landed(dve,g_in,i,par)
                    nc.vector.tensor_tensor(z[:,par,:,:],gs[:,par,:,16:20],pr[:,par,:,0:4],ALU.add).then_inc(shaped.sem,1)
                    shaped.of(dve,i)
                    nc.vector.scalar_tensor_tensor(z[:,par,:,:],z[:,par,:,:],0.2,z[:,par,:,:],ALU.mult,ALU.max).then_inc(zs,1)
                    dve.wait_ge(zs,i+3)
                    nc.vector.tensor_tensor(z[:,par,:,:],z[:,par,:,:],pr[:,par,:,4:8],ALU.subtract).then_inc(shifted.sem,1)
                def sums(i,par,begin=False):
                    weighed.of(dve,i)
                    out.done.before(dve,i,2)
                    if not begin: summed.of(dve,i-1)
                    nc.vector.tensor_copy(wh[:,par,:,16:20],wt[:,par,:,:])
                    nc.vector.tensor_tensor(wh[:,par,:,0:16].rearrange("p c (h e) -> p c h e",e=4),gs[:,par,:,0:16].rearrange("p c (h e) -> p c h e",e=4),wt[:,par,:,:].unsqueeze(3).broadcast_to([P,C,4,4]),ALU.mult).then_inc(spread.sem,1)
                    spread.of(dve,i)
                    for f in range(NF):
                        ins=nc.vector.tensor_tensor_scan(wh[:,par,:,f],cont[:,bass.ds(i*C,C)],wh[:,par,:,f],0.0 if begin else wh[:,1-par,C-1,f:f+1],ALU.mult,ALU.add)
                    ins.then_inc(summed.sem,1)
                tile(0,0,True); tile(1,1); sums(0,0,True)
                with dve.Fori(1,N//2) as t:
                    tile(t*2,0); sums(t*2-1,1); tile(t*2+1,1); sums(t*2,0)
                sums(N-1,1)
                summed.of(dve,N-1)
                nc.vector.tensor_copy(last[:,:],wh[:,1,C-1,:]).then_inc(done,1)
                dve.wait_ge(pe_done,1)
                nc.vector.memset(lrow[:,:,:],0.0).then_inc(step,1)
                dve.wait_ge(step,1)
                nc.vector.tensor_tensor(lrow[:,0,1:P],rowsP[:,3,0:P-1],joins[:,0,1:P],ALU.mult).then_inc(step,1)
                dve.wait_ge(step,2)
                nc.vector.tensor_tensor_scan(lrow[:,1,:],joins[:,1,:],lrow[:,0,:],0.0,ALU.mult,ALU.add).then_inc(done,1)
                dve.wait_ge(pe_done,2)
                nc.vector.tensor_copy(carry[:,:],colP[:,:]).then_inc(carried,1)
            @block.scalar
            def _(act):
                weighed.start(act)
                def weigh(i,par):
                    shifted.of(act,i)
                    spread.before(act,i,2)
                    nc.scalar.activation(wt[:,par,:,:],z[:,par,:,:],ACT.Exp).then_inc(weighed.sem,1)
                paired(act,N,weigh)
            @block.gpsimd
            def _(pool):
                def store(i,par):
                    summed.of(pool,i)
                    pool.dma_start(ssr[:,bass.ds(i*C,C),:],wh[:,par,:,:]).then_inc(out.sems[par],16)
                    out.landed(pool,i,par)
                out.start(pool)
                paired(pool,N,store)
            @block.tensor
            def _(pe):
                pe.wait_ge(done,1)
                nc.tensor.matmul(rowsP[:,3,:],last[:,:],ident[:,:],start=True,stop=True).then_inc(pe_done,1)
                pe.wait_ge(done,2)
                nc.tensor.matmul(colP[:,:],lrow[:,1,:],ident[0:NF,0:NF],start=True,stop=True).then_inc(pe_done,1)
        with ExitStack() as ctx:
            ctx.enter_context(nc.cleanup_on_exit())
            r5=Room(nc,ctx,tag+"5")
            tot=r5.sb("tot",[P,HI,NF]); car=r5.sb("car",[P,HI,NF]); cidx=r5.sb("cidx",[P,HI],u32); si=r5.sb("si",[P,HI],i32); ei=r5.sb("ei",[P,HI],i32); pe_=r5.sb("pe",[P,HI]); ps=r5.sb("ps",[P,HI])
            par3=r5.sb("par",[P,3,16]); w4=r5.sb("w4",[P,HI,4]); big=r5.sb("big",[P,HI,16]); one=r5.sb("one",[P,HI]); eps=r5.sb("eps",[P,1]); sc=r5.sb("sc",[P,4,HI]); ex=r5.sb("ex",[P,4,HI]); cmp=r5.sb("cmp",[P,HI]); rank=r5.sb("rank",[P,4,HI]); g=r5.sb("g",[P,4,HI])
            n=[0]
            def prepare(r):
                p_in=r.sem("p_in"); step=r.sem("step"); a_go=r.sem("a_go"); a_done=r.sem("a_done"); g_ready=r.sem("g_ready"); g_out=r.sem("g_out")
                def sync(sp):
                    for k,a in enumerate((bgat,gamma,beta)): sp.dma_start(par3[:,k,:],a.partition_broadcast(P)).then_inc(p_in,16)
                    sp.wait_ge(g_ready,1)
                    for e in range(4): sp.dma_start(gates[e,:].rearrange("(p n) -> p n",p=P),g[:,e,:]).then_inc(g_out,16)
                    sp.wait_ge(g_out,64)
                def vector(dve):
                    do=steps(dve,step,n)
                    do(nc.vector.tensor_copy(si[:,:],stf[:,:]))
                    do(nc.vector.tensor_copy(ei[:,:],endr[:,:]))
                    do(nc.vector.tensor_single_scalar(si[:,:],si[:,:],12,ALU.logical_shift_right))
                    do(nc.vector.tensor_single_scalar(ei[:,:],ei[:,:],12,ALU.logical_shift_right))
                    do(nc.vector.tensor_copy(ps[:,:],si[:,:]))
                    do(nc.vector.tensor_copy(pe_[:,:],ei[:,:]))
                    do(nc.vector.tensor_tensor(ps[:,:],pe_[:,:],ps[:,:],ALU.is_gt))
                    do(nc.vector.scalar_tensor_tensor(pe_[:,:],pe_[:,:],float(-P),ps[:,:],ALU.add,ALU.mult))
                    do(nc.vector.tensor_scalar(cidx[:,:],pe_[:,:],float(P),None,ALU.add))
                def scalar(act):
                    for k,(o,i,f,kw) in enumerate(((w4[:,:,:],w4[:,:,:],ACT.Exp,{}),(one[:,:],one[:,:],ACT.Ln,dict(bias=eps[:,0:1])),(one[:,:],one[:,:],ACT.Exp,dict(scale=-0.5)),(ex[:,:,:],ex[:,:,:],ACT.Exp,{}))):
                        act.wait_ge(a_go,k+1)
                        nc.scalar.activation(o,i,f,**kw).then_inc(a_done,1)
                return dict(sync=sync,vector=vector,scalar=scalar,step=step,a_go=a_go,a_done=a_done,g_ready=g_ready,p_in=p_in)
            def finish(dve,r,prep):
                do=steps(dve,prep["step"],n)
                acts=[0]
                def act_turn():
                    acts[0]+=1; dve.sem_inc(prep["a_go"],1); dve.wait_ge(prep["a_done"],acts[0])
                V=nc.vector
                dve.wait_ge(prep["p_in"],48)
                do(V.memset(eps[:,:],1e-5))
                do(V.tensor_tensor(tot[:,:,:],tot[:,:,:],bc(has[:,:],NF),ALU.mult))
                do(V.tensor_tensor(tot[:,:,:],tot[:,:,:],car[:,:,:],ALU.add))
                do(V.tensor_tensor(w4[:,:,:],nodes[:,:,16:20],nodes[:,:,20:24],ALU.add))
                do(V.scalar_tensor_tensor(w4[:,:,:],w4[:,:,:],0.2,w4[:,:,:],ALU.mult,ALU.max))
                do(V.tensor_tensor(w4[:,:,:],w4[:,:,:],nrow[:,:,4:8],ALU.subtract))
                act_turn()
                h4=lambda a: a.rearrange("p n (h e) -> p n h e",e=4)
                b4=lambda a: a.unsqueeze(3).broadcast_to([P,HI,4,4])
                do(V.tensor_tensor(tot[:,:,16:20],tot[:,:,16:20],w4[:,:,:],ALU.add))
                do(V.tensor_tensor(h4(big[:,:,:]),h4(nodes[:,:,0:16]),b4(w4[:,:,:]),ALU.mult))
                do(V.tensor_tensor(big[:,:,:],big[:,:,:],tot[:,:,0:16],ALU.add))
                do(V.tensor_scalar(w4[:,:,:],tot[:,:,16:20],1e-16,None,ALU.add))
                do(V.reciprocal(w4[:,:,:],w4[:,:,:]))
                do(V.tensor_tensor(h4(big[:,:,:]),h4(big[:,:,:]),b4(w4[:,:,:]),ALU.mult))
                par=lambda k: par3[:,k,:].unsqueeze(1).broadcast_to([P,HI,16])
                do(V.tensor_tensor(big[:,:,:],big[:,:,:],par(0),ALU.add))
                do(V.tensor_reduce(one[:,:],big[:,:,:],AX.X,ALU.add))
                do(V.tensor_scalar(one[:,:],one[:,:],1/16,None,ALU.mult))
                do(V.tensor_tensor(big[:,:,:],big[:,:,:],bc(one[:,:],16),ALU.subtract))
                do(V.tensor_tensor(tot[:,:,0:16],big[:,:,:],big[:,:,:],ALU.mult))
                do(V.tensor_reduce(one[:,:],tot[:,:,0:16],AX.X,ALU.add))
                do(V.tensor_scalar(one[:,:],one[:,:],1/16,None,ALU.mult))
                act_turn(); act_turn()
                do(V.tensor_tensor(big[:,:,:],big[:,:,:],bc(one[:,:],16),ALU.mult))
                do(V.tensor_tensor(big[:,:,:],big[:,:,:],par(1),ALU.mult))
                do(V.tensor_tensor(big[:,:,:],big[:,:,:],par(2),ALU.add))
                do(V.tensor_reduce(sc[:,:,:],big[:,:,:].rearrange("p n (h e) -> p e n h",e=4),AX.X,ALU.add))
                do(V.tensor_scalar(sc[:,:,:],sc[:,:,:],0.25,None,ALU.mult))
                for e in range(4):
                    first_=True
                    for j in range(4):
                        if j==e: continue
                        op=ALU.is_ge if j<e else ALU.is_gt
                        if first_: do(V.tensor_tensor(rank[:,e,:],sc[:,j,:],sc[:,e,:],op)); first_=False
                        else:
                            do(V.tensor_tensor(cmp[:,:],sc[:,j,:],sc[:,e,:],op))
                            do(V.tensor_tensor(rank[:,e,:],rank[:,e,:],cmp[:,:],ALU.add))
                do(V.tensor_scalar(rank[:,:,:],rank[:,:,:],2.0,None,ALU.is_lt))
                do(V.tensor_tensor(cmp[:,:],sc[:,0,:],sc[:,1,:],ALU.max))
                do(V.tensor_tensor(cmp[:,:],cmp[:,:],sc[:,2,:],ALU.max))
                do(V.tensor_tensor(cmp[:,:],cmp[:,:],sc[:,3,:],ALU.max))
                do(V.tensor_tensor(ex[:,:,:],sc[:,:,:],cmp[:,:].unsqueeze(1).broadcast_to([P,4,HI]),ALU.subtract))
                act_turn()
                do(V.tensor_tensor(ex[:,:,:],ex[:,:,:],rank[:,:,:],ALU.mult))
                do(V.tensor_reduce(cmp[:,:],ex[:,:,:].rearrange("p e n -> p n e"),AX.X,ALU.add))
                do(V.reciprocal(cmp[:,:],cmp[:,:]))
                do(V.tensor_tensor(g[:,:,:],ex[:,:,:],cmp[:,:].unsqueeze(1).broadcast_to([P,4,HI]),ALU.mult))
                dve.sem_inc(prep["g_ready"],1)
            fetch_by_node("4",prepare,[(endr,ss_d,tot,NF),(cidx,ct_d,car,NF)],finish)


EX=4; FF=256
def experts(nc, x, xn, gates, w1, b1, w2, b2, x_out, tag="f"):
    with ExitStack() as ctx:
        ctx.enter_context(nc.cleanup_on_exit())
        r=Room(nc,ctx,tag)
        xt=r.sb("x",[P,2,T]); xs=r.sb("xn",[P,2,T]); gt=r.sb("gate",[P,2,EX,T]); w1s=r.sb("w1",[P,EX,FF]); b1s=r.sb("b1",[P,EX,2]); w2s=r.sb("w2",[P,EX,2,P]); b2s=r.sb("b2",[P,EX])
        hid=r.sb("hid",[P,2,2,T]); part=r.sb("part",[P,2,T]); acc=r.sb("acc",[P,2,T])
        hP=[r.pb(f"hP{k}",[P,2,T]) for k in range(2)]; oP=[r.pb(f"oP{k}",[P,T]) for k in range(2)]
        w_in=r.sem("w_in"); x_in=r.pair("x_in"); n_in=r.pair("n_in"); g_in=r.pair("g_in"); out=Stores(r,"out")
        up,active,down,gated,summed=r.flags("up active down gated summed")
        block=ctx.enter_context(nc.Block())
        def tiles(eng, tile):
            with eng.Fori(0,TILES//2-1) as t:
                tile(t*2,0,True); tile(t*2+1,1,True)
            tile(TILES-2,0,True); tile(TILES-1,1,False)
        @block.sync
        def _(sp):
            for d,s in ((w1s[:,:,:],w1),(b1s[:,:,:],b1),(w2s[:,:,:,:],w2),(b2s[:,:],b2)):
                sp.dma_start(d,s).then_inc(w_in,16)
            def load(i,par):
                up.before(sp,i*EX+EX-1,2*EX) if not isinstance(i,int) else None
                summed.before(sp,i*EX+EX-1,2*EX) if not isinstance(i,int) else None
                sp.dma_start(xs[:,par,:],xn[:,bass.ds(i*T,T)]).then_inc(n_in[par],16)
                sp.dma_start(gt[:,par,:,:],gates[:,bass.ds(i*T,T)].partition_broadcast(P)).then_inc(g_in[par],16)
                sp.dma_start(xt[:,par,:],x[:,bass.ds(i*T,T)]).then_inc(x_in[par],16)
            load(0,0); load(1,1)
            with sp.Fori(1,TILES//2) as t:
                load(t*2,0); load(t*2+1,1)
        @block.tensor
        def _(pe):
            up.start(pe); down.start(pe)
            pe.wait_ge(w_in,64)
            def go_up(i,e,par):
                if e==0: landed(pe,n_in,i,par)
                u=i*EX+e
                active.before(pe,u,2)
                for f in range(2):
                    last=nc.tensor.matmul(hP[e%2][:,f,:],w1s[:,e,f*P:f*P+P],xs[:,par,:],start=True,stop=True)
                last.then_inc(up.sem,1)
            def go_down(i,e):
                u=i*EX+e
                active.of(pe,u)
                gated.before(pe,u,2)
                for f in range(2):
                    last=nc.tensor.matmul(oP[e%2][:,:],w2s[:,e,f,:],hid[:,e%2,f,:],start=(f==0),stop=(f==1))
                last.then_inc(down.sem,1)
            def tile(i,par,more):
                for e in range(EX):
                    if e<EX-1: go_up(i,e+1,par)
                    elif more: go_up(i+1,0,1-par)
                    go_down(i,e)
            go_up(0,0,0)
            tiles(pe,tile)
        @block.scalar
        def _(act):
            active.start(act)
            act.wait_ge(w_in,64)
            def tile(i,par,more):
                for e in range(EX):
                    u=i*EX+e
                    up.of(act,u)
                    down.before(act,u,2)
                    for f in range(2):
                        last=nc.scalar.activation(hid[:,e%2,f,:],hP[e%2][:,f,:],ACT.Gelu,bias=b1s[:,e,f:f+1])
                    last.then_inc(active.sem,1)
            tiles(act,tile)
        @block.vector
        def _(dve):
            gated.start(dve); summed.start(dve)
            dve.wait_ge(w_in,64)
            def tile(i,par,more):
                landed(dve,g_in,i,par)
                landed(dve,x_in,i,par)
                out.done.before(dve,i,2)
                for e in range(EX):
                    u=i*EX+e
                    down.of(dve,u)
                    nc.vector.scalar_tensor_tensor(part[:,e%2,:],oP[e%2][:,:],b2s[:,e:e+1],gt[:,par,e,:],ALU.add,ALU.mult).then_inc(gated.sem,1)
                    gated.of(dve,u)
                    if e: summed.of(dve,u-1)
                    nc.vector.tensor_tensor(acc[:,par,:],xt[:,par,:] if e==0 else acc[:,par,:],part[:,e%2,:],ALU.add).then_inc(summed.sem,1)
            tiles(dve,tile)
        @block.gpsimd
        def _(pool):
            def store(i,par):
                summed.of(pool,i*EX+EX-1)
                pool.dma_start(x_out[:,bass.ds(i*T,T)],acc[:,par,:]).then_inc(out.sems[par],16)
                out.landed(pool,i,par)
            out.start(pool)
            paired(pool,TILES,store)


PADT=TOK+2; NDT=32
def mamba_in(nc, x, lnw, lnb, wdt, dtb, ones, xs_out, dt_out, tag="m1"):
    with ExitStack() as ctx:
        ctx.enter_context(nc.cleanup_on_exit())
        r=Room(nc,ctx,tag)
        xt=r.sb("x",[P,2,T]); x1=r.sb("x1",[P,2,T]); xs=r.sb("xs",[P,2,T]); mw=r.sb("mw",[P,P]); wd=r.sb("wd",[P,NDT]); lw=r.sb("lw",[P,1]); lb=r.sb("lb",[P,1]); db=r.sb("db",[NDT,1]); eps=r.sb("eps",[P,2]); zero=r.sb("zero",[P,2])
        lin=r.sb("lin",[NDT,2,T]); mag=r.sb("mag",[NDT,2,T]); soft=r.sb("soft",[NDT,2,T]); dt=r.sb("dt",[NDT,2,T])
        dP=r.pb("dP",[NDT,T])
        w_in=r.sem("w_in"); const=r.sem("const"); pads=r.sem("pads")
        x_in=r.pair("x_in"); xs_stores=Stores(r,"xs_out"); dt_stores=Stores(r,"dt_out")
        affine,stepped,lined,sized,decayed,logged,softened=r.flags("affine stepped lined sized decayed logged softened")
        n1=Norm(nc,r,"n1",mw[:,:],eps[:,0:1],lambda i,par:xt[:,par,:],lambda e,i,par: landed(e,x_in,i,par),lambda i,par:x1[:,par,:],lambda e,i,par: n2.centred.before(e,i,2))
        def free(e,i,par):
            xs_stores.done.before(e,i,2)
            stepped.before(e,i,2)
        n2=Norm(nc,r,"n2",mw[:,:],eps[:,1:2],lambda i,par:x1[:,par,:],lambda e,i,par: n1.normed.of(e,i),lambda i,par:xs[:,par,:],free)
        block=ctx.enter_context(nc.Block())
        @block.sync
        def _(sp):
            for d,s in ((mw[:,:],ones),(wd[:,:],wdt),(lw[:,:],lnw),(lb[:,:],lnb),(db[:,:],dtb)): sp.dma_start(d,s).then_inc(w_in,16)
            sp.wait_ge(const,1)
            with sp.Fori(0,B) as b:
                sp.dma_start(xs_out[:,bass.ds(b*PADT,2)],zero[:,:]).then_inc(pads,16)
            def load(i,par):
                n1.centred.before(sp,i,2)
                sp.dma_start(xt[:,par,:],x[:,bass.ds(i*T,T)]).then_inc(x_in[par],16)
            paired(sp,TILES,load)
            sp.wait_ge(pads,16*B)
        @block.tensor
        def _(pe):
            n1.pe_start(pe); n2.pe_start(pe); stepped.start(pe)
            pe.wait_ge(w_in,80)
            def step_sizes(i,par):
                affine.of(pe,i)
                lined.before(pe,i,1)
                nc.tensor.matmul(dP[:,:],wd[:,:],xs[:,par,:],start=True,stop=True).then_inc(stepped.sem,1)
            lagged(pe,TILES,[lambda i,p:n1.pe_mean(pe,i,p),lambda i,p:n1.pe_var(pe,i,p),lambda i,p:n2.pe_mean(pe,i,p),lambda i,p:n2.pe_var(pe,i,p),step_sizes])
        @block.scalar
        def _(act):
            nc.scalar.preload_act_table_set("natural_log_exp_and_others")
            n1.act_start(act); n2.act_start(act)
            for f in (lined,sized,decayed,logged): f.start(act)
            act.wait_ge(const,1); act.wait_ge(w_in,80)
            def softplus(i,par):
                stepped.of(act,i)
                softened.before(act,i,2)
                nc.scalar.activation(lin[:,par,:],dP[:,:],ACT.Identity,bias=db[:,0:1]).then_inc(lined.sem,1)
                lined.of(act,i)
                nc.scalar.activation(mag[:,par,:],lin[:,par,:],ACT.Abs).then_inc(sized.sem,1)
                sized.of(act,i)
                nc.scalar.activation(soft[:,par,:],mag[:,par,:],ACT.Exp,scale=-1.0).then_inc(decayed.sem,1)
                decayed.of(act,i)
                nc.scalar.activation(soft[:,par,:],soft[:,par,:],ACT.Ln,bias=1.0).then_inc(logged.sem,1)
            lagged(act,TILES,[lambda i,p:n1.act_square(act,i,p),lambda i,p:n1.act_root(act,i,p),lambda i,p:n2.act_square(act,i,p),lambda i,p:n2.act_root(act,i,p),softplus])
        @block.vector
        def _(dve):
            n1.dve_start(dve); n2.dve_start(dve); affine.start(dve); softened.start(dve)
            nc.vector.memset(eps[:,0:1],1e-6); nc.vector.memset(eps[:,1:2],1e-5)
            nc.vector.memset(zero[:,:],0.0).then_inc(const,1)
            dve.wait_ge(w_in,80)
            def scale(i,par):
                n2.dve_scale(dve,i,par)
                n2.normed.of(dve,i)
                nc.vector.tensor_scalar(xs[:,par,:],xs[:,par,:],lw[:,0:1],lb[:,0:1],ALU.mult,ALU.add).then_inc(affine.sem,1)
            def soften(i,par):
                logged.of(dve,i)
                dt_stores.done.before(dve,i,2)
                nc.vector.scalar_tensor_tensor(dt[:,par,:],lin[:,par,:],0.0,soft[:,par,:],ALU.max,ALU.add).then_inc(softened.sem,1)
            lagged(dve,TILES,[lambda i,p:n1.dve_centre(dve,i,p),lambda i,p:n1.dve_scale(dve,i,p),lambda i,p:n2.dve_centre(dve,i,p),scale,soften])
        @block.gpsimd
        def _(pool):
            xs_stores.start(pool); dt_stores.start(pool)
            with pool.Fori(0,B) as b:
                with pool.Fori(0,TPI//2) as t:
                    for par in range(2):
                        i=b*TPI+t*2+par
                        affine.of(pool,i)
                        pool.dma_start(xs_out[:,bass.ds(b*PADT+(t*2+par)*T+2,T)],xs[:,par,:]).then_inc(xs_stores.sems[par],16)
                        softened.of(pool,i)
                        pool.dma_start(dt_out[:,bass.ds(i*T,T)],dt[:,par,:]).then_inc(dt_stores.sems[par],16)
                        xs_stores.landed(pool,i,par); dt_stores.landed(pool,i,par)


PADT=TOK+2; NDT=32; K=32; CH=T//K; H=4; SP=4; HD=8; UNITS=2*TPI
def mamba_core(nc, xs, dt, wx, wb, wc, wz, cw, cb, alog_row, alog_col, dcol, consts, y_out, placed=None, rec=None, tag="m2"):
    with ExitStack() as ctx:
        ctx.enter_context(nc.cleanup_on_exit())
        r=Room(nc,ctx,tag)
        wk=r.sb("wk",[P,3,2,3,P]); raw=r.sb("raw",[P,2,P]); cws=r.sb("cw",[P,9,P]); wzs=r.sb("wz",[P,2,P]); hb=r.sb("hb",[P,3]); arow=r.sb("arow",[P,4]); acol=r.sb("acol",[P,1]); ds=r.sb("ds",[P,1])
        tri=r.sb("tri",[P,K]); after=r.sb("after",[P,P]); same=r.sb("same",[P,P]); blk=r.sb("blk",[P,4]); place=r.sb("place",[NDT,2,P]); expand=r.sb("expand",[NDT,2,P]); keep=r.sb("keep",[P,T]); perm=r.sb("perm",[P,P])
        xq=r.sb("xq",[P,2,T+2]); dr=r.sb("dr",[NDT,2,T])
        half=r.sb("half",[P,4,T]); tan=r.sb("tan",[P,4,T]); X,Bc,Cc,Z=[r.sb(n,[P,2,T]) for n in ("X","B","C","Z")]
        dtT=r.sb("dtT",[P,2,T]); dAT=r.sb("dAT",[P,2,CH*H]); XT=r.sb("XT",[P,T]); BT=r.sb("BT",[P,2,T]); xdt=r.sb("xdt",[P,2,T]); xdec=r.sb("xdec",[P,T])
        R=r.sb("R",[P,CH*H,K]); EX=r.sb("EX",[P,CH*H,K]); M=r.sb("M",[P,2,CH*H,K]); XB=r.sb("XB",[P,2,CH*H,SP,HD]); PB=r.sb("PB",[P,2,CH,H,SP,HD]); Gm=r.sb("Gm",[P,T])
        dA=r.sb("dA",[P,2,T]); ac=r.sb("ac",[P,2,T]); EA=r.sb("EA",[P,2,T]); cd=r.sb("cd",[P,CH*H]); D0=r.sb("D0",[P,32,CH]); S1=r.sb("S1",[P,32,CH]); ST=r.sb("ST",[P,2,T]); carry=r.sb("carry",[P,2,32]); tmp=r.sb("tmp",[P,32])
        y1=r.sb("y1",[P,T]); y2=r.sb("y2",[P,T]); y3=r.sb("y3",[P,2,T])
        pj=[r.pb(f"pj{k}",[P,T]) for k in range(2)]; sg=[r.pb(f"sg{k}",[P,T]) for k in range(2)]; GP=r.pb("G",[P,T]); SPs=r.pb("S",[P,T]); YP=r.pb("Y",[P,T]); YO=r.pb("YO",[P,T])
        w_in=r.sem("w_in"); raw_in=r.sem("raw_in"); raw_used=r.sem("raw_used"); w_ready=r.sem("w_ready"); aexp=r.sem("aexp"); reset=r.sem("reset"); pe_gate=r.sem("pe_gate"); wstep=r.sem("wstep")
        x_in=r.pair("x_in"); d_in=r.pair("d_in"); out_s=r.pair("out"); stored,=r.flags("stored")
        pT,pA,pX,pB,pC,pZ,segs,gs,ss,cds,ys,yos=r.flags("pT pA pX pB pC pZ segs gs ss cds ys yos")
        stepped,hX,hB,hC,hZ,exs,cde,eas,scop,xbs,pbs=r.flags("stepped hX hB hC hZ exs cde eas scop xbs pbs")
        dtt,dat,rs,scn,sX,sB,sC,sZ,xtt,btt,xd,gm,dec,ms,d0,tm,pb0,s1,sts,car,yy1,yy2,yy3=r.flags("dtt dat rs scn sX sB sC sZ xtt btt xd gm dec ms d0 tm pb0 s1 sts car yy1 yy2 yy3")
        block=ctx.enter_context(nc.Block())
        V,A,TE=nc.vector,nc.scalar,nc.tensor
        def images(eng, stages, begin=None):
            with eng.Fori(0,B) as b:
                if begin: begin(b)
                lagged(eng,UNITS,stages,base=b*UNITS,last_first=True)
        @block.sync
        def _(sp):
            small=((cws[:,:,:],cw.partition_broadcast(P)),(wzs[:,:,:],wz),(hb[:,:],cb),(arow[:,:],alog_row.partition_broadcast(P)),(acol[:,:],alog_col),(ds[:,:],dcol))
            for d,s in small: sp.dma_start(d,s).then_inc(w_in,16)
            for d,n in ((tri[:,:],"tri"),(after[:,:],"after"),(same[:,:],"same"),(blk[:,:],"block"),(place[:,:,:],"place"),(expand[:,:,:],"expand"),(keep[:,:],"keep"),(perm[:,:],"perm")):
                sp.dma_start(d,consts[n]).then_inc(w_in,16)
            for k,w in enumerate((wx,wb,wc)):
                if k: sp.wait_ge(raw_used,k)
                sp.dma_start(raw[:,:,:],w).then_inc(raw_in,16)
            def load(b,j,q):
                pZ.before(sp,b*UNITS+j*2+q,2)
                sp.dma_start(xq[:,q,:],xs[:,bass.ds(b*PADT+j*T,T+2)]).then_inc(x_in[q],16)
                sp.dma_start(dr[:,q,:],dt[:,bass.ds(b*TOK+j*T,T)]).then_inc(d_in[q],16)
            def store(i,q):
                yy3.of(sp,i)
                sp.dma_start(y_out[q,:,bass.ds((i-q)*(T//2),T)],y3[:,q,:]).then_inc(out_s[q],16)
            def stored_before(i,q):
                sp.wait_ge(out_s[1-q],(i-1-(1-q))*8+16)
                sp.sem_inc(stored.sem,1)
            stored.start(sp)
            for j in range(2):
                for q in range(2): load(0,j,q)
            store(0,0); load(0,2,0)
            store(1,1); stored_before(1,1); load(0,2,1)
            with sp.Fori(3,TPI) as j:
                for q in range(2):
                    store(j*2+q-4,q); stored_before(j*2+q-4,q); load(0,j,q)
            with sp.Fori(1,B) as b:
                with sp.Fori(0,TPI) as j:
                    for q in range(2):
                        store(b*UNITS+j*2+q-4,q); stored_before(b*UNITS+j*2+q-4,q); load(b,j,q)
            for i in range(B*UNITS-4,B*UNITS): store(i,i%2); stored_before(i,i%2)
            for q in range(2): sp.wait_ge(out_s[q],8*B*UNITS)
        @block.tensor
        def _(pe):
            for f in (pT,pA,pX,pB,pC,pZ,segs,gs,ss,cds,ys,yos): f.start(pe)
            pe.wait_ge(w_in,16*14); pe.wait_ge(w_ready,1)
            def project(i,q):
                landed(pe,x_in,i,q); landed(pe,d_in,i,q)
                hC.before(pe,i,1)
                TE.matmul(pj[0][:,:],place[:,q,:],dr[:,q,:],start=True,stop=True).then_inc(pT.sem,1)
                hZ.before(pe,i,1)
                TE.matmul(pj[1][:,:],expand[:,q,:],dr[:,q,:],start=True,stop=True).then_inc(pA.sem,1)
                for k,(p,bank,free) in enumerate(((pX,0,dtt),(pB,1,stepped),(pC,0,hX))):
                    free.of(pe,i)
                    for tap in range(3):
                        last=TE.matmul(pj[bank][:,:],wk[:,k,q,tap,:],xq[:,q,tap:tap+T],start=(tap==0),stop=(tap==2))
                    last.then_inc(p.sem,1)
                hB.of(pe,i)
                TE.matmul(pj[1][:,:],wzs[:,q,:],xq[:,q,2:T+2],start=True,stop=True).then_inc(pZ.sem,1)
            def middle(i,q):
                dat.of(pe,i); yy1.before(pe,i,1)
                TE.matmul(YO[:,0:CH*H],same[:,:],dAT[:,q,:],start=True,stop=True).then_inc(cds.sem,1)
                rs.of(pe,i)
                for c in range(4):
                    exs.before(pe,i*4+c,2)
                    TE.matmul(sg[c%2][:,:],after[:,:],R[:,c*16:c*16+16,:],start=True,stop=True).then_inc(segs.sem,1)
                sB.of(pe,i); sC.of(pe,i); gm.before(pe,i,1)
                pe.sem_inc(pe_gate,1)
                for c in range(CH):
                    for s in range(SP):
                        q4=slice(32*s,32*s+32); k=slice(c*K,c*K+K)
                        last=TE.matmul(GP[q4,k],Bc[q4,q,k],Cc[q4,q,k],start=True,stop=True,skip_group_check=True)
                last.then_inc(gs.sem,1)
                btt.of(pe,i); dec.of(pe,i); scop.before(pe,i,1)
                pe.sem_inc(pe_gate,1)
                for c in range(CH):
                    for s in range(SP):
                        q4=slice(32*s,32*s+32); k=slice(c*K,c*K+K)
                        last=TE.matmul(SPs[q4,k],BT[q4,q,k],xdec[q4,k],start=True,stop=True,skip_group_check=True)
                last.then_inc(ss.sem,1)
            def outputs(i,q):
                yy2.before(pe,i,1); sX.of(pe,i)
                TE.matmul(YP[:,:],perm[:,:],X[:,q,:],start=True,stop=False,skip_group_check=True)
                ms.of(pe,i); xbs.of(pe,i)
                pe.sem_inc(pe_gate,1)
                for c in range(CH):
                    for h in range(H):
                        last=TE.matmul(YP[32*h:32*h+32,c*K:c*K+K],XB[:,q,c*H+h,:,:],M[:,q,c*H+h,:],start=False,stop=True,skip_group_check=True)
                last.then_inc(ys.sem,1)
                pbs.of(pe,i); pb0.of(pe,i); cde.of(pe,i)
                for c in range(CH):
                    last=TE.matmul(YO[:,c*K:c*K+K],PB[:,q,c,:,:,:],Cc[:,q,c*K:c*K+K],start=True,stop=True,skip_group_check=True)
                last.then_inc(yos.sem,1)
            images(pe,[project,middle,outputs])
        @block.scalar
        def _(act):
            A.preload_act_table_set("exp_and_others")
            for f in (stepped,hX,hB,hC,hZ,exs,cde,eas,scop,xbs,pbs): f.start(act)
            act.wait_ge(w_in,16*14)
            A.activation(arow[:,:],arow[:,:],ACT.Exp)
            A.activation(acol[:,:],acol[:,:],ACT.Exp).then_inc(aexp,1)
            act.wait_ge(w_ready,1)
            def halves(i,q):
                pA.of(act,i); scn.before(act,i,2)
                A.activation(dA[:,q,:],pj[1][:,:],ACT.Copy,scale=acol[:,0:1]).then_inc(stepped.sem,1)
                for k,(p,bank,flag,used) in enumerate(((pX,0,hX,sX),(pB,1,hB,sB),(pC,0,hC,sC),(pZ,1,hZ,sZ))):
                    p.of(act,i); used.before(act,i,1)
                    kw=dict(bias=hb[:,k:k+1]) if k<3 else {}
                    A.activation(half[:,k,:],pj[bank][:,:],ACT.Identity,scale=0.5,**kw)
                    A.activation(tan[:,k,:],pj[bank][:,:],ACT.Tanh,scale=0.5,**kw).then_inc(flag.sem,1)
            def middle(i,q):
                cds.of(act,i); d0.before(act,i,1); tm.before(act,i,1)
                A.activation(cd[:,:],YO[:,0:CH*H],ACT.Exp).then_inc(cde.sem,1)
                ms.before(act,i,1); dec.before(act,i,1)
                for c in range(4):
                    segs.of(act,i*4+c)
                    A.activation(EX[:,c*16:c*16+16,:],sg[c%2][:,:].rearrange("p (a l) -> p a l",l=K),ACT.Exp).then_inc(exs.sem,1)
                scn.of(act,i); yy1.before(act,i,2)
                A.activation(EA[:,q,:],ac[:,q,:],ACT.Exp).then_inc(eas.sem,1)
                xd.of(act,i); ys.before(act,i,2)
                for s in range(SP):
                    last=A.activation(XB[:,q,:,s,:],xdt[:,q,:].rearrange("p (a d) -> p a d",d=HD),ACT.Copy,scale=blk[:,s:s+1])
                last.then_inc(xbs.sem,1)
                ss.of(act,i); sts.before(act,i,1)
                A.copy(S1[:,:,:],SPs[:,:].rearrange("p (c x) -> p x c",x=32)).then_inc(scop.sem,1)
                sts.of(act,i); yos.before(act,i,2)
                for s in range(SP):
                    last=A.activation(PB[:,q,1:CH,:,s,:],ST[:,q,:].rearrange("p (h x c) -> p c h x",h=H,c=CH)[:,0:CH-1,:,:],ACT.Copy,scale=blk[:,s:s+1])
                last.then_inc(pbs.sem,1)
            images(act,[halves,middle,lambda i,q:None])
        @block.vector
        def _(dve):
            for f in (dtt,dat,rs,scn,sX,sB,sC,sZ,xtt,btt,xd,gm,dec,ms,d0,tm,pb0,s1,sts,car,yy1,yy2,yy3): f.start(dve)
            dve.wait_ge(w_in,16*14); dve.wait_ge(aexp,1)
            for k in range(3):
                dve.wait_ge(raw_in,16*(k+1))
                for q in range(2):
                    for tap in range(3):
                        last=V.tensor_tensor(wk[:,k,q,tap,:],raw[:,q,:],cws[:,k*3+tap,:],ALU.mult)
                last.then_inc(raw_used,1)
            V.tensor_scalar(arow[:,:],arow[:,:],-1.0,None,ALU.mult)
            V.tensor_scalar(acol[:,:],acol[:,:],-1.0,None,ALU.mult)
            V.tensor_scalar(hb[:,:],hb[:,:],0.5,None,ALU.mult)
            V.memset(D0[:,:,:],0.0)
            V.tensor_scalar(perm[:,:],perm[:,:],ds[:,0:1],None,ALU.mult).then_inc(w_ready,1)
            dve.wait_ge(w_ready,1)
            trib=lambda n: tri[:,:].unsqueeze(1).broadcast_to([P,n,K])
            def ahead(i,q):
                pT.of(dve,i); xd.before(dve,i,2)
                V.transpose(dtT[:,q,:],pj[0][:,:]).then_inc(dtt.sem,1)
                dtt.of(dve,i); cds.before(dve,i,2)
                d=dtT[:,q,:].rearrange("p (c x) -> p c x",x=32)[:,:,0:H]
                V.tensor_tensor(dAT[:,q,:].rearrange("p (c h) -> p c h",h=H),d,arow[:,:].unsqueeze(1).broadcast_to([P,CH,H]),ALU.mult).then_inc(dat.sem,1)
                dat.of(dve,i); segs.of(dve,i*4-1)
                V.tensor_tensor(R[:,:,:],dAT[:,q,:].unsqueeze(2).broadcast_to([P,CH*H,K]),trib(CH*H),ALU.mult).then_inc(rs.sem,1)
                stepped.of(dve,i); eas.before(dve,i,2)
                V.tensor_tensor_scan(ac[:,q,:],keep[:,:],dA[:,q,:],0.0,ALU.mult,ALU.add).then_inc(scn.sem,1)
                for k,(h_,s_,o) in enumerate(((hX,sX,X),(hB,sB,Bc),(hC,sC,Cc),(hZ,sZ,Z))):
                    h_.of(dve,i)
                    if k==0: ys.before(dve,i,2)
                    if k==1: gs.before(dve,i,2)
                    if k==2: yos.before(dve,i,2)
                    if k==3: yy3.before(dve,i,2)
                    V.scalar_tensor_tensor(o[:,q,:],tan[:,k,:],1.0,half[:,k,:],ALU.add,ALU.mult).then_inc(s_.sem,1)
                sX.of(dve,i); xd.before(dve,i,1)
                V.transpose(XT[:,:],X[:,q,:]).then_inc(xtt.sem,1)
                sB.of(dve,i); ss.before(dve,i,2)
                V.transpose(BT[:,q,:],Bc[:,q,:]).then_inc(btt.sem,1)
                xtt.of(dve,i); xbs.before(dve,i,2); dec.before(dve,i,2)
                V.tensor_tensor(xdt[:,q,:].rearrange("p (c h d) -> p c h d",h=H,d=HD),XT[:,:].rearrange("p (c h d) -> p c h d",h=H,d=HD),d.unsqueeze(3).broadcast_to([P,CH,H,HD]),ALU.mult).then_inc(xd.sem,1)
            def middle(i,q):
                exs.of(dve,i*4+3); xd.of(dve,i); ss.before(dve,i,1)
                V.tensor_tensor(xdec[:,:].rearrange("p (a d) -> p a d",d=HD),xdt[:,q,:].rearrange("p (a d) -> p a d",d=HD),EX[:,:,K-1:K].broadcast_to([P,CH*H,HD]),ALU.mult).then_inc(dec.sem,1)
                gs.of(dve,i); ms.before(dve,i,1)
                V.tensor_tensor(Gm[:,:].rearrange("p (c l) -> p c l",l=K),GP[:,:].rearrange("p (c l) -> p c l",l=K),trib(CH),ALU.mult).then_inc(gm.sem,1)
                gm.of(dve,i); ys.before(dve,i,2)
                V.tensor_tensor(M[:,q,:,:].rearrange("p (c h) l -> p c h l",h=H),EX[:,:,:].rearrange("p (c h) l -> p c h l",h=H),Gm[:,:].rearrange("p (c l) -> p c l",l=K).unsqueeze(2).broadcast_to([P,CH,H,K]),ALU.mult).then_inc(ms.sem,1)
                cde.of(dve,i); sts.before(dve,i,1)
                cv=cd[:,:].rearrange("p (c h) -> p h c",h=H)
                V.tensor_copy(D0[:,:,1:CH].rearrange("p (h x) c -> p h x c",h=H),cv[:,:,1:CH].unsqueeze(2).broadcast_to([P,H,HD,CH-1])).then_inc(d0.sem,1)
                s1.before(dve,i,1); car.before(dve,i,1)
                V.tensor_tensor(tmp[:,:].rearrange("p (h x) -> p h x",h=H),carry[:,q,:].rearrange("p (h x) -> p h x",h=H),cv[:,:,0:1].broadcast_to([P,H,HD]),ALU.mult).then_inc(tm.sem,1)
                yos.before(dve,i,2)
                V.tensor_tensor(PB[:,q,0,:,:,:],carry[:,q,:].rearrange("p (h x) -> p h x",h=H).unsqueeze(2).broadcast_to([P,H,SP,HD]),blk[:,:].unsqueeze(1).unsqueeze(3).broadcast_to([P,H,SP,HD]),ALU.mult).then_inc(pb0.sem,1)
                scop.of(dve,i); tm.of(dve,i)
                V.tensor_tensor(S1[:,:,0],S1[:,:,0],tmp[:,:],ALU.add).then_inc(s1.sem,1)
                s1.of(dve,i); d0.of(dve,i); pbs.before(dve,i,2)
                V.tensor_tensor_scan(ST[:,q,:],D0[:,:,:].rearrange("p x c -> p (x c)"),S1[:,:,:].rearrange("p x c -> p (x c)"),0.0,ALU.mult,ALU.add).then_inc(sts.sem,1)
                sts.of(dve,i); pb0.of(dve,i)
                V.tensor_copy(carry[:,q,:],ST[:,q,:].rearrange("p (x c) -> p x c",c=CH)[:,:,CH-1]).then_inc(car.sem,1)
            def finish(i,q):
                yos.of(dve,i); eas.of(dve,i); yy2.before(dve,i,1)
                V.tensor_tensor(y1[:,:],YO[:,:],EA[:,q,:],ALU.mult).then_inc(yy1.sem,1)
                yy1.of(dve,i); ys.of(dve,i); yy3.before(dve,i,1)
                V.tensor_tensor(y2[:,:],YP[:,:],y1[:,:],ALU.add).then_inc(yy2.sem,1)
                yy2.of(dve,i); sZ.of(dve,i); stored.before(dve,i,2)
                V.tensor_tensor(y3[:,q,:],y2[:,:],Z[:,q,:],ALU.mult).then_inc(yy3.sem,1)
            def begin(b):
                car.of(dve,b*UNITS-1)
                V.memset(carry[:,:,:],0.0).then_inc(reset,1)
                dve.wait_ge(reset,b+1)
            images(dve,[ahead,middle,finish],begin)
        if placed is not None:
            scatter=Scatter(nc,r,placed,rec,0,COLS//(2*SHALF))
            block.gpsimd(scatter.pool)

def core_consts():
    p=np.arange(P); f=np.float32
    tri=(p[:,None]%K<=np.arange(K)[None]).astype(f)
    same=(p[:,None]//32==p[None]//32).astype(f)
    after=(same*(p[:,None]%32>p[None]%32)).astype(f)
    block=(p[:,None]//32==np.arange(4)[None]).astype(f)
    place=np.zeros((NDT,2,P),f); expand=np.zeros((NDT,2,P),f); perm=np.zeros((P,P),f)
    for q in range(2):
        for h in range(4):
            for s_ in range(4):
                place[q*16+h*4+s_,q,s_*32+h]=1
                expand[q*16+h*4+s_,q,h*32+s_*8:h*32+s_*8+8]=1
                for d in range(8): perm[s_*32+h*8+d,h*32+s_*8+d]=1
    keep=np.ones((P,T),f); keep[:,::K]=0
    return dict(tri=tri,after=after,same=same,block=block,place=place,expand=expand,keep=keep,perm=perm)
def core_weights(W_in,conv_w,conv_b,A_log,D):
    f=np.float32; wx,wb,wc,wz=[np.zeros((P,2,P),f) for _ in range(4)]; wdt=np.zeros((P,NDT),f)
    for q in range(2):
        for s_ in range(4):
            rows=slice((q*4+s_)*16,(q*4+s_)*16+16)
            for w,o in ((wx,32),(wb,64),(wc,96)): w[rows,q,s_*32:s_*32+32]=W_in[:,o:o+32]
            for h in range(4):
                wz[rows,q,h*32+s_*8:h*32+s_*8+8]=W_in[:,h*8:h*8+8]
                wdt[rows,q*16+h*4+s_]=W_in[:,128+h]
    cw=conv_w[:,0,:].reshape(3,32,3)
    cw=np.tile(cw.transpose(0,2,1),(1,1,4)).reshape(9,P)
    cb=np.tile(conv_b.reshape(3,1,32),(1,4,1)).reshape(3,P).T
    hsp=np.repeat(A_log,32)[:,None]
    dcol=np.tile(np.repeat(D,8),4)[:,None]
    return dict(wx=wx,wb=wb,wc=wc,wz=wz,cw=np.ascontiguousarray(cw),cb=np.ascontiguousarray(cb),alog_row=A_log,alog_col=np.ascontiguousarray(hsp),dcol=np.ascontiguousarray(dcol)),wdt


PADT=TOK+2
def mamba_out(nc, y, xs, x, wo, rms, skip, lnw, lnb, pw, pb, same_mean, ones, x_out, tag="m3"):
    with ExitStack() as ctx:
        ctx.enter_context(nc.cleanup_on_exit())
        r=Room(nc,ctx,tag)
        yt=r.sb("y",[P,2,2,T]); xst=r.sb("xs",[P,2,T]); xt=r.sb("x",[P,2,T]); sq=r.sb("sq",[P,2,2,T]); lg=r.sb("lg",[P,2,T]); rs=r.sb("rs",[P,2,2,T]); yn=r.sb("yn",[P,2,2,T]); ym=r.sb("ym",[P,2,T]); nn=r.sb("nn",[P,2,T]); xo=r.sb("xo",[P,2,T])
        wos=r.sb("wo",[P,2,P]); rm=r.sb("rms",[P,1]); sk=r.sb("skip",[P,1]); lw=r.sb("lw",[P,1]); lb=r.sb("lb",[P,1]); pws=r.sb("pw",[P,P]); pbs=r.sb("pb",[P,1]); sm=r.sb("sm",[P,P]); mw=r.sb("mw",[P,P]); eps=r.sb("eps",[P,1])
        rP=r.pb("rP",[P,2,T]); oP=r.pb("oP",[P,T]); qP=r.pb("qP",[P,T])
        w_in=r.sem("w_in"); ready=r.sem("ready"); y_in=r.pair("y_in"); s_in=r.pair("s_in"); x_in=r.pair("x_in"); out=Stores(r,"out")
        squared,meaned,logged,rooted,scaled,mixed,skipped,affine,projected,added=r.flags("squared meaned logged rooted scaled mixed skipped affine projected added")
        nm=Norm(nc,r,"n",mw[:,:],eps[:,0:1],lambda i,par:ym[:,par,:],lambda e,i,par: skipped.of(e,i),lambda i,par:nn[:,par,:],lambda e,i,par: projected.before(e,i,2))
        block=ctx.enter_context(nc.Block())
        @block.sync
        def _(sp):
            for d,s in ((wos[:,:,:],wo),(rm[:,:],rms),(sk[:,:],skip.partition_broadcast(P)),(lw[:,:],lnw),(lb[:,:],lnb),(pws[:,:],pw),(pbs[:,:],pb),(sm[:,:],same_mean),(mw[:,:],ones)): sp.dma_start(d,s).then_inc(w_in,16)
            with sp.Fori(0,B) as b:
                with sp.Fori(0,TPI//2) as t:
                    for par in range(2):
                        i=b*TPI+t*2+par
                        scaled.before(sp,i,2)
                        sp.dma_start(yt[:,par,:,:],y.rearrange("q p n -> p q n")[:,:,bass.ds(i*T,T)]).then_inc(y_in[par],16)
                        skipped.before(sp,i,2)
                        sp.dma_start(xst[:,par,:],xs[:,bass.ds(b*PADT+(t*2+par)*T+2,T)]).then_inc(s_in[par],16)
        @block.tensor
        def _(pe):
            nm.pe_start(pe)
            for f in (meaned,mixed,projected): f.start(pe)
            pe.wait_ge(w_in,16*9); pe.wait_ge(ready,1)
            def mean_square(i,par):
                squared.of(pe,i); logged.before(pe,i,1)
                for q in range(2): last=nc.tensor.matmul(rP[:,q,:],sm[:,:],sq[:,par,q,:],start=True,stop=True)
                last.then_inc(meaned.sem,1)
            def mix(i,par):
                scaled.of(pe,i); skipped.before(pe,i,1)
                for q in range(2): last=nc.tensor.matmul(oP[:,:],wos[:,q,:],yn[:,par,q,:],start=(q==0),stop=(q==1))
                last.then_inc(mixed.sem,1)
            def project(i,par):
                affine.of(pe,i); added.before(pe,i,1)
                nc.tensor.matmul(qP[:,:],pws[:,:],nn[:,par,:],start=True,stop=True).then_inc(projected.sem,1)
            lagged(pe,TILES,[mean_square,mix,lambda i,p:nm.pe_mean(pe,i,p),lambda i,p:nm.pe_var(pe,i,p),project])
        @block.scalar
        def _(act):
            nc.scalar.preload_act_table_set("natural_log_exp_and_others")
            nm.act_start(act)
            for f in (squared,logged,rooted): f.start(act)
            act.wait_ge(ready,1)
            def square(i,par):
                landed(act,y_in,i,par); meaned.before(act,i,2)
                nc.scalar.activation(sq[:,par,:,:],yt[:,par,:,:],ACT.Square).then_inc(squared.sem,1)
            def root(i,par):
                meaned.of(act,i)
                rooted.before(act,i,1); scaled.before(act,i,2)
                for q in range(2): last=nc.scalar.activation(rs[:,par,q,:],rP[:,q,:],ACT.Ln,bias=eps[:,0:1])
                last.then_inc(logged.sem,1)
                logged.of(act,i)
                nc.scalar.activation(rs[:,par,:,:],rs[:,par,:,:],ACT.Exp,scale=-0.5).then_inc(rooted.sem,1)
            lagged(act,TILES,[square,root,lambda i,p:None,lambda i,p:nm.act_square(act,i,p),lambda i,p:nm.act_root(act,i,p)])
        @block.vector
        def _(dve):
            nm.dve_start(dve)
            for f in (scaled,skipped,affine,added): f.start(dve)
            dve.wait_ge(w_in,16*9)
            nc.vector.memset(eps[:,:],1e-5)
            for q in range(2): last=nc.vector.tensor_scalar(wos[:,q,:],wos[:,q,:],rm[:,0:1],None,ALU.mult)
            last.then_inc(ready,1)
            def scale(i,par):
                rooted.of(dve,i); mixed.before(dve,i,2)
                nc.vector.tensor_tensor(yn[:,par,:,:],yt[:,par,:,:],rs[:,par,:,:],ALU.mult).then_inc(scaled.sem,1)
            def add_skip(i,par):
                mixed.of(dve,i); landed(dve,s_in,i,par); nm.centred.before(dve,i,2)
                nc.vector.scalar_tensor_tensor(ym[:,par,:],xst[:,par,:],sk[:,0:1],oP[:,:],ALU.mult,ALU.add).then_inc(skipped.sem,1)
            def norm(i,par):
                nm.dve_scale(dve,i,par)
                nm.normed.of(dve,i)
                nc.vector.tensor_scalar(nn[:,par,:],nn[:,par,:],lw[:,0:1],lb[:,0:1],ALU.mult,ALU.add).then_inc(affine.sem,1)
            def add_x(i,par):
                projected.of(dve,i); landed(dve,x_in,i,par); out.done.before(dve,i,2)
                nc.vector.scalar_tensor_tensor(xo[:,par,:],qP[:,:],pbs[:,0:1],xt[:,par,:],ALU.add,ALU.add).then_inc(added.sem,1)
            lagged(dve,TILES,[scale,add_skip,lambda i,p:nm.dve_centre(dve,i,p),norm,add_x])
        @block.gpsimd
        def _(pool):
            def load(i,par):
                pool.dma_start(xt[:,par,:],x[:,bass.ds(i*T,T)]).then_inc(x_in[par],16)
            def store(i,par):
                added.of(pool,i)
                pool.dma_start(x_out[:,bass.ds(i*T,T)],xo[:,par,:]).then_inc(out.sems[par],16)
            out.start(pool)
            load(0,0); load(1,1)
            with pool.Fori(0,TILES//2-1) as t:
                for par in range(2):
                    store(t*2+par,par); load(t*2+par+2,par); out.landed(pool,t*2+par,par)
            for par in range(2): store(TILES-2+par,par); out.landed(pool,TILES-2+par,par)
def out_weights(W_out,rms_w):
    wo=np.zeros((P,2,P),np.float32); rms=np.zeros((P,1),np.float32)
    for q in range(2):
        for h in range(4):
            for s in range(4):
                for d in range(8):
                    k=h*32+s*8+d
                    wo[k,q,(q*4+s)*16:(q*4+s)*16+16]=W_out[h*8+d]; rms[k]=rms_w[h*8+d]
    p=np.arange(P); sm=((p[:,None]//8%4)==(p[None]//8%4)).astype(np.float32)/32
    return wo,rms,sm


def build(nc, a, out):
    dram=lambda n,s,d=f32: nc.dram_tensor(n,s,d).ap()
    consts={k[2:]: v for k,v in a.items() if k.startswith("c_")}
    rec=[dram(f"rec{l}",[E,2],i32) for l in range(2)]
    start=[dram(f"start{l}",[P,HI]) for l in range(2)]; deg=[dram(f"deg{l}",[P,HI]) for l in range(2)]
    placed=dram("placed",[P,COLS,3],i32)
    x1,x2,x3=dram("x1",[P,NODES]),dram("x2",[P,NODES]),dram("x3",[P,NODES])
    xn,table,gates=dram("xn",[P,NODES]),dram("table",[NODES,HW]),dram("gates",[EX,NODES])
    by_edge=edge_arrays(nc,"e")
    def project(l,x): heads(nc,x,a[f"wg{l}"],a[f"att{l}"],a["c_ones"],xn,table,tag=f"h{l}")
    def attend_and_feed(l,x,x_out):
        attention(nc,rec[l],start[l],deg[l],table,a[f"bgat{l}"],a[f"gamma{l}"],a[f"beta{l}"],a["c_eye"],gates,by_edge,tag=f"g{l}")
        experts(nc,x,xn,gates,a[f"w1_{l}"],a[f"b1_{l}"],a[f"w2_{l}"],a[f"b2_{l}"],x_out,tag=f"f{l}")
    def first_part(room,chunks): return None,Scatter(nc,room,placed,rec[0],0,FIRST_TURNS,chunks).pool
    sort_edges(nc,a["edges0"],placed,start[0],deg[0],first_part,tag="s0")
    def second_part(room): return Scatter(nc,room,placed,rec[0],FIRST_TURNS,COLS//(2*SHALF)).pool
    involution(nc,a["x"],a["cw1"],a["cb1"],a["cwd"],a["cw2"],a["cbd"],a["cb2"],a["c_pick"],a["c_ones"],x1,second_part)
    project(0,x1)
    def gather_beside(room,chunks):
        g=gather_of(nc,room,rec[0],table,by_edge)
        return g.sync,g.pool
    sort_edges(nc,a["edges1"],placed,start[1],deg[1],gather_beside,tag="s1")
    attend_and_feed(0,x1,x2)
    xs,dt,y=dram("xs",[P,B*PADT]),dram("dt",[NDT,NODES]),dram("y",[2,P,NODES])
    mamba_in(nc,x2,a["lnw"],a["lnb"],a["wdt"],a["dtb"],a["c_ones"],xs,dt)
    mamba_core(nc,xs,dt,a["wx"],a["wb"],a["wc"],a["wz"],a["cw"],a["cb"],a["alog_row"],a["alog_col"],a["dcol"],consts,y,placed,rec[1])
    mamba_out(nc,y,xs,x2,a["wo"],a["rms"],a["skip"],a["lnw"],a["lnb"],a["pw"],a["pb"],a["c_same_mean"],a["c_ones"],x3)
    project(1,x3)
    gather_alone(nc,rec[1],table,by_edge)
    attend_and_feed(1,x3,out)


def laid_out(i):
    tok=np.ascontiguousarray
    col=lambda v: tok(v.reshape(-1,1))
    a={}
    a["x"]=tok(i["x"].transpose(1,0,2,3).reshape(P,NODES))
    a["cw1"]=tok(np.tile(i["L0_conv_w1"].T,(1,3))); a["cb1"]=col(np.tile(i["L0_conv_b1"],3))
    a["cwd"]=tok(i["L0_conv_wd"][:,0].transpose(2,0,1).reshape(3*RED,3))
    a["cw2"]=tok(np.tile(i["L0_conv_w2"].T,(3,1))); a["cbd"]=col(i["L0_conv_bd"]); a["cb2"]=col(i["L0_conv_b2"])
    for l in range(2):
        p=f"L{l}_ffn_"
        a[f"edges{l}"]=tok(i[p+"edge_index"])
        a[f"wg{l}"]=tok(i[p+"W_gat"]); a[f"att{l}"]=tok(np.concatenate([i[p+"att_src"].ravel(),i[p+"att_dst"].ravel()]))
        a[f"bgat{l}"]=tok(i[p+"b_gat"]); a[f"gamma{l}"]=tok(i[p+"ln_gamma"]); a[f"beta{l}"]=tok(i[p+"ln_beta"])
        a[f"w1_{l}"]=tok(i[p+"W1"].transpose(1,0,2)); a[f"b1_{l}"]=tok(i[p+"b1"].reshape(EX,2,P).transpose(2,0,1))
        a[f"w2_{l}"]=tok(i[p+"W2"].reshape(EX,2,P,P).transpose(2,0,1,3)); a[f"b2_{l}"]=tok(i[p+"b2"].T)
    p="L1_conv_"
    ws,wdt=core_weights(i[p+"W_in"],i[p+"conv_w"],i[p+"conv_b"],i[p+"A_log"],i[p+"D"])
    a.update(ws); a["wdt"]=wdt
    a["dtb"]=col(np.tile(np.repeat(i[p+"dt_bias"],4),2))
    a["wo"],a["rms"],same_mean=out_weights(i[p+"W_out"],i[p+"rms_w"])
    a["skip"]=tok(i[p+"skip_scale"]); a["lnw"]=col(i[p+"ln_w"]); a["lnb"]=col(i[p+"ln_b"]); a["pw"]=tok(i[p+"proj_w"]); a["pb"]=col(i[p+"proj_b"])
    c=core_consts()
    c["same_mean"]=same_mean; c["ones"]=np.full((P,P),1/P,np.float32); c["eye"]=np.eye(P,dtype=np.float32)
    pick=np.zeros((GK,9,P),np.float32)
    for k in range(9):
        for ch in range(P): pick[(ch//16)*9+k,k,ch]=1
    c["pick"]=pick
    a.update({"c_"+k: v for k,v in c.items()})
    return a


def kernel(**inputs):
    import numpy as _np
    import concourse.bacc as _bacc
    from concourse import mybir as _mybir
    from concourse.bass_utils import run_bass_kernel_spmd as _run

    nc=_bacc.Bacc("TRN2", target_bir_lowering=False, num_devices=1)
    arrays,args={},{}
    for name,v in laid_out({k: _np.asarray(v) for k,v in inputs.items()}).items():
        arrays[f"in_{name}"]=v
        args[name]=nc.dram_tensor(f"in_{name}",v.shape,_mybir.dt.from_np(v.dtype),kind="ExternalInput").ap()
    out=nc.dram_tensor("out_x",(P,NODES),_mybir.dt.float32,kind="ExternalOutput").ap()
    build(nc,args,out)
    r=_run(nc,[arrays],core_ids=[0])
    got=r.results[0]["out_x"]
    return _np.ascontiguousarray(got.reshape(P,B,W,W).transpose(1,0,2,3))
```

```python
import numpy as np
import concourse.bass as bass
from concourse import mybir
from contextlib import ExitStack

f32=mybir.dt.float32
u32=mybir.dt.uint32
i32=mybir.dt.int32
bf16=mybir.dt.bfloat16
ALU=mybir.AluOpType
ACT=mybir.ActivationFunctionType
AX=mybir.AxisListType
P=128
NODES=32768
B=8
TOK=4096
T=512
TILES=NODES//T
TPI=TOK//T
W=64
ROWS=T//W
LEAD=2

class Flag:
    def __init__(self, sem): self.sem=sem
    def start(self, eng): eng.sem_inc(self.sem, LEAD)
    def of(self, eng, i): eng.wait_ge(self.sem, i+LEAD+1)
    def before(self, eng, i, buffers): eng.wait_ge(self.sem, i+LEAD+1-buffers)

class Room:
    def __init__(self, nc, ctx, tag):
        self.nc,self.ctx,self.tag=nc,ctx,tag
        self.sems=[]
    def sb(self,n,s,d=f32):
        return self.ctx.enter_context(self.nc.sbuf_tensor(f"{self.tag}_{n}",s,d))
    def pb(self,n,s,d=f32):
        return self.ctx.enter_context(self.nc.psum_tensor(f"{self.tag}_{n}",s,d))
    def sem(self,n): return self.nc.alloc_semaphore(f"{self.tag}_{n}")
    def flags(self,names): return [Flag(self.sem(n)) for n in names.split()]
    def pair(self,n): return [self.sem(f"{n}0"),self.sem(f"{n}1")]

def landed(eng, sems, i, par):
    eng.wait_ge(sems[par], (i-par)*8+16)
class Stores:
    def __init__(self, room, name):
        self.sems=room.pair(name)
        self.done,=room.flags(name+"_done")
    def start(self, eng): self.done.start(eng)
    def landed(self, eng, i, par):
        landed(eng,self.sems,i,par)
        eng.sem_inc(self.done.sem,1)

class Rows:
    def __init__(self, room, name, half):
        self.half=half
        self.sems=[[room.sem(f"{name}{par}{k}") for k in range(2)] for par in range(2)]
    def of(self, k, par): return self.sems[par][k%2]
    def wait(self, eng, turns, par):
        for s in self.sems[par]: eng.wait_ge(s, turns*(8*self.half))

def paired(eng, n, body, peel=False):
    if peel:
        body(0,0)
        body(1,1)
    with eng.Fori(1 if peel else 0,n//2) as t:
        body(t*2,0)
        body(t*2+1,1)

def skewed(eng, n, ahead, body):
    ahead(0,0)
    with eng.Fori(0,n//2-1) as t:
        ahead(t*2+1,1)
        body(t*2,0)
        ahead(t*2+2,0)
        body(t*2+1,1)
    ahead(n-1,1)
    body(n-2,0)
    body(n-1,1)

class Norm:
    def __init__(self, nc, room, name, mean_w, eps, source, arrived, dest, dest_free):
        self.nc,self.eps,self.mean_w=nc,eps,mean_w
        self.source,self.arrived,self.dest,self.dest_free=source,arrived,dest,dest_free
        self.cen=room.sb(name+"_cen",[P,2,T])
        self.sq=room.sb(name+"_sq",[P,2,T])
        self.log=room.sb(name+"_log",[P,2,T])
        self.rstd=room.sb(name+"_rstd",[P,2,T])
        self.logged,=room.flags(name+"_logged")
        self.mean=room.pb(name+"_mean",[P,T])
        self.var=room.pb(name+"_var",[P,T])
        self.averaged,self.centred,self.squared,self.spread,self.scaled,self.normed=room.flags(
            " ".join(name+"_"+s for s in ("averaged","centred","squared","spread","scaled","normed")))
    def pe_start(self,pe):
        self.averaged.start(pe)
        self.spread.start(pe)
    def dve_start(self,dve):
        self.centred.start(dve)
        self.normed.start(dve)
    def act_start(self,act):
        self.squared.start(act)
        self.scaled.start(act)
        self.logged.start(act)
    def pe_mean(self,pe,i,par):
        self.arrived(pe,i,par)
        self.centred.before(pe,i,1)
        self.nc.tensor.matmul(self.mean[:,:],self.mean_w,self.source(i,par),start=True,stop=True).then_inc(self.averaged.sem,1)
    def pe_var(self,pe,i,par):
        self.squared.of(pe,i)
        self.logged.before(pe,i,1)
        self.nc.tensor.matmul(self.var[:,:],self.mean_w,self.sq[:,par,:],start=True,stop=True).then_inc(self.spread.sem,1)
    def dve_centre(self,dve,i,par):
        self.averaged.of(dve,i)
        self.normed.before(dve,i,2)
        self.squared.before(dve,i,2)
        self.nc.vector.tensor_tensor(self.cen[:,par,:],self.source(i,par),self.mean[:,:],ALU.subtract).then_inc(self.centred.sem,1)
    def act_square(self,act,i,par):
        self.centred.of(act,i)
        self.spread.before(act,i,2)
        self.nc.scalar.activation(self.sq[:,par,:],self.cen[:,par,:],ACT.Square).then_inc(self.squared.sem,1)
    def act_root(self,act,i,par):
        self.spread.of(act,i)
        self.normed.before(act,i,2)
        self.nc.scalar.activation(self.log[:,par,:],self.var[:,:],ACT.Ln,bias=self.eps).then_inc(self.logged.sem,1)
        self.logged.of(act,i)
        self.nc.scalar.activation(self.rstd[:,par,:],self.log[:,par,:],ACT.Exp,scale=-0.5).then_inc(self.scaled.sem,1)
    def dve_scale(self,dve,i,par):
        self.scaled.of(dve,i)
        self.dest_free(dve,i,par)
        self.nc.vector.tensor_tensor(self.dest(i,par),self.cen[:,par,:],self.rstd[:,par,:],ALU.mult).then_inc(self.normed.sem,1)

def lagged(eng, n, stages, base=0, last_first=False, order=None):
    depth=len(stages)
    k0=(depth-1)+(depth-1)%2
    order=[(j,stages[j]) for j in (order or range(depth)[::-1 if last_first else 1])]
    def step(k, par):
        for j,stage in order:
            if isinstance(k,int) and not 0<=k-j<n: continue
            i=k-j if isinstance(base,int) and base==0 else base+(k-j)
            stage(i,(par-j)%2)
    for k in range(k0): step(k,k%2)
    with eng.Fori(0,(n-k0)//2) as t:
        step(t*2+k0,0)
        step(t*2+k0+1,1)
    for k in range(n,n+depth-1): step(k,k%2)

E=524288
LO=128
HI=256
COLS=E//P
S=4
SRING=8
SLOTS=4
SHALF=64
FIRST_TURNS=23

def sort_edges(nc, edges, placed_dram, start_dram, deg_dram, beside, tag='s'):
    TURNS=COLS//SRING
    GROUPS=COLS//S
    with ExitStack() as ctx:
        ctx.enter_context(nc.cleanup_on_exit())
        sb=lambda n,s,d: ctx.enter_context(nc.sbuf_tensor(tag+n,s,d))
        pb=lambda n,s,d: ctx.enter_context(nc.psum_tensor(tag+n,s,d))
        sem=lambda n: nc.alloc_semaphore(tag+n)
        ei=sb("s_ei",[P,2,COLS],i32)
        rec=sb("s_rec",[P,COLS,3],i32)
        part=sb("s_part",[P,COLS],i32)
        lo=sb("s_lo",[P,COLS],f32)
        hi=sb("s_hi",[P,COLS],f32)
        iota_i=sb("s_iotai",[P,HI],i32)
        iota=sb("s_iota",[P,HI],bf16)
        pid_i=sb("s_pidi",[P,P],i32)
        ident=sb("s_ident",[P,P],bf16)
        identf=sb("s_identf",[P,P],f32)
        tri=sb("s_tri",[P,P],f32)
        zeros=sb("s_zeros",[P,2*HI],bf16)
        hots=sb("s_hots",[P,S,SLOTS,LO+HI],bf16)
        olo=hots[:,:,:,0:LO]
        ohi=hots[:,:,:,LO:LO+HI]
        dist=sb("s_dist",[P,2,LO+HI],bf16)
        oloT=sb("s_oloT",[P,S,P],bf16)
        oloTf=sb("s_oloTf",[P,2,S,P],f32)
        same=sb("s_same",[P,2,S,P],bf16)
        cnt=sb("s_cnt",[P,S,HI],f32)
        deg=sb("s_deg",[P,HI],f32)
        incl=sb("s_incl",[P,HI],f32)
        start=sb("s_start",[P,HI],f32)
        base=sb("s_base",[P,S,HI],f32)
        zf=sb("s_zf",[P,HI],f32)
        prod=sb("s_prod",[P,S,HI],f32)
        posf=sb("s_posf",[P,SRING],f32)
        neg=sb("s_neg",[P,4,P],bf16)
        cntP=pb("s_cntP",[P,S,HI],f32)
        TP=pb("s_TP",[P,S,P],bf16)
        AP_=pb("s_AP",[P,S,P],f32)
        PP=pb("s_PP",[P,S,HI],f32)
        edges_in=sem("edges_in")
        iotas=sem("iotas")
        consts=sem("consts")
        prep=sem("prep")
        hot_c=sem("hot_c")
        hot_a=sem("hot_a")
        measured=sem("measured")
        keyed=sem("keyed")
        counted=sem("counted")
        tot=sem("tot")
        offs=sem("offs")
        based=sem("based")
        tables_out=sem("tables_out")
        seeded=sem("seeded")
        hot=sem("hot")
        turned=sem("turned")
        turnedc=sem("turnedc")
        turnedf=sem("turnedf")
        pairs=sem("pairs")
        masked=sem("masked")
        ranks=sem("ranks")
        updated=sem("updated")
        cnt_copied=sem("cnt_copied")
        placed=sem("placed")
        posready=sem("posready")
        chunk_out=sem("chunk_out")
        chunks=sem("chunks")
        beside_sync,beside_pool=beside(Room(nc,ctx,tag),chunks)
        block=ctx.enter_context(nc.Block())

        @block.sync
        def _(sp):
            sp.dma_start(ei[:,:,:], edges.rearrange("a (p c) -> p a c", p=P)).then_inc(edges_in,16)
            if beside_sync: beside_sync(sp)
            sp.wait_ge(based,1)
            sp.dma_start(start_dram, start[:,:]).then_inc(tables_out,16)
            sp.dma_start(deg_dram, deg[:,:]).then_inc(tables_out,16)
            sp.wait_ge(tables_out,32)
            with sp.Fori(0,COLS//SHALF) as k:
                sp.wait_ge(posready,k*(SHALF//S)+SHALF//S)
                sp.dma_start(placed_dram[:,bass.ds(k*SHALF,SHALF),:],rec[:,bass.ds(k*SHALF,SHALF),:]).then_inc(chunk_out,16)
                sp.wait_ge(chunk_out,k*16+16)
                sp.sem_inc(chunks,1)

        @block.gpsimd
        def _(pool):
            pool.iota(iota_i[:,:], pattern=[[1,HI]], base=0, channel_multiplier=0).then_inc(iotas,1)
            pool.iota(pid_i[:,:], pattern=[[1,P]], base=0, channel_multiplier=-1).then_inc(iotas,1)
            beside_pool(pool)

        def onehots(dve,c,slot,par,done):
            nc.vector.tensor_scalar(olo[:,slot,par,:], iota[:,0:LO], lo[:,bass.ds(c,1)], None, ALU.is_equal)
            nc.vector.tensor_scalar(ohi[:,slot,par,:], iota[:,:], hi[:,bass.ds(c,1)], None, ALU.is_equal).then_inc(done,1)

        @block.vector
        def _(dve):
            dve.wait_ge(iotas,2)
            nc.vector.tensor_copy(iota[:,:],iota_i[:,:])
            nc.vector.tensor_scalar(ident[:,:],pid_i[:,:],0,None,ALU.is_equal)
            nc.vector.tensor_scalar(identf[:,:],pid_i[:,:],0,None,ALU.is_equal)
            nc.vector.tensor_scalar(tri[:,:],pid_i[:,:],0,None,ALU.is_gt)
            for s in range(4):
                nc.vector.tensor_scalar(neg[:,s,:],pid_i[:,:],0,-1.0,ALU.is_le,ALU.mult)
            nc.vector.memset(zf[:,:],0.0)
            nc.vector.memset(zeros[:,:],0.0).then_inc(consts,1)
            dve.wait_ge(edges_in,16)
            nc.vector.tensor_copy(rec[:,:,0],ei[:,0,:])
            nc.vector.tensor_copy(rec[:,:,1],ei[:,1,:])
            nc.vector.tensor_single_scalar(part[:,:],ei[:,1,:],8,ALU.logical_shift_right).then_inc(prep,1)
            dve.wait_ge(prep,1)
            nc.vector.tensor_copy(lo[:,:],part[:,:]).then_inc(prep,1)
            dve.wait_ge(prep,2)
            nc.vector.tensor_single_scalar(part[:,:],ei[:,1,:],HI-1,ALU.bitwise_and).then_inc(prep,1)
            dve.wait_ge(prep,3)
            nc.vector.tensor_copy(hi[:,:],part[:,:]).then_inc(prep,1)
            dve.wait_ge(prep,4)
            dve.wait_ge(consts,1)
            dve.sem_inc(keyed,1)
            def count(i,par):
                if not isinstance(i,int): dve.wait_ge(counted,i-1)
                for s in range(S-1): onehots(dve,i*S+s,s,par,hot_c)
            paired(dve,2*TURNS,count,peel=True)
            dve.wait_ge(counted,TURNS*2)
            nc.vector.tensor_copy(cnt[:,:,:],cntP[:,:,:]).then_inc(tot,1)
            dve.wait_ge(tot,1)
            nc.vector.tensor_tensor(deg[:,:],cnt[:,0,:],cnt[:,1,:],ALU.add).then_inc(tot,1)
            for s in range(2,S):
                dve.wait_ge(tot,s)
                nc.vector.tensor_tensor(deg[:,:],deg[:,:],cnt[:,s,:],ALU.add).then_inc(tot,1)
            dve.wait_ge(tot,S)
            nc.vector.tensor_tensor_scan(incl[:,:],deg[:,:],zf[:,:],0.0,ALU.add,ALU.add).then_inc(tot,1)
            dve.wait_ge(offs,1)
            dve.wait_ge(tot,S+1)
            nc.vector.scalar_tensor_tensor(start[:,:],incl[:,:],PP[:,0,0:1],deg[:,:],ALU.add,ALU.subtract).then_inc(based,1)
            dve.wait_ge(based,1)
            nc.vector.tensor_copy(base[:,0,:],start[:,:]).then_inc(based,1)
            for s in range(1,S):
                dve.wait_ge(based,s+1)
                nc.vector.tensor_tensor(base[:,s,:],base[:,s-1,:],cnt[:,s-1,:],ALU.add).then_inc(based,1)
            def hots_of(g,slot):
                for s in range(S): onehots(dve,g*S+s,s,slot,hot)
            for g in range(3): hots_of(g,g)
            def group(g,slot,next_hots=True):
                par=slot%2
                def places(h):
                    dve.wait_ge(ranks,g*2+h+1)
                    for s in (2*h,2*h+1):
                        nc.vector.tensor_tensor_reduce(out=prod[:,s,:],in0=PP[:,s,:],in1=ohi[:,s,slot,:],scale=1.0,scalar=0.0,op0=ALU.mult,op1=ALU.add,accum_out=posf[:,par*S+s:par*S+s+1]).then_inc(placed,1)
                places(0)
                places(1)
                if next_hots:
                    if not (isinstance(g,int) and g==0): dve.wait_ge(updated,g*2)
                    hots_of(g+3,(slot+3)%SLOTS)
                dve.wait_ge(placed,g*S+S)
                nc.vector.tensor_copy(rec[:,bass.ds(g*S,S),2],posf[:,par*S:par*S+S]).then_inc(posready,1)
            for j in range(SLOTS): group(j,j)
            with dve.Fori(1,GROUPS//SLOTS-1) as u:
                for j in range(SLOTS): group(u*SLOTS+j,j)
            for j in range(SLOTS): group(GROUPS-SLOTS+j,j,next_hots=j<1)

        @block.scalar
        def _(act):
            def copy_cnt(h):
                nc.scalar.copy(cnt[:,2*h:2*h+2,:],cntP[:,2*h:2*h+2,:]).then_inc(cnt_copied,1)
            def copy_turned(par):
                nc.scalar.copy(oloT[:,:,:],TP[:,:,:]).then_inc(turnedc,1)
                nc.scalar.copy(oloTf[:,par,:,:],TP[:,:,:]).then_inc(turnedf,1)
            def mask(g,par):
                act.wait_ge(pairs,g+1)
                nc.scalar.activation(same[:,par,:,:],AP_[:,:,:],ACT.Relu).then_inc(masked,1)
            act.wait_ge(keyed,1)
            def count(i,par):
                c=i*S+(S-1)
                nc.scalar.activation(dist[:,par,0:LO],iota[:,0:LO],ACT.Square,scale=-1.0,bias=lo[:,bass.ds(c,1)])
                nc.scalar.activation(dist[:,par,LO:LO+HI],iota[:,:],ACT.Square,scale=-1.0,bias=hi[:,bass.ds(c,1)]).then_inc(measured,1)
                act.wait_ge(measured,i+1)
                if not isinstance(i,int): act.wait_ge(counted,i-1)
                nc.scalar.activation(hots[:,S-1,par,:],dist[:,par,:],ACT.Relu,scale=-1.0,bias=1.0).then_inc(hot_a,1)
            paired(act,2*TURNS,count,peel=True)
            for h in range(2):
                act.wait_ge(seeded,h+1)
                copy_cnt(h)
            act.wait_ge(turned,1)
            copy_turned(0)
            mask(0,0)
            def group(g,par):
                act.wait_ge(turned,g+2)
                act.wait_ge(pairs,g+1)
                copy_turned(1-par)
                act.wait_ge(updated,g*2+1)
                copy_cnt(0)
                mask(g+1,1-par)
                act.wait_ge(updated,g*2+2)
                copy_cnt(1)
            with act.Fori(0,TURNS-1) as t:
                group(t*2,0)
                group(t*2+1,1)
            group(GROUPS-2,0)

        @block.tensor
        def _(pe):
            pe.wait_ge(consts,1)
            for b in range(2):
                nc.tensor.matmul(cntP[:,2*b:2*b+2,:],zeros[:,0:P],zeros[:,:],start=True,stop=False,skip_group_check=True)
            def count(i,par):
                for s in range(S):
                    if s<S-1: pe.wait_ge(hot_c,i*(S-1)+s+1)
                    else: pe.wait_ge(hot_a,i+1)
                    last=nc.tensor.matmul(cntP[:,s,:],olo[:,s,par,:],ohi[:,s,par,:],start=False,stop=False,skip_group_check=True)
                last.then_inc(counted,1)
            paired(pe,2*TURNS,count)
            pe.wait_ge(tot,S+1)
            nc.tensor.matmul(PP[:,0,0:1],tri[:,:],incl[:,HI-1:HI],start=True,stop=True).then_inc(offs,1)
            pe.wait_ge(based,S+1)
            for b in range(2):
                nc.tensor.matmul(cntP[:,2*b:2*b+2,:],identf[:,:],base[:,2*b:2*b+2,:],start=True,stop=False,skip_group_check=True).then_inc(seeded,1)
            def turn_hots(g,slot):
                pe.wait_ge(hot,g*S+S)
                if not (isinstance(g,int) and g==0): pe.wait_ge(turnedf,g)
                for s in range(S):
                    last=nc.tensor.transpose(TP[:,s,:],olo[:,s,slot,:],ident[:,:])
                last.then_inc(turned,1)
            def pair_up(g):
                pe.wait_ge(turnedc,g+1)
                nc.tensor.matmul(AP_[:,:,:],ident[:,:],neg[:,:,:],start=True,stop=False,skip_group_check=True)
                for s in range(S):
                    last=nc.tensor.matmul(AP_[:,s,:],oloT[:,s,:],oloT[:,s,:],start=False,stop=True,skip_group_check=True)
                last.then_inc(pairs,1)
            turn_hots(0,0)
            pair_up(0)
            def look_up(g,slot,h,first):
                par=slot%2
                pe.wait_ge(cnt_copied,g*2+h+1)
                pe.wait_ge(turnedf,g+1)
                if not first: pe.wait_ge(placed,g*S-S+2*h+2)
                for s in (2*h,2*h+1):
                    nc.tensor.matmul(PP[:,s,:],oloTf[:,par,s,:],cnt[:,s,:],start=(s==2*h),stop=False,skip_group_check=True)
                pe.wait_ge(masked,g+1)
                for s in (2*h,2*h+1):
                    last=nc.tensor.matmul(PP[:,s,:],same[:,par,s,:],ohi[:,s,slot,:],start=False,stop=True,skip_group_check=True)
                last.then_inc(ranks,1)
                for s in (2*h,2*h+1):
                    last=nc.tensor.matmul(cntP[:,s,:],olo[:,s,slot,:],ohi[:,s,slot,:],start=False,stop=False,skip_group_check=True)
                last.then_inc(updated,1)
            def group(g,slot,first=False,nxt=True):
                if nxt: turn_hots(g+1,(slot+1)%SLOTS)
                look_up(g,slot,0,first)
                if nxt: pair_up(g+1)
                look_up(g,slot,1,first)
            for j in range(SLOTS): group(j,j,first=j==0)
            with pe.Fori(1,GROUPS//SLOTS-1) as u:
                for j in range(SLOTS): group(u*SLOTS+j,j)
            for j in range(SLOTS): group(GROUPS-SLOTS+j,j,nxt=j<3)

class Scatter:
    def __init__(self, nc, room, placed, rec, t0, t1, chunks=None):
        self.nc,self.placed,self.rec,self.t0,self.t1,self.chunks=nc,placed,rec,t0,t1,chunks
        self.ring=room.sb("ring",[P,2,SHALF,3],i32)
        self.ring_in=room.pair("ring_in")
        self.sent=Rows(room,"sent",SHALF)
        self.gate=room.sem("sgate")
    def load(self, pool, i, par):
        if self.chunks is not None: pool.wait_ge(self.chunks,i+(self.t0*2+1))
        pool.dma_start(self.ring[:,par,:,:],self.placed[:,bass.ds((i+self.t0*2)*SHALF,SHALF),:]).then_inc(self.ring_in[par],16)
    def send(self, pool, par, lo, hi):
        for k in range(lo,hi):
            pool.indirect_dma_start(self.rec,bass.IndirectOffsetOnAxis(ap=self.ring[:,par,k,2:3],axis=0),self.ring[:,par,k,0:2],None).then_inc(self.sent.of(k,par),16)
    def pool(self, pool):
        def half(t,par,first=False,last=False):
            pool.wait_ge(self.ring_in[par],t*16+16)
            pool.sem_inc(self.gate,1)
            self.send(pool,par,0,SHALF//2)
            if not last:
                if not first: self.sent.wait(pool,t+par,1-par)
                self.load(pool,t*2+(par+1),1-par)
            self.send(pool,par,SHALF//2,SHALF)
        n=self.t1-self.t0
        self.load(pool,0,0)
        half(0,0,first=True)
        with pool.Fori(0,n-1) as t:
            half(t,1)
            half(t+1,0)
        half(n-1,1,last=True)
        for par in range(2): self.sent.wait(pool,n,par)


RED=32
GK=72
PADW=W+2
def involution(nc, x, w1, b1, wd, w2, bd, b2, pick, ones, x_out, beside=None, tag="c"):
    with ExitStack() as ctx:
        ctx.enter_context(nc.cleanup_on_exit())
        r=Room(nc,ctx,tag)
        img=[r.sb(f"img{k}",[P,TOK]) for k in range(2)]
        xn=[r.sb(f"xn{k}",[P,PADW,PADW]) for k in range(2)]
        y=[r.sb(f"y{k}",[96,PADW,PADW]) for k in range(2)]
        mw=r.sb("mw",[P,P])
        w1s=r.sb("w1",[P,96])
        b1s=r.sb("b1",[96,1])
        wds=r.sb("wd",[96,3])
        w2s=r.sb("w2",[96,GK])
        bds=r.sb("bd",[RED,1])
        b2s=r.sb("b2",[GK,1])
        picks=r.sb("pick",[P,9,P])
        wk=r.sb("wk",[96,3,GK])
        bias=r.sb("bias",[GK,1])
        eps=r.sb("eps",[P,1])
        kern=r.sb("kern",[P,2,T])
        prod=r.sb("prod",[P,3,T])
        acc=r.sb("acc",[P,2,T])
        yP=r.pb("yP",[96,T])
        kP=r.pb("kP",[GK,T])
        eP=[r.pb(f"eP{k}",[P,T]) for k in range(3)]
        w_in=r.sem("w_in")
        w_ready=r.sem("w_ready")
        folded=r.sem("folded")
        img_in=r.pair("img_in")
        out=Stores(r,"out")
        squeezed,padded,kernels,biased,added=r.flags("squeezed padded kernels biased added")
        spreadk=r.sem("spread_k")
        times=r.sem("times")
        summed=r.sem("summed")
        image_used=r.sem("image_used")
        edges=r.sem("edges")
        block=ctx.enter_context(nc.Block())
        at={"j":0,"ip":0}
        nm=Norm(nc,r,"n",mw[:,:],eps[:,0:1],lambda i,par: img[at["ip"]][:,bass.ds(at["j"]*T,T)],lambda e,i,par: None,
                lambda i,par: xn[at["ip"]][:,bass.ds(at["j"]*ROWS+1,ROWS),1:W+1],lambda e,i,par: None)
        def images(eng, body):
            with eng.Fori(0,B//2) as t:
                for ip in range(2): body(t*2+ip, ip)
        @block.sync
        def _(sp):
            for d,s in ((mw[:,:],ones),(w1s[:,:],w1),(b1s[:,:],b1),(wds[:,:],wd),(w2s[:,:],w2),(bds[:,:],bd),(b2s[:,:],b2),(picks[:,:,:],pick)):
                sp.dma_start(d,s).then_inc(w_in,16)
            out.start(sp)
            def load(b,ip):
                sp.dma_start(img[ip][:,:],x[:,bass.ds(b*TOK,TOK)]).then_inc(img_in[ip],16)
            load(0,0)
            load(1,1)
            def stores(b,ip):
                def store(j,par):
                    i=b*TPI+j
                    sp.wait_ge(summed,i*9+9)
                    sp.dma_start(x_out[:,bass.ds(i*T,T)],acc[:,par,:]).then_inc(out.sems[par],16)
                    out.landed(sp,i,par)
                paired(sp,TPI,store)
            with sp.Fori(0,B//2-1) as t:
                for ip in range(2):
                    stores(t*2+ip,ip)
                    sp.wait_ge(image_used,t*2+ip+1)
                    load(t*2+ip+2,ip)
            for ip in range(2): stores(B-2+ip,ip)
        def tiles(eng,b,ip,ahead,body):
            def call(f,j,par):
                at.update(j=j,ip=ip)
                f(b*TPI+j,j,par,ip)
            if ahead is None:
                with eng.Fori(0,TPI//2) as jj:
                    call(body,jj*2,0)
                    call(body,jj*2+1,1)
                return
            call(ahead,0,0)
            with eng.Fori(0,TPI//2-1) as jj:
                call(ahead,jj*2+1,1)
                call(body,jj*2,0)
                call(ahead,jj*2+2,0)
                call(body,jj*2+1,1)
            call(ahead,TPI-1,1)
            call(body,TPI-2,0)
            call(body,TPI-1,1)
        @block.tensor
        def _(pe):
            nm.pe_start(pe)
            squeezed.start(pe)
            kernels.start(pe)
            pe.wait_ge(w_in,16*8)
            nc.tensor.matmul(kP[:,0:1],w2s[0:RED,:],bds[:,:],start=True,stop=True).then_inc(folded,1)
            pe.wait_ge(w_ready,1)
            pe.wait_ge(edges,1)
            def image(b,ip):
                pe.wait_ge(img_in[ip],(b-ip)*8+16)
                def var_and_squeeze(i,j,par,ip):
                    nm.pe_var(pe,i,par)
                    nm.normed.of(pe,i)
                    padded.before(pe,i,1)
                    nc.tensor.matmul(yP[:,:],w1s[:,:],xn[ip][:,bass.ds(j*ROWS+1,ROWS),1:W+1],start=True,stop=True).then_inc(squeezed.sem,1)
                tiles(pe,b,ip,lambda i,j,par,ip: nm.pe_mean(pe,i,par),var_and_squeeze)
                padded.of(pe,b*TPI+TPI-1)
                def kernel_of(i,j,par,ip):
                    biased.before(pe,i,1)
                    for kh in range(3):
                        last=nc.tensor.matmul(kP[:,:],wk[:,kh,:],y[ip][:,bass.ds(j*ROWS+kh,ROWS),1:W+1],start=(kh==0),stop=(kh==2))
                    last.then_inc(kernels.sem,1)
                def spread(i,j,par,ip):
                    biased.of(pe,i)
                    for k in range(9):
                        pe.wait_ge(times,i*9+k+1)
                        nc.tensor.matmul(eP[k%3][:,:],picks[:,k,:],kern[:,par,:],start=True,stop=True).then_inc(spreadk,1)
                tiles(pe,b,ip,kernel_of,spread)
            images(pe,image)
        @block.scalar
        def _(act):
            nc.scalar.preload_act_table_set("natural_log_exp_and_others")
            nm.act_start(act)
            padded.start(act)
            biased.start(act)
            act.wait_ge(w_ready,1)
            def image(b,ip):
                def root_and_pad(i,j,par,ip):
                    nm.act_root(act,i,par)
                    squeezed.of(act,i)
                    for kw in range(3):
                        q=slice(RED*kw,RED*kw+RED)
                        last=nc.scalar.activation(y[ip][q,bass.ds(j*ROWS+1,ROWS),2-kw:2-kw+W],yP[q,:].rearrange("p (a b) -> p a b",b=W),ACT.Identity,bias=b1s[q,0:1])
                    last.then_inc(padded.sem,1)
                tiles(act,b,ip,lambda i,j,par,ip: nm.act_square(act,i,par),root_and_pad)
                def add_bias(i,j,par,ip):
                    kernels.of(act,i)
                    added.before(act,i,2)
                    nc.scalar.activation(kern[0:GK,par,:],kP[:,:],ACT.Identity,bias=bias[:,0:1]).then_inc(biased.sem,1)
                tiles(act,b,ip,None,add_bias)
            images(act,image)
        @block.vector
        def _(dve):
            nm.dve_start(dve)
            added.start(dve)
            dve.sem_inc(times,3)
            nc.vector.memset(eps[:,:],1e-6)
            nc.vector.memset(kern[:,:,:],0.0)
            for k in range(2):
                nc.vector.memset(xn[k][:,:,:],0.0)
                last=nc.vector.memset(y[k][:,:,:],0.0)
            last.then_inc(edges,1)
            dve.wait_ge(w_in,16*8)
            for kh in range(3):
                nc.vector.tensor_scalar(wk[:,kh,:],w2s[:,:],wds[:,kh:kh+1],None,ALU.mult)
            dve.wait_ge(folded,1)
            nc.vector.tensor_tensor(bias[:,:],kP[:,0:1],b2s[:,:],ALU.add).then_inc(w_ready,1)
            def image(b,ip):
                dve.wait_ge(img_in[ip],(b-ip)*8+16)
                dve.wait_ge(edges,1)
                tiles(dve,b,ip,lambda i,j,par,ip: nm.dve_centre(dve,i,par),lambda i,j,par,ip: nm.dve_scale(dve,i,par))
                def weigh(i,j,par,ip):
                    out.done.before(dve,i,2)
                    def multiply(k):
                        kh,kw=k//3,k%3
                        dve.wait_ge(spreadk,i*9+k+1)
                        if k>=3: dve.wait_ge(summed,i*9+k-2)
                        nc.vector.tensor_tensor(prod[:,k%3,:].rearrange("p (a b) -> p a b",b=W),eP[k%3][:,:].rearrange("p (a b) -> p a b",b=W),xn[ip][:,bass.ds(j*ROWS+kh,ROWS),kw:kw+W],ALU.mult).then_inc(times,1)
                    def add(k):
                        before=img[ip][:,bass.ds(j*T,T)] if k==0 else acc[:,par,:]
                        dve.wait_ge(times,i*9+k+4)
                        if k: dve.wait_ge(summed,i*9+k)
                        nc.vector.tensor_tensor(acc[:,par,:],before,prod[:,k%3,:],ALU.add).then_inc(summed,1)
                    multiply(0)
                    for k in range(1,9):
                        multiply(k)
                        add(k-1)
                    add(8)
                    dve.wait_ge(summed,i*9+9)
                    nc.vector.sem_inc(added.sem,1)
                tiles(dve,b,ip,None,weigh)
                dve.sem_inc(image_used,1)
            images(dve,image)
        if beside:
            block.gpsimd(beside(r))


HW=24
def heads(nc, x, wg, att, ones, xn_out, table, tag="h"):
    with ExitStack() as ctx:
        ctx.enter_context(nc.cleanup_on_exit())
        r=Room(nc,ctx,tag)
        xt=r.sb("x",[P,2,T])
        xn=r.sb("xn",[P,2,T])
        mw=r.sb("mw",[P,P])
        w=r.sb("w",[P,HW])
        at=r.sb("att",[P,32])
        prod=r.sb("prod",[P,2,16])
        hp=[r.pb(f"hp{k}",[P,4,HW]) for k in range(2)]
        hs=r.sb("hs",[P,2,4,HW])
        eps=r.sb("eps",[P,1])
        w_in=r.sem("w_in")
        w_prod=r.sem("w_prod")
        w_ready=r.sem("w_ready")
        rows,copied=r.flags("rows copied")
        x_in=r.pair("x_in")
        xn_stores=Stores(r,"xn_out")
        t_stores=Stores(r,"t_out")
        def dest_free(dve,i,par):
            xn_stores.done.before(dve,i,2)
            rows.before(dve,i,2)
        nm=Norm(nc,r,"n",mw[:,:],eps[:,0:1],lambda i,par:xt[:,par,:],lambda e,i,par: landed(e,x_in,i,par),lambda i,par:xn[:,par,:],dest_free)
        block=ctx.enter_context(nc.Block())
        @block.sync
        def _(sp):
            sp.dma_start(mw[:,:],ones).then_inc(w_in,16)
            sp.dma_start(w[:,0:16],wg).then_inc(w_in,16)
            sp.dma_start(at[:,:],att.partition_broadcast(P)).then_inc(w_in,16)
            def load(i,par):
                nm.centred.before(sp,i,2)
                sp.dma_start(xt[:,par,:],x[:,bass.ds(i*T,T)]).then_inc(x_in[par],16)
            paired(sp,TILES,load)
        @block.tensor
        def _(pe):
            nm.pe_start(pe)
            rows.start(pe)
            pe.wait_ge(w_in,48)
            pe.wait_ge(w_ready,3)
            def body(i,par):
                nm.normed.of(pe,i)
                copied.before(pe,i,2)
                for q in range(4):
                    last=nc.tensor.matmul(hp[par][:,q,:],xn[:,par,q*P:(q+1)*P],w[:,:],start=True,stop=True,skip_group_check=True)
                last.then_inc(rows.sem,1)
            lagged(pe,TILES,[lambda i,par: nm.pe_mean(pe,i,par),lambda i,par: nm.pe_var(pe,i,par),body])
        @block.vector
        def _(dve):
            nm.dve_start(dve)
            nc.vector.memset(eps[:,:],1e-5).then_inc(w_ready,1)
            dve.wait_ge(w_in,48)
            for k in range(2):
                nc.vector.tensor_tensor(prod[:,k,:],w[:,0:16],at[:,16*k:16*k+16],ALU.mult).then_inc(w_prod,1)
            dve.wait_ge(w_prod,2)
            for k in range(2):
                nc.vector.tensor_reduce(w[:,16+4*k:20+4*k],prod[:,k,:].rearrange("p (h e) -> p h e",e=4),AX.X,ALU.add).then_inc(w_ready,1)
            lagged(dve,TILES,[lambda i,par: nm.dve_centre(dve,i,par),lambda i,par: nm.dve_scale(dve,i,par),lambda i,par: None])
        @block.scalar
        def _(act):
            nc.scalar.preload_act_table_set("natural_log_exp_and_others")
            nm.act_start(act)
            copied.start(act)
            act.wait_ge(w_ready,1)
            def body(i,par):
                rows.of(act,i)
                t_stores.done.before(act,i,2)
                nc.scalar.copy(hs[:,par,:,:],hp[par][:,:,:]).then_inc(copied.sem,1)
            lagged(act,TILES,[lambda i,par: nm.act_square(act,i,par),lambda i,par: nm.act_root(act,i,par),body])
        @block.gpsimd
        def _(pool):
            def body(i,par):
                nm.normed.of(pool,i)
                pool.dma_start(xn_out[:,bass.ds(i*T,T)],xn[:,par,:]).then_inc(xn_stores.sems[par],16)
                copied.of(pool,i)
                pool.dma_start(table[bass.ds(i*T,T),:].rearrange("(q p) f -> p q f",p=P),hs[:,par,:,:]).then_inc(t_stores.sems[par],16)
                xn_stores.landed(pool,i,par)
                t_stores.landed(pool,i,par)
            xn_stores.start(pool)
            t_stores.start(pool)
            paired(pool,TILES,body)


E=524288
COLS=E//P
HI=256
HW=24
GHALF=16
RING=16
HALF=8
C=128
NF=20
FAR=1e30
class Gather:
    def __init__(self, nc, room, rec, table, rows, zero_edges):
        self.nc,self.table,self.rows,self.zero_edges=nc,table,rows,zero_edges
        self.rec=rec.rearrange("(p c) f -> p c f",p=P)
        self.ring=room.sb("ring",[P,2,GHALF,2],i32)
        self.got=room.sb("got",[P,2,GHALF,HW])
        self.zero=room.sb("zero",[P,1024])
        self.ring_in,self.stored=room.pair("ring_in"),room.pair("stored")
        self.gathered=Rows(room,"gathered",GHALF)
        self.zeroed=room.sem("zeroed")
        self.zeros_out=room.sem("zeros_out")
        self.gate=room.sem("gather_gate")
    def load(self,sp,i,par):
        sp.dma_start(self.ring[:,par,:,:],self.rec[:,bass.ds(i*GHALF,GHALF),:]).then_inc(self.ring_in[par],16)
    def store(self,sp,t,par):
        i=t*2+par
        self.gathered.wait(sp,t+1,par)
        sp.dma_start(self.rows[:,bass.ds(i*GHALF,GHALF),:],self.got[:,par,:,:]).then_inc(self.stored[par],16)
    def sync(self,sp):
        self.load(sp,0,0)
        self.load(sp,1,1)
        sp.wait_ge(self.zeroed,1)
        edz=self.zero_edges.rearrange("(p n) f -> p (n f)",p=P)
        n=E*8//(P*1024)
        with sp.Fori(0,n) as i:
            sp.dma_start(edz[:,bass.ds(i*1024,1024)],self.zero[:,:]).then_inc(self.zeros_out,16)
        with sp.Fori(0,COLS//(2*GHALF)-1) as t:
            for par in range(2):
                self.store(sp,t,par)
                self.load(sp,t*2+par+2,par)
        for par in range(2): self.store(sp,COLS//(2*GHALF)-1,par)
        for par in range(2): sp.wait_ge(self.stored[par],8*COLS//GHALF)
        sp.wait_ge(self.zeros_out,16*n)
    def fetch(self,pool,i,par,first):
        pool.wait_ge(self.ring_in[par],(i-par)*8+16)
        pool.sem_inc(self.gate,1)
        if not first:
            pool.wait_ge(self.stored[par],(i-par)*8)
            pool.sem_inc(self.gate,1)
        for k in range(GHALF):
            pool.indirect_dma_start(self.got[:,par,k,:],None,self.table,bass.IndirectOffsetOnAxis(ap=self.ring[:,par,k,0:1],axis=0)).then_inc(self.gathered.of(k,par),16)
    def pool(self,pool):
        self.nc.gpsimd.memset(self.zero[:,:],0.0).then_inc(self.zeroed,1)
        self.fetch(pool,0,0,True)
        self.fetch(pool,1,1,True)
        with pool.Fori(1,COLS//(2*GHALF)) as t:
            for par in range(2): self.fetch(pool,t*2+par,par,False)

def edge_arrays(nc, tag):
    dram=lambda n,s: nc.dram_tensor(f"{tag}_{n}",s,f32).ap()
    return dict(rows=dram("rows",[P,COLS,HW]),mx=dram("mx",[E,4]),ed=dram("ed",[E+P,8]),ss=dram("ss",[E,NF]),nr=dram("nr",[NODES,8]))
def gather_of(nc, room, rec, table, d): return Gather(nc,room,rec,table,d["rows"],d["ed"][0:E,:])
def gather_alone(nc, rec, table, d, tag="ga"):
    with ExitStack() as ctx:
        ctx.enter_context(nc.cleanup_on_exit())
        g=gather_of(nc,Room(nc,ctx,tag),rec,table,d)
        block=ctx.enter_context(nc.Block())
        block.sync(g.sync)
        block.gpsimd(g.pool)

def attention(nc, rec, start, deg, table, bgat, gamma, beta, eye, gates, d, tag="g"):
    rows_d,mx_d,ed_d,ss_d,nr_d=[d[k] for k in ("rows","mx","ed","ss","nr")]
    with ExitStack() as ctx0:
        ctx0.enter_context(nc.cleanup_on_exit())
        r0=Room(nc,ctx0,tag)
        cont=r0.sb("cont",[P,COLS])
        meta=r0.sb("meta",[P,3,NF])
        ident=r0.sb("eye",[P,P])
        rowsP=r0.pb("rowsP",[NF,4,P])
        colP=r0.pb("colP",[P,NF])
        brought=r0.sb("brought",[P,NF])
        joins=r0.sb("joins",[NF,3,P])
        first=r0.sb("first",[P,1],u32)
        with ExitStack() as ctx:
            ctx.enter_context(nc.cleanup_on_exit())
            r=Room(nc,ctx,tag+"1")
            recs=r.sb("recs",[P,COLS,2],i32)
            brk=r.sb("brk",[P,COLS])
            asrc=r.sb("asrc",[P,COLS,4])
            zero=r.sb("zero",[P,1])
            got=r.sb("got",[P,2,C,HW])
            last=r.sb("last",[P,4])
            lrow=r.sb("lrow",[4,5,P])
            carry=r.sb("carry",[P,4])
            rec_in=r.sem("rec_in")
            a_copied=r.sem("a_copied")
            rows_in=r.pair("rows_in")
            step=r.sem("step")
            pe_done=r.sem("pe_done")
            mx_out=r.sem("mx_out")
            scanned=r.sem("scanned")
            meta_ready=r.sem("meta_ready")
            N=COLS//C
            block=ctx.enter_context(nc.Block())
            @block.sync
            def _(sp):
                sp.dma_start(recs[:,:,:],rec.rearrange("(p c) f -> p c f",p=P)).then_inc(rec_in,16)
                sp.dma_start(ident[:,:],eye).then_inc(rec_in,16)
                def load(i,par):
                    sp.wait_ge(a_copied,i+1)
                    sp.dma_start(got[:,par,:,:],rows_d[:,bass.ds(i*C,C),:]).then_inc(rows_in[par],16)
                paired(sp,N,load)
                sp.wait_ge(scanned,1)
                sp.dma_start(mx_d.rearrange("(p c) f -> p c f",p=P),asrc[:,:,:]).then_inc(mx_out,16)
                sp.wait_ge(mx_out,16)
            @block.scalar
            def _(act):
                act.sem_inc(a_copied,2)
                def keep(i,par):
                    landed(act,rows_in,i,par)
                    nc.scalar.copy(asrc[:,bass.ds(i*C,C),:],got[:,par,:,16:20]).then_inc(a_copied,1)
                paired(act,N,keep)
            @block.vector
            def _(dve):
                n=[0]
                def do(ins):
                    n[0]+=1
                    ins.then_inc(step,1)
                    dve.wait_ge(step,n[0])
                dve.wait_ge(rec_in,32)
                nc.vector.memset(cont[:,0:1],1.0)
                do(nc.vector.tensor_tensor(cont[:,1:COLS],recs[:,1:COLS,1],recs[:,0:COLS-1,1],ALU.is_equal))
                do(nc.vector.tensor_scalar(brk[:,:],cont[:,:],-1.0,FAR,ALU.add,ALU.mult))
                nc.vector.tensor_copy(meta[:,0,:],recs[:,0:1,1].broadcast_to([P,NF]))
                nc.vector.tensor_copy(first[:,:],recs[:,0:1,1])
                nc.vector.tensor_copy(meta[:,1,:],recs[:,COLS-1:COLS,1].broadcast_to([P,NF]))
                do(nc.vector.tensor_reduce(last[:,0:1],cont[:,1:COLS],AX.X,ALU.min))
                do(nc.vector.tensor_copy(meta[:,2,:],last[:,0:1].broadcast_to([P,NF])))
                dve.wait_ge(a_copied,N+2)
                for h in range(4):
                    nc.vector.tensor_tensor_scan(asrc[:,:,h],brk[:,:],asrc[:,:,h],-FAR,ALU.add,ALU.max)
                do(nc.vector.memset(zero[:,0:1],0.0))
                nc.vector.tensor_copy(last[:,:],asrc[:,COLS-1,:]).then_inc(meta_ready,1)
                dve.wait_ge(pe_done,1)
                nc.vector.memset(joins[:,:,:],0.0).then_inc(meta_ready,1)
                dve.wait_ge(meta_ready,2)
                do(nc.vector.tensor_copy(joins[:,2,:],rowsP[:,1,:]))
                do(nc.vector.tensor_tensor(joins[:,0,1:P],rowsP[:,0,1:P],joins[:,2,0:P-1],ALU.is_equal))
                do(nc.vector.tensor_tensor(joins[:,1,1:P],joins[:,0,1:P],rowsP[:,2,0:P-1],ALU.mult))
                do(nc.vector.tensor_scalar(lrow[:,0,:],joins[0:4,1,:],-1.0,FAR,ALU.add,ALU.mult))
                do(nc.vector.tensor_scalar(lrow[:,1,:],joins[0:4,0,:],-1.0,FAR,ALU.add,ALU.mult))
                do(nc.vector.tensor_tensor(lrow[:,2,1:P],rowsP[0:4,3,0:P-1],joins[0:4,0,1:P],ALU.mult))
                do(nc.vector.tensor_tensor(lrow[:,1,1:P],lrow[:,1,1:P],lrow[:,2,1:P],ALU.add))
                do(nc.vector.tensor_tensor_scan(lrow[:,4,:],lrow[:,0,:],lrow[:,1,:],-FAR,ALU.add,ALU.max))
                nc.vector.sem_inc(meta_ready,1)
                dve.wait_ge(pe_done,2)
                do(nc.vector.tensor_copy(carry[:,:],colP[:,0:4]))
                for h in range(4):
                    nc.vector.tensor_tensor_scan(asrc[:,:,h],brk[:,:],asrc[:,:,h],carry[:,h:h+1],ALU.add,ALU.max)
                do(nc.vector.memset(zero[:,0:1],0.0))
                do(nc.vector.memset(cont[:,0:1],0.0))
                dve.sem_inc(scanned,1)
            @block.tensor
            def _(pe):
                pe.wait_ge(rec_in,32)
                pe.wait_ge(meta_ready,1)
                for k in range(3):
                    nc.tensor.matmul(rowsP[:,k,:],meta[:,k,:],ident[:,:],start=True,stop=True,skip_group_check=True)
                nc.tensor.matmul(rowsP[0:4,3,:],last[:,:],ident[:,:],start=True,stop=True,skip_group_check=True).then_inc(pe_done,1)
                pe.wait_ge(meta_ready,3)
                nc.tensor.matmul(colP[:,0:4],lrow[:,4,:],ident[0:4,0:4],start=True,stop=True).then_inc(pe_done,1)
        nodes=r0.sb("nodes",[P,HI,HW])
        endr=r0.sb("endr",[P,HI],u32)
        stf=r0.sb("stf",[P,HI])
        has=r0.sb("has",[P,HI])
        nrow=r0.sb("nrow",[P,HI,8])
        rowfirst=r0.sb("rowfirst",[P,8])
        bc=lambda a,w: a.unsqueeze(2).broadcast_to([P,HI,w])
        def fetch_by_node(tg, prepare, jobs, finish):
            with ExitStack() as ctx:
                ctx.enter_context(nc.cleanup_on_exit())
                r=Room(nc,ctx,tag+tg)
                idx=r.sb("idx",[P,RING],u32)
                got=[r.sb(f"got{n}",[P,RING,j[3]]) for n,j in enumerate(jobs)]
                ready=r.sem("ready")
                gate=r.sem("gate")
                copied=r.sem("copied")
                sg=r.pair("sg")
                N=HI//HALF
                prep=prepare(r)
                block=ctx.enter_context(nc.Block())
                if "sync" in prep: block.sync(prep["sync"])
                if "tensor" in prep: block.tensor(prep["tensor"])
                @block.gpsimd
                def _(pool):
                    if "pool" in prep: prep["pool"](pool)
                    for n,(ix,tb,o,w) in enumerate(jobs):
                        def fetch(i,par):
                            pool.wait_ge(ready,i+1+n*N)
                            pool.sem_inc(gate,1)
                            pool.wait_ge(copied,i+1+n*N)
                            pool.sem_inc(gate,1)
                            for k in range(par*HALF,par*HALF+HALF):
                                pool.indirect_dma_start(got[n][:,k,:],None,tb,bass.IndirectOffsetOnAxis(ap=idx[:,k:k+1],axis=0)).then_inc(sg[par],16)
                        paired(pool,N,fetch)
                    if "pool_after" in prep: prep["pool_after"](pool)
                @block.vector
                def _(dve):
                    prep["vector"](dve)
                    for n,(ix,tb,o,w) in enumerate(jobs):
                        def index(i,par):
                            if not (isinstance(i,int) and n==0):
                                dve.wait_ge(sg[par],(i-par)*8*HALF+n*N*8*HALF)
                            nc.vector.tensor_copy(idx[:,par*HALF:par*HALF+HALF],ix[:,bass.ds(i*HALF,HALF)]).then_inc(ready,1)
                        paired(dve,N,index,peel=True)
                    dve.wait_ge(copied,2+N*len(jobs))
                    finish(dve,r,prep)
                @block.scalar
                def _(act):
                    act.sem_inc(copied,2)
                    for n,(ix,tb,o,w) in enumerate(jobs):
                        def keep(i,par):
                            act.wait_ge(sg[par],((i-par)*8+16+n*N*8)*HALF)
                            nc.scalar.copy(o[:,bass.ds(i*HALF,HALF),:],got[n][:,par*HALF:par*HALF+HALF,:]).then_inc(copied,1)
                        paired(act,N,keep)
                    if "scalar" in prep: prep["scalar"](act)
        def steps(dve,sem,n):
            def do(ins):
                n[0]+=1
                ins.then_inc(sem,1)
                dve.wait_ge(sem,n[0])
            return do
        with ExitStack() as ctxm:
            ctxm.enter_context(nc.cleanup_on_exit())
            rm=Room(nc,ctxm,tag+"m")
            top=rm.sb("top",[P,HI,4])
            degf=rm.sb("degf",[P,HI])
            sidx=rm.sb("sidx",[P,HI],u32)
            pid=rm.sb("pid",[P,1],i32)
            pidf=rm.sb("pidf",[P,1])
            tmp=rm.sb("tmp",[P,HI])
            n=[0]
            def prepare(r):
                n_in=r.sem("n_in")
                iot=r.sem("iot")
                step=r.sem("step")
                nrow_ready=r.sem("nrow_ready")
                nr_out=r.sem("nr_out")
                ring=r.sem("ring")
                rr=r.sb("rr",[P,RING,8])
                ri=r.sb("ri",[P,RING],u32)
                sc=r.pair("sc")
                g2=r.sem("g2")
                f1=r.sem("f1")
                def sync(sp):
                    sp.dma_start(nodes[:,:,:],table.rearrange("(p n) f -> p n f",p=P)).then_inc(n_in,16)
                    sp.dma_start(stf[:,:],start).then_inc(n_in,16)
                    sp.dma_start(degf[:,:],deg).then_inc(n_in,16)
                    sp.wait_ge(nrow_ready,1)
                    sp.dma_start(nr_d.rearrange("(p n) f -> p n f",p=P),nrow[:,:,:]).then_inc(nr_out,16)
                def pool(p):
                    p.iota(pid[:,:],pattern=[[0,1]],base=E,channel_multiplier=1).then_inc(iot,1)
                def vector(dve):
                    do=steps(dve,step,n)
                    dve.wait_ge(n_in,48)
                    dve.wait_ge(iot,1)
                    do(nc.vector.tensor_copy(pidf[:,:],pid[:,:]))
                    do(nc.vector.tensor_scalar(has[:,:],degf[:,:],0.0,None,ALU.is_gt))
                    do(nc.vector.scalar_tensor_tensor(tmp[:,:],stf[:,:],-1.0,degf[:,:],ALU.add,ALU.add))
                    do(nc.vector.tensor_scalar(endr[:,:],tmp[:,:],0.0,None,ALU.max))
                    do(nc.vector.tensor_scalar(tmp[:,:],has[:,:],-1.0,-1.0,ALU.mult,ALU.subtract))
                    do(nc.vector.tensor_scalar(tmp[:,:],tmp[:,:],pidf[:,0:1],None,ALU.mult))
                    do(nc.vector.tensor_tensor(degf[:,:],stf[:,:],has[:,:],ALU.mult))
                    do(nc.vector.tensor_tensor(sidx[:,:],tmp[:,:],degf[:,:],ALU.add))
                def pool_after(p):
                    def send(i,par):
                        p.wait_ge(ring,i+1)
                        p.sem_inc(g2,1)
                        for k in range(par*HALF,par*HALF+HALF):
                            p.indirect_dma_start(ed_d,bass.IndirectOffsetOnAxis(ap=ri[:,k:k+1],axis=0),rr[:,k,:],None).then_inc(sc[par],16)
                    paired(p,HI//HALF,send)
                    p.wait_ge(nr_out,16)
                    p.sem_inc(g2,1)
                    p.indirect_dma_start(rowfirst[:,:],None,nr_d,bass.IndirectOffsetOnAxis(ap=first[:,:],axis=0)).then_inc(f1,16)
                    for k in range(2): p.wait_ge(sc[k],8*HI)
                    p.wait_ge(f1,16)
                return dict(sync=sync,pool=pool,vector=vector,pool_after=pool_after,step=step,nrow_ready=nrow_ready,ring=ring,rr=rr,ri=ri,sc=sc)
            def finish(dve,r,prep):
                do=steps(dve,prep["step"],n)
                do(nc.vector.tensor_tensor(top[:,:,:],top[:,:,:],bc(has[:,:],4),ALU.mult))
                do(nc.vector.tensor_scalar(tmp[:,:],has[:,:],-1.0,FAR,ALU.add,ALU.mult))
                do(nc.vector.tensor_tensor(top[:,:,:],top[:,:,:],bc(tmp[:,:],4),ALU.add))
                do(nc.vector.tensor_tensor(top[:,:,:],top[:,:,:],nodes[:,:,16:20],ALU.max))
                do(nc.vector.tensor_tensor(top[:,:,:],top[:,:,:],nodes[:,:,20:24],ALU.add))
                do(nc.vector.tensor_copy(nrow[:,:,0:4],nodes[:,:,20:24]))
                do(nc.vector.scalar_tensor_tensor(nrow[:,:,4:8],top[:,:,:],0.2,top[:,:,:],ALU.mult,ALU.max))
                dve.sem_inc(prep["nrow_ready"],1)
                def fill(i,par):
                    if not isinstance(i,int): dve.wait_ge(prep["sc"][par],(i-par)*8*HALF)
                    nc.vector.tensor_copy(prep["ri"][:,par*HALF:par*HALF+HALF],sidx[:,bass.ds(i*HALF,HALF)])
                    nc.vector.tensor_copy(prep["rr"][:,par*HALF:par*HALF+HALF,:],nrow[:,bass.ds(i*HALF,HALF),:]).then_inc(prep["ring"],1)
                paired(dve,HI//HALF,fill,peel=True)
            fetch_by_node("2",prepare,[(endr,mx_d,top,4)],finish)
        with ExitStack() as ctx:
            ctx.enter_context(nc.cleanup_on_exit())
            r=Room(nc,ctx,tag+"3")
            gs=r.sb("gs",[P,2,C,HW])
            ed=r.sb("ed",[P,2,C,8])
            pr=r.sb("pr",[P,2,C,8])
            z=r.sb("z",[P,2,C,4])
            wt=r.sb("wt",[P,2,C,4])
            wh=r.sb("wh",[P,2,C,NF])
            zc=r.sb("zc",[P,8])
            lrow=r.sb("lrow",[NF,4,P])
            last=r.sb("last",[P,NF])
            g_in=r.pair("g_in")
            e_in=r.pair("e_in")
            out=Stores(r,"out")
            zs=r.sem("zs")
            step=r.sem("step")
            done=r.sem("done")
            pe_done=r.sem("pe_done")
            shaped,shifted,weighed,spread,summed,known=r.flags("shaped shifted weighed spread summed known")
            N=COLS//C
            edr=ed_d[0:E,:].rearrange("(p c) f -> p c f",p=P)
            ssr=ss_d.rearrange("(p c) f -> p c f",p=P)
            block=ctx.enter_context(nc.Block())
            @block.sync
            def _(sp):
                def load(i,par):
                    spread.before(sp,i,2)
                    sp.dma_start(gs[:,par,:,:],rows_d[:,bass.ds(i*C,C),:]).then_inc(g_in[par],16)
                    sp.dma_start(ed[:,par,:,:],edr[:,bass.ds(i*C,C),:]).then_inc(e_in[par],16)
                paired(sp,N,load)
            @block.vector
            def _(dve):
                for f in (shaped,shifted,spread,summed,known): f.start(dve)
                nc.vector.memset(zc[:,:],0.0).then_inc(zs,1)
                dve.wait_ge(zs,1)
                def tile(i,par,begin=False):
                    landed(dve,e_in,i,par)
                    if begin:
                        nc.vector.tensor_copy(ed[:,0,0,:],rowfirst[:,:]).then_inc(zs,1)
                        dve.wait_ge(zs,2)
                    else: known.of(dve,i-1)
                    for f in range(8):
                        ins=nc.vector.tensor_tensor_scan(pr[:,par,:,f],cont[:,bass.ds(i*C,C)],ed[:,par,:,f],0.0 if begin else pr[:,1-par,C-1,f:f+1],ALU.mult,ALU.add)
                    ins.then_inc(known.sem,1)
                    known.of(dve,i)
                    landed(dve,g_in,i,par)
                    nc.vector.tensor_tensor(z[:,par,:,:],gs[:,par,:,16:20],pr[:,par,:,0:4],ALU.add).then_inc(shaped.sem,1)
                    shaped.of(dve,i)
                    nc.vector.scalar_tensor_tensor(z[:,par,:,:],z[:,par,:,:],0.2,z[:,par,:,:],ALU.mult,ALU.max).then_inc(zs,1)
                    dve.wait_ge(zs,i+3)
                    nc.vector.tensor_tensor(z[:,par,:,:],z[:,par,:,:],pr[:,par,:,4:8],ALU.subtract).then_inc(shifted.sem,1)
                def sums(i,par,begin=False):
                    weighed.of(dve,i)
                    out.done.before(dve,i,2)
                    if not begin: summed.of(dve,i-1)
                    nc.vector.tensor_copy(wh[:,par,:,16:20],wt[:,par,:,:])
                    nc.vector.tensor_tensor(wh[:,par,:,0:16].rearrange("p c (h e) -> p c h e",e=4),gs[:,par,:,0:16].rearrange("p c (h e) -> p c h e",e=4),wt[:,par,:,:].unsqueeze(3).broadcast_to([P,C,4,4]),ALU.mult).then_inc(spread.sem,1)
                    spread.of(dve,i)
                    for f in range(NF):
                        ins=nc.vector.tensor_tensor_scan(wh[:,par,:,f],cont[:,bass.ds(i*C,C)],wh[:,par,:,f],0.0 if begin else wh[:,1-par,C-1,f:f+1],ALU.mult,ALU.add)
                    ins.then_inc(summed.sem,1)
                tile(0,0,True)
                tile(1,1)
                sums(0,0,True)
                with dve.Fori(1,N//2) as t:
                    tile(t*2,0)
                    sums(t*2-1,1)
                    tile(t*2+1,1)
                    sums(t*2,0)
                sums(N-1,1)
                summed.of(dve,N-1)
                nc.vector.tensor_copy(last[:,:],wh[:,1,C-1,:]).then_inc(done,1)
                dve.wait_ge(pe_done,1)
                nc.vector.memset(lrow[:,:,:],0.0).then_inc(step,1)
                dve.wait_ge(step,1)
                nc.vector.tensor_tensor(lrow[:,0,1:P],rowsP[:,3,0:P-1],joins[:,0,1:P],ALU.mult).then_inc(step,1)
                dve.wait_ge(step,2)
                nc.vector.tensor_scalar(lrow[:,2,0:P-1],joins[:,1,1:P],-1.0,-1.0,ALU.mult,ALU.subtract)
                nc.vector.tensor_tensor_scan(lrow[:,1,:],joins[:,1,:],lrow[:,0,:],0.0,ALU.mult,ALU.add).then_inc(step,1)
                dve.wait_ge(step,3)
                nc.vector.tensor_copy(lrow[:,3,P-1:P],lrow[:,1,P-1:P])
                nc.vector.tensor_tensor(lrow[:,3,0:P-1],lrow[:,1,0:P-1],lrow[:,2,0:P-1],ALU.mult).then_inc(done,1)
                dve.wait_ge(pe_done,2)
                nc.vector.tensor_copy(brought[:,:],colP[:,:])
            @block.scalar
            def _(act):
                weighed.start(act)
                def weigh(i,par):
                    shifted.of(act,i)
                    spread.before(act,i,2)
                    nc.scalar.activation(wt[:,par,:,:],z[:,par,:,:],ACT.Exp).then_inc(weighed.sem,1)
                paired(act,N,weigh)
            @block.gpsimd
            def _(pool):
                def store(i,par):
                    summed.of(pool,i)
                    pool.dma_start(ssr[:,bass.ds(i*C,C),:],wh[:,par,:,:]).then_inc(out.sems[par],16)
                    out.landed(pool,i,par)
                out.start(pool)
                paired(pool,N,store)
            @block.tensor
            def _(pe):
                pe.wait_ge(done,1)
                nc.tensor.matmul(rowsP[:,3,:],last[:,:],ident[:,:],start=True,stop=True).then_inc(pe_done,1)
                pe.wait_ge(done,2)
                nc.tensor.matmul(colP[:,:],lrow[:,3,:],ident[0:NF,0:NF],start=True,stop=True).then_inc(pe_done,1)
        with ExitStack() as ctx:
            ctx.enter_context(nc.cleanup_on_exit())
            r5=Room(nc,ctx,tag+"5")
            tot=r5.sb("tot",[P,HI,NF])
            node_i=r5.sb("node_i",[P,3],i32)
            node=r5.sb("node",[P,2])
            count_i=r5.sb("count_i",[P,HI],i32)
            count=r5.sb("count",[P,HI])
            to_row=r5.sb("to_row",[P,P])
            to_col=r5.sb("to_col",[P,HI])
            spreadc=r5.sb("spreadc",[P,NF,HI])
            movedP=[r5.pb(f"movedP{k}",[P,2,HI]) for k in range(2)]
            par3=r5.sb("par",[P,3,16])
            w4=r5.sb("w4",[P,HI,4])
            big=r5.sb("big",[P,HI,16])
            one=r5.sb("one",[P,HI])
            eps=r5.sb("eps",[P,1])
            sc=r5.sb("sc",[P,4,HI])
            ex=r5.sb("ex",[P,4,HI])
            cmp=r5.sb("cmp",[P,HI])
            rank=r5.sb("rank",[P,4,HI])
            g=r5.sb("g",[P,4,HI])
            n=[0]
            def prepare(r):
                p_in=r.sem("p_in")
                step=r.sem("step")
                a_go=r.sem("a_go")
                a_done=r.sem("a_done")
                g_ready=r.sem("g_ready")
                g_out=r.sem("g_out")
                counting=r.sem("counting")
                c_ready=r.sem("c_ready")
                moved=r.sem("moved")
                m_used=r.sem("m_used")
                def sync(sp):
                    for k,a in enumerate((bgat,gamma,beta)):
                        sp.dma_start(par3[:,k,:],a.partition_broadcast(P)).then_inc(p_in,16)
                    sp.wait_ge(g_ready,1)
                    for e in range(4):
                        sp.dma_start(gates[e,:].rearrange("(p n) -> p n",p=P),g[:,e,:]).then_inc(g_out,16)
                    sp.wait_ge(g_out,64)
                def vector(dve):
                    do=steps(dve,step,n)
                    dve.wait_ge(counting,1)
                    do(nc.vector.tensor_copy(count[:,:],count_i[:,:]))
                    do(nc.vector.tensor_copy(node_i[:,0:1],meta[:,0,0:1]))
                    do(nc.vector.tensor_single_scalar(node_i[:,1:2],node_i[:,0:1],8,ALU.logical_shift_right))
                    do(nc.vector.tensor_single_scalar(node_i[:,2:3],node_i[:,0:1],HI-1,ALU.bitwise_and))
                    do(nc.vector.tensor_copy(node[:,:],node_i[:,1:3]))
                    do(nc.vector.tensor_scalar(to_row[:,:],count[:,0:P],node[:,0:1],None,ALU.is_equal))
                    do(nc.vector.tensor_scalar(to_col[:,:],count[:,:],node[:,1:2],None,ALU.is_equal))
                    for f in range(NF):
                        last=nc.vector.tensor_scalar(spreadc[:,f,:],to_col[:,:],brought[:,f:f+1],None,ALU.mult)
                    last.then_inc(c_ready,1)
                def pool(p):
                    p.iota(count_i[:,:],pattern=[[1,HI]],base=0,channel_multiplier=0).then_inc(counting,1)
                def tensor(pe):
                    pe.wait_ge(c_ready,1)
                    for k in range(NF//2):
                        if k>=2: pe.wait_ge(m_used,k-1)
                        nc.tensor.matmul(movedP[k%2][:,:,:],to_row[:,:],spreadc[:,2*k:2*k+2,:],start=True,stop=True).then_inc(moved,1)
                def scalar(act):
                    for k,(o,i,f,kw) in enumerate(((w4[:,:,:],w4[:,:,:],ACT.Exp,{}),(one[:,:],one[:,:],ACT.Ln,dict(bias=eps[:,0:1])),(one[:,:],one[:,:],ACT.Exp,dict(scale=-0.5)),(ex[:,:,:],ex[:,:,:],ACT.Exp,{}))):
                        act.wait_ge(a_go,k+1)
                        nc.scalar.activation(o,i,f,**kw).then_inc(a_done,1)
                return dict(sync=sync,vector=vector,scalar=scalar,pool=pool,tensor=tensor,moved=moved,m_used=m_used,step=step,a_go=a_go,a_done=a_done,g_ready=g_ready,p_in=p_in)
            def finish(dve,r,prep):
                do=steps(dve,prep["step"],n)
                acts=[0]
                def act_turn():
                    acts[0]+=1
                    dve.sem_inc(prep["a_go"],1)
                    dve.wait_ge(prep["a_done"],acts[0])
                V=nc.vector
                dve.wait_ge(prep["p_in"],48)
                do(V.memset(eps[:,:],1e-5))
                do(V.tensor_tensor(tot[:,:,:],tot[:,:,:],bc(has[:,:],NF),ALU.mult))
                for k in range(NF//2):
                    dve.wait_ge(prep["moved"],k+1)
                    V.tensor_tensor(tot[:,:,2*k:2*k+2],tot[:,:,2*k:2*k+2],movedP[k%2][:,:,:].rearrange("p f n -> p n f"),ALU.add).then_inc(prep["m_used"],1)
                dve.wait_ge(prep["m_used"],NF//2)
                do(V.tensor_tensor(w4[:,:,:],nodes[:,:,16:20],nodes[:,:,20:24],ALU.add))
                do(V.scalar_tensor_tensor(w4[:,:,:],w4[:,:,:],0.2,w4[:,:,:],ALU.mult,ALU.max))
                do(V.tensor_tensor(w4[:,:,:],w4[:,:,:],nrow[:,:,4:8],ALU.subtract))
                act_turn()
                h4=lambda a: a.rearrange("p n (h e) -> p n h e",e=4)
                b4=lambda a: a.unsqueeze(3).broadcast_to([P,HI,4,4])
                do(V.tensor_tensor(tot[:,:,16:20],tot[:,:,16:20],w4[:,:,:],ALU.add))
                do(V.tensor_tensor(h4(big[:,:,:]),h4(nodes[:,:,0:16]),b4(w4[:,:,:]),ALU.mult))
                do(V.tensor_tensor(big[:,:,:],big[:,:,:],tot[:,:,0:16],ALU.add))
                do(V.tensor_scalar(w4[:,:,:],tot[:,:,16:20],1e-16,None,ALU.add))
                do(V.reciprocal(w4[:,:,:],w4[:,:,:]))
                do(V.tensor_tensor(h4(big[:,:,:]),h4(big[:,:,:]),b4(w4[:,:,:]),ALU.mult))
                par=lambda k: par3[:,k,:].unsqueeze(1).broadcast_to([P,HI,16])
                do(V.tensor_tensor(big[:,:,:],big[:,:,:],par(0),ALU.add))
                do(V.tensor_reduce(one[:,:],big[:,:,:],AX.X,ALU.add))
                do(V.tensor_scalar(one[:,:],one[:,:],1/16,None,ALU.mult))
                do(V.tensor_tensor(big[:,:,:],big[:,:,:],bc(one[:,:],16),ALU.subtract))
                do(V.tensor_tensor(tot[:,:,0:16],big[:,:,:],big[:,:,:],ALU.mult))
                do(V.tensor_reduce(one[:,:],tot[:,:,0:16],AX.X,ALU.add))
                do(V.tensor_scalar(one[:,:],one[:,:],1/16,None,ALU.mult))
                act_turn()
                act_turn()
                do(V.tensor_tensor(big[:,:,:],big[:,:,:],bc(one[:,:],16),ALU.mult))
                do(V.tensor_tensor(big[:,:,:],big[:,:,:],par(1),ALU.mult))
                do(V.tensor_tensor(big[:,:,:],big[:,:,:],par(2),ALU.add))
                do(V.tensor_reduce(sc[:,:,:],big[:,:,:].rearrange("p n (h e) -> p e n h",e=4),AX.X,ALU.add))
                do(V.tensor_scalar(sc[:,:,:],sc[:,:,:],0.25,None,ALU.mult))
                for e in range(4):
                    first_=True
                    for j in range(4):
                        if j==e: continue
                        op=ALU.is_ge if j<e else ALU.is_gt
                        if first_:
                            do(V.tensor_tensor(rank[:,e,:],sc[:,j,:],sc[:,e,:],op))
                            first_=False
                        else:
                            do(V.tensor_tensor(cmp[:,:],sc[:,j,:],sc[:,e,:],op))
                            do(V.tensor_tensor(rank[:,e,:],rank[:,e,:],cmp[:,:],ALU.add))
                do(V.tensor_scalar(rank[:,:,:],rank[:,:,:],2.0,None,ALU.is_lt))
                do(V.tensor_tensor(cmp[:,:],sc[:,0,:],sc[:,1,:],ALU.max))
                do(V.tensor_tensor(cmp[:,:],cmp[:,:],sc[:,2,:],ALU.max))
                do(V.tensor_tensor(cmp[:,:],cmp[:,:],sc[:,3,:],ALU.max))
                do(V.tensor_tensor(ex[:,:,:],sc[:,:,:],cmp[:,:].unsqueeze(1).broadcast_to([P,4,HI]),ALU.subtract))
                act_turn()
                do(V.tensor_tensor(ex[:,:,:],ex[:,:,:],rank[:,:,:],ALU.mult))
                do(V.tensor_reduce(cmp[:,:],ex[:,:,:].rearrange("p e n -> p n e"),AX.X,ALU.add))
                do(V.reciprocal(cmp[:,:],cmp[:,:]))
                do(V.tensor_tensor(g[:,:,:],ex[:,:,:],cmp[:,:].unsqueeze(1).broadcast_to([P,4,HI]),ALU.mult))
                dve.sem_inc(prep["g_ready"],1)
            fetch_by_node("4",prepare,[(endr,ss_d,tot,NF)],finish)


EX=4
FF=256
def experts(nc, x, xn, gates, w1, b1, w2, b2, x_out, tag="f"):
    with ExitStack() as ctx:
        ctx.enter_context(nc.cleanup_on_exit())
        r=Room(nc,ctx,tag)
        xt=r.sb("x",[P,2,T])
        xs=r.sb("xn",[P,2,T])
        gt=r.sb("gate",[P,2,EX,T])
        w1s=r.sb("w1",[P,EX,FF])
        b1s=r.sb("b1",[P,EX,2])
        w2s=r.sb("w2",[P,EX,2,P])
        b2s=r.sb("b2",[P,EX])
        hid=r.sb("hid",[P,2,2,T])
        part=r.sb("part",[P,2,T])
        acc=r.sb("acc",[P,2,T])
        hP=[r.pb(f"hP{k}",[P,2,T]) for k in range(2)]
        oP=[r.pb(f"oP{k}",[P,T]) for k in range(2)]
        w_in=r.sem("w_in")
        x_in=r.pair("x_in")
        n_in=r.pair("n_in")
        g_in=r.pair("g_in")
        out=Stores(r,"out")
        up,active,down,gated,summed=r.flags("up active down gated summed")
        block=ctx.enter_context(nc.Block())
        def tiles(eng, tile):
            with eng.Fori(0,TILES//2-1) as t:
                tile(t*2,0,True)
                tile(t*2+1,1,True)
            tile(TILES-2,0,True)
            tile(TILES-1,1,False)
        @block.sync
        def _(sp):
            for d,s in ((w1s[:,:,:],w1),(b1s[:,:,:],b1),(w2s[:,:,:,:],w2),(b2s[:,:],b2)):
                sp.dma_start(d,s).then_inc(w_in,16)
            def load(i,par):
                up.before(sp,i*EX+EX-1,2*EX) if not isinstance(i,int) else None
                summed.before(sp,i*EX+EX-1,2*EX) if not isinstance(i,int) else None
                sp.dma_start(xs[:,par,:],xn[:,bass.ds(i*T,T)]).then_inc(n_in[par],16)
                sp.dma_start(gt[:,par,:,:],gates[:,bass.ds(i*T,T)].partition_broadcast(P)).then_inc(g_in[par],16)
                sp.dma_start(xt[:,par,:],x[:,bass.ds(i*T,T)]).then_inc(x_in[par],16)
            load(0,0)
            load(1,1)
            with sp.Fori(1,TILES//2) as t:
                load(t*2,0)
                load(t*2+1,1)
        @block.tensor
        def _(pe):
            up.start(pe)
            down.start(pe)
            pe.wait_ge(w_in,64)
            def go_up(i,e,par):
                if e==0: landed(pe,n_in,i,par)
                u=i*EX+e
                active.before(pe,u,2)
                for f in range(2):
                    last=nc.tensor.matmul(hP[e%2][:,f,:],w1s[:,e,f*P:f*P+P],xs[:,par,:],start=True,stop=True)
                last.then_inc(up.sem,1)
            def go_down(i,e):
                u=i*EX+e
                active.of(pe,u)
                gated.before(pe,u,2)
                for f in range(2):
                    last=nc.tensor.matmul(oP[e%2][:,:],w2s[:,e,f,:],hid[:,e%2,f,:],start=(f==0),stop=(f==1))
                last.then_inc(down.sem,1)
            def tile(i,par,more):
                for e in range(EX):
                    if e<EX-1: go_up(i,e+1,par)
                    elif more:
                        go_up(i+1,0,1-par)
                    go_down(i,e)
            go_up(0,0,0)
            tiles(pe,tile)
        @block.scalar
        def _(act):
            active.start(act)
            nc.scalar.preload_act_table(ACT.Gelu)
            act.wait_ge(w_in,64)
            def tile(i,par,more):
                for e in range(EX):
                    u=i*EX+e
                    up.of(act,u)
                    down.before(act,u,2)
                    for f in range(2):
                        last=nc.scalar.activation(hid[:,e%2,f,:],hP[e%2][:,f,:],ACT.Gelu,bias=b1s[:,e,f:f+1])
                    last.then_inc(active.sem,1)
            tiles(act,tile)
        @block.vector
        def _(dve):
            gated.start(dve)
            summed.start(dve)
            dve.wait_ge(w_in,64)
            def tile(i,par,more):
                landed(dve,g_in,i,par)
                landed(dve,x_in,i,par)
                out.done.before(dve,i,2)
                for e in range(EX):
                    u=i*EX+e
                    down.of(dve,u)
                    nc.vector.scalar_tensor_tensor(part[:,e%2,:],oP[e%2][:,:],b2s[:,e:e+1],gt[:,par,e,:],ALU.add,ALU.mult).then_inc(gated.sem,1)
                    gated.of(dve,u)
                    if e: summed.of(dve,u-1)
                    nc.vector.tensor_tensor(acc[:,par,:],xt[:,par,:] if e==0 else acc[:,par,:],part[:,e%2,:],ALU.add).then_inc(summed.sem,1)
            tiles(dve,tile)
        @block.gpsimd
        def _(pool):
            def store(i,par):
                summed.of(pool,i*EX+EX-1)
                pool.dma_start(x_out[:,bass.ds(i*T,T)],acc[:,par,:]).then_inc(out.sems[par],16)
                out.landed(pool,i,par)
            out.start(pool)
            paired(pool,TILES,store)


PADT=TOK+2
NDT=32
def mamba_in(nc, x, lnw, lnb, wdt, dtb, ones, xs_out, dt_out, tag="m1"):
    with ExitStack() as ctx:
        ctx.enter_context(nc.cleanup_on_exit())
        r=Room(nc,ctx,tag)
        xt=r.sb("x",[P,2,T])
        x1=r.sb("x1",[P,2,T])
        xs=r.sb("xs",[P,2,T])
        mw=r.sb("mw",[P,P])
        wd=r.sb("wd",[P,NDT])
        lw=r.sb("lw",[P,1])
        lb=r.sb("lb",[P,1])
        db=r.sb("db",[NDT,1])
        eps=r.sb("eps",[P,2])
        zero=r.sb("zero",[P,2])
        lin=r.sb("lin",[NDT,2,T])
        mag=r.sb("mag",[NDT,2,T])
        soft=r.sb("soft",[NDT,2,T])
        dt=r.sb("dt",[NDT,2,T])
        dP=r.pb("dP",[NDT,T])
        w_in=r.sem("w_in")
        const=r.sem("const")
        pads=r.sem("pads")
        x_in=r.pair("x_in")
        xs_stores=Stores(r,"xs_out")
        dt_stores=Stores(r,"dt_out")
        affine,stepped,lined,sized,decayed,logged,softened=r.flags("affine stepped lined sized decayed logged softened")
        n1=Norm(nc,r,"n1",mw[:,:],eps[:,0:1],lambda i,par:xt[:,par,:],lambda e,i,par: landed(e,x_in,i,par),lambda i,par:x1[:,par,:],lambda e,i,par: n2.centred.before(e,i,2))
        def free(e,i,par):
            xs_stores.done.before(e,i,2)
            stepped.before(e,i,2)
        n2=Norm(nc,r,"n2",mw[:,:],eps[:,1:2],lambda i,par:x1[:,par,:],lambda e,i,par: n1.normed.of(e,i),lambda i,par:xs[:,par,:],free)
        block=ctx.enter_context(nc.Block())
        @block.sync
        def _(sp):
            for d,s in ((mw[:,:],ones),(wd[:,:],wdt),(lw[:,:],lnw),(lb[:,:],lnb),(db[:,:],dtb)):
                sp.dma_start(d,s).then_inc(w_in,16)
            sp.wait_ge(const,1)
            with sp.Fori(0,B) as b:
                sp.dma_start(xs_out[:,bass.ds(b*PADT,2)],zero[:,:]).then_inc(pads,16)
            def load(i,par):
                n1.centred.before(sp,i,2)
                sp.dma_start(xt[:,par,:],x[:,bass.ds(i*T,T)]).then_inc(x_in[par],16)
            paired(sp,TILES,load)
            sp.wait_ge(pads,16*B)
        @block.tensor
        def _(pe):
            n1.pe_start(pe)
            n2.pe_start(pe)
            stepped.start(pe)
            pe.wait_ge(w_in,80)
            def step_sizes(i,par):
                affine.of(pe,i)
                lined.before(pe,i,1)
                nc.tensor.matmul(dP[:,:],wd[:,:],xs[:,par,:],start=True,stop=True).then_inc(stepped.sem,1)
            lagged(pe,TILES,[lambda i,p:n1.pe_mean(pe,i,p),lambda i,p:n1.pe_var(pe,i,p),lambda i,p:n2.pe_mean(pe,i,p),lambda i,p:n2.pe_var(pe,i,p),step_sizes],order=[3,1,2,0,4])
        @block.scalar
        def _(act):
            nc.scalar.preload_act_table_set("natural_log_exp_and_others")
            n1.act_start(act)
            n2.act_start(act)
            for f in (lined,sized,decayed,logged): f.start(act)
            act.wait_ge(const,1)
            act.wait_ge(w_in,80)
            def softplus(i,par):
                stepped.of(act,i)
                softened.before(act,i,2)
                nc.scalar.activation(lin[:,par,:],dP[:,:],ACT.Identity,bias=db[:,0:1]).then_inc(lined.sem,1)
                lined.of(act,i)
                nc.scalar.activation(mag[:,par,:],lin[:,par,:],ACT.Abs).then_inc(sized.sem,1)
                sized.of(act,i)
                nc.scalar.activation(soft[:,par,:],mag[:,par,:],ACT.Exp,scale=-1.0).then_inc(decayed.sem,1)
                decayed.of(act,i)
                nc.scalar.activation(soft[:,par,:],soft[:,par,:],ACT.Ln,bias=1.0).then_inc(logged.sem,1)
            lagged(act,TILES,[lambda i,p:n1.act_square(act,i,p),lambda i,p:n1.act_root(act,i,p),lambda i,p:n2.act_square(act,i,p),lambda i,p:n2.act_root(act,i,p),softplus],order=[3,1,2,0,4])
        @block.vector
        def _(dve):
            n1.dve_start(dve)
            n2.dve_start(dve)
            affine.start(dve)
            softened.start(dve)
            nc.vector.memset(eps[:,0:1],1e-6)
            nc.vector.memset(eps[:,1:2],1e-5)
            nc.vector.memset(zero[:,:],0.0).then_inc(const,1)
            dve.wait_ge(w_in,80)
            def scale(i,par):
                n2.dve_scale(dve,i,par)
                n2.normed.of(dve,i)
                nc.vector.tensor_scalar(xs[:,par,:],xs[:,par,:],lw[:,0:1],lb[:,0:1],ALU.mult,ALU.add).then_inc(affine.sem,1)
            def soften(i,par):
                logged.of(dve,i)
                dt_stores.done.before(dve,i,2)
                nc.vector.scalar_tensor_tensor(dt[:,par,:],lin[:,par,:],0.0,soft[:,par,:],ALU.max,ALU.add).then_inc(softened.sem,1)
            lagged(dve,TILES,[lambda i,p:n1.dve_centre(dve,i,p),lambda i,p:n1.dve_scale(dve,i,p),lambda i,p:n2.dve_centre(dve,i,p),scale,soften],order=[3,1,2,0,4])
        @block.gpsimd
        def _(pool):
            xs_stores.start(pool)
            dt_stores.start(pool)
            with pool.Fori(0,B) as b:
                with pool.Fori(0,TPI//2) as t:
                    for par in range(2):
                        i=b*TPI+t*2+par
                        affine.of(pool,i)
                        pool.dma_start(xs_out[:,bass.ds(b*PADT+(t*2+par)*T+2,T)],xs[:,par,:]).then_inc(xs_stores.sems[par],16)
                        softened.of(pool,i)
                        pool.dma_start(dt_out[:,bass.ds(i*T,T)],dt[:,par,:]).then_inc(dt_stores.sems[par],16)
                        xs_stores.landed(pool,i,par)
                        dt_stores.landed(pool,i,par)


PADT=TOK+2
NDT=32
K=32
CH=T//K
H=4
SP=4
HD=8
UNITS=2*TPI
def mamba_core(nc, xs, dt, wx, wb, wc, wz, cw, cb, alog_row, alog_col, dcol, consts, y_out, placed=None, rec=None, tag="m2"):
    with ExitStack() as ctx:
        ctx.enter_context(nc.cleanup_on_exit())
        r=Room(nc,ctx,tag)
        wk=r.sb("wk",[P,3,2,3,P])
        raw=r.sb("raw",[P,2,P])
        cws=r.sb("cw",[P,9,P])
        wzs=r.sb("wz",[P,2,P])
        hb=r.sb("hb",[P,3])
        arow=r.sb("arow",[P,4])
        acol=r.sb("acol",[P,1])
        ds=r.sb("ds",[P,1])
        tri=r.sb("tri",[P,K])
        after=r.sb("after",[P,P])
        same=r.sb("same",[P,P])
        blk=r.sb("blk",[P,4])
        place=r.sb("place",[NDT,2,P])
        expand=r.sb("expand",[NDT,2,P])
        keep=r.sb("keep",[P,T])
        perm=r.sb("perm",[P,P])
        xq=r.sb("xq",[P,2,T+2])
        dr=r.sb("dr",[NDT,2,T])
        half=r.sb("half",[P,4,T])
        tan=r.sb("tan",[P,4,T])
        X,Bc,Cc,Z=[r.sb(n,[P,2,T]) for n in ("X","B","C","Z")]
        dtT=r.sb("dtT",[P,2,T])
        dAT=r.sb("dAT",[P,2,CH*H])
        XT=r.sb("XT",[P,T])
        BT=r.sb("BT",[P,2,T])
        xdt=r.sb("xdt",[P,2,T])
        xdec=r.sb("xdec",[P,T])
        R=r.sb("R",[P,CH*H,K])
        EX=r.sb("EX",[P,CH*H,K])
        M=r.sb("M",[P,2,CH*H,K])
        XB=r.sb("XB",[P,2,CH*H,SP,HD])
        PB=r.sb("PB",[P,2,CH,H,SP,HD])
        Gm=r.sb("Gm",[P,T])
        dA=r.sb("dA",[P,2,T])
        ac=r.sb("ac",[P,2,T])
        EA=r.sb("EA",[P,2,T])
        cd=r.sb("cd",[P,CH*H])
        D0=r.sb("D0",[P,32,CH])
        S1=r.sb("S1",[P,32,CH])
        ST=r.sb("ST",[P,2,T])
        carry=r.sb("carry",[P,2,32])
        tmp=r.sb("tmp",[P,32])
        y1=r.sb("y1",[P,T])
        y2=r.sb("y2",[P,T])
        y3=r.sb("y3",[P,2,T])
        pj=[r.pb(f"pj{k}",[P,T]) for k in range(2)]
        sg=[r.pb(f"sg{k}",[P,T]) for k in range(2)]
        GP=r.pb("G",[P,T])
        SPs=r.pb("S",[P,T])
        YP=r.pb("Y",[P,T])
        YO=r.pb("YO",[P,T])
        w_in=r.sem("w_in")
        raw_in=r.sem("raw_in")
        raw_used=r.sem("raw_used")
        w_ready=r.sem("w_ready")
        aexp=r.sem("aexp")
        reset=r.sem("reset")
        pe_gate=r.sem("pe_gate")
        x_in=r.pair("x_in")
        d_in=r.pair("d_in")
        out_s=r.pair("out")
        stored,=r.flags("stored")
        pT,pA,pX,pB,pC,pZ,segs,gs,ss,cds,ys,yos=r.flags("pT pA pX pB pC pZ segs gs ss cds ys yos")
        stepped,hX,hB,hC,hZ,exs,cde,eas,scop,xbs,pbs=r.flags("stepped hX hB hC hZ exs cde eas scop xbs pbs")
        dtt,dat,rs,scn,sX,sB,sC,sZ,xtt,btt,xd,gm,dec,ms,d0,tm,pb0,s1,sts,car,yy1,yy2,yy3=r.flags("dtt dat rs scn sX sB sC sZ xtt btt xd gm dec ms d0 tm pb0 s1 sts car yy1 yy2 yy3")
        block=ctx.enter_context(nc.Block())
        V,A,TE=nc.vector,nc.scalar,nc.tensor
        def images(eng, stages, begin=None):
            with eng.Fori(0,B) as b:
                if begin: begin(b)
                lagged(eng,UNITS,stages,base=b*UNITS,last_first=True)
        @block.sync
        def _(sp):
            small=((cws[:,:,:],cw.partition_broadcast(P)),(wzs[:,:,:],wz),(hb[:,:],cb),(arow[:,:],alog_row.partition_broadcast(P)),(acol[:,:],alog_col),(ds[:,:],dcol))
            for d,s in small: sp.dma_start(d,s).then_inc(w_in,16)
            for d,n in ((tri[:,:],"tri"),(after[:,:],"after"),(same[:,:],"same"),(blk[:,:],"block"),(place[:,:,:],"place"),(expand[:,:,:],"expand"),(keep[:,:],"keep"),(perm[:,:],"perm")):
                sp.dma_start(d,consts[n]).then_inc(w_in,16)
            for k,w in enumerate((wx,wb,wc)):
                if k: sp.wait_ge(raw_used,k)
                sp.dma_start(raw[:,:,:],w).then_inc(raw_in,16)
            def load(b,j,q):
                pZ.before(sp,b*UNITS+j*2+q,2)
                sp.dma_start(xq[:,q,:],xs[:,bass.ds(b*PADT+j*T,T+2)]).then_inc(x_in[q],16)
                sp.dma_start(dr[:,q,:],dt[:,bass.ds(b*TOK+j*T,T)]).then_inc(d_in[q],16)
            def store(i,q):
                yy3.of(sp,i)
                sp.dma_start(y_out[q,:,bass.ds((i-q)*(T//2),T)],y3[:,q,:]).then_inc(out_s[q],16)
            def stored_before(i,q):
                sp.wait_ge(out_s[1-q],(i-1-(1-q))*8+16)
                sp.sem_inc(stored.sem,1)
            stored.start(sp)
            for j in range(2):
                for q in range(2): load(0,j,q)
            store(0,0)
            load(0,2,0)
            store(1,1)
            stored_before(1,1)
            load(0,2,1)
            with sp.Fori(3,TPI) as j:
                for q in range(2):
                    store(j*2+q-4,q)
                    stored_before(j*2+q-4,q)
                    load(0,j,q)
            with sp.Fori(1,B) as b:
                with sp.Fori(0,TPI) as j:
                    for q in range(2):
                        store(b*UNITS+j*2+q-4,q)
                        stored_before(b*UNITS+j*2+q-4,q)
                        load(b,j,q)
            for i in range(B*UNITS-4,B*UNITS):
                store(i,i%2)
                stored_before(i,i%2)
            for q in range(2): sp.wait_ge(out_s[q],8*B*UNITS)
        @block.tensor
        def _(pe):
            for f in (pT,pA,pX,pB,pC,pZ,segs,gs,ss,cds,ys,yos): f.start(pe)
            pe.wait_ge(w_in,16*14)
            pe.wait_ge(w_ready,1)
            def project(i,q):
                landed(pe,x_in,i,q)
                landed(pe,d_in,i,q)
                hC.before(pe,i,1)
                TE.matmul(pj[0][:,:],place[:,q,:],dr[:,q,:],start=True,stop=True).then_inc(pT.sem,1)
                hZ.before(pe,i,1)
                TE.matmul(pj[1][:,:],expand[:,q,:],dr[:,q,:],start=True,stop=True).then_inc(pA.sem,1)
                for k,(p,bank,free) in enumerate(((pX,0,dtt),(pB,1,stepped),(pC,0,hX))):
                    free.of(pe,i)
                    for tap in range(3):
                        last=TE.matmul(pj[bank][:,:],wk[:,k,q,tap,:],xq[:,q,tap:tap+T],start=(tap==0),stop=(tap==2))
                    last.then_inc(p.sem,1)
                hB.of(pe,i)
                TE.matmul(pj[1][:,:],wzs[:,q,:],xq[:,q,2:T+2],start=True,stop=True).then_inc(pZ.sem,1)
            def middle(i,q):
                dat.of(pe,i)
                yy1.before(pe,i,1)
                TE.matmul(YO[:,0:CH*H],same[:,:],dAT[:,q,:],start=True,stop=True).then_inc(cds.sem,1)
                rs.of(pe,i)
                for c in range(4):
                    exs.before(pe,i*4+c,2)
                    TE.matmul(sg[c%2][:,:],after[:,:],R[:,c*16:c*16+16,:],start=True,stop=True).then_inc(segs.sem,1)
                sB.of(pe,i)
                sC.of(pe,i)
                gm.before(pe,i,1)
                pe.sem_inc(pe_gate,1)
                for c in range(CH):
                    for s in range(SP):
                        q4=slice(32*s,32*s+32)
                        k=slice(c*K,c*K+K)
                        last=TE.matmul(GP[q4,k],Bc[q4,q,k],Cc[q4,q,k],start=True,stop=True,skip_group_check=True)
                last.then_inc(gs.sem,1)
                btt.of(pe,i)
                dec.of(pe,i)
                scop.before(pe,i,1)
                pe.sem_inc(pe_gate,1)
                for c in range(CH):
                    for s in range(SP):
                        q4=slice(32*s,32*s+32)
                        k=slice(c*K,c*K+K)
                        last=TE.matmul(SPs[q4,k],BT[q4,q,k],xdec[q4,k],start=True,stop=True,skip_group_check=True)
                last.then_inc(ss.sem,1)
            def outputs(i,q):
                yy2.before(pe,i,1)
                sX.of(pe,i)
                TE.matmul(YP[:,:],perm[:,:],X[:,q,:],start=True,stop=False,skip_group_check=True)
                ms.of(pe,i)
                xbs.of(pe,i)
                pe.sem_inc(pe_gate,1)
                for c in range(CH):
                    for h in range(H):
                        last=TE.matmul(YP[32*h:32*h+32,c*K:c*K+K],XB[:,q,c*H+h,:,:],M[:,q,c*H+h,:],start=False,stop=True,skip_group_check=True)
                last.then_inc(ys.sem,1)
                pbs.of(pe,i)
                pb0.of(pe,i)
                cde.of(pe,i)
                for c in range(CH):
                    last=TE.matmul(YO[:,c*K:c*K+K],PB[:,q,c,:,:,:],Cc[:,q,c*K:c*K+K],start=True,stop=True,skip_group_check=True)
                last.then_inc(yos.sem,1)
            images(pe,[project,middle,outputs])
        @block.scalar
        def _(act):
            A.preload_act_table_set("exp_and_others")
            for f in (stepped,hX,hB,hC,hZ,exs,cde,eas,scop,xbs,pbs): f.start(act)
            act.wait_ge(w_in,16*14)
            A.activation(arow[:,:],arow[:,:],ACT.Exp)
            A.activation(acol[:,:],acol[:,:],ACT.Exp).then_inc(aexp,1)
            act.wait_ge(w_ready,1)
            def halves(i,q):
                pA.of(act,i)
                scn.before(act,i,2)
                A.activation(dA[:,q,:],pj[1][:,:],ACT.Copy,scale=acol[:,0:1]).then_inc(stepped.sem,1)
                for k,(p,bank,flag,used) in enumerate(((pX,0,hX,sX),(pB,1,hB,sB),(pC,0,hC,sC),(pZ,1,hZ,sZ))):
                    p.of(act,i)
                    used.before(act,i,1)
                    kw=dict(bias=hb[:,k:k+1]) if k<3 else {}
                    A.activation(half[:,k,:],pj[bank][:,:],ACT.Identity,scale=0.5,**kw)
                    A.activation(tan[:,k,:],pj[bank][:,:],ACT.Tanh,scale=0.5,**kw).then_inc(flag.sem,1)
            def middle(i,q):
                cds.of(act,i)
                d0.before(act,i,1)
                tm.before(act,i,1)
                A.activation(cd[:,:],YO[:,0:CH*H],ACT.Exp).then_inc(cde.sem,1)
                ms.before(act,i,1)
                dec.before(act,i,1)
                for c in range(4):
                    segs.of(act,i*4+c)
                    A.activation(EX[:,c*16:c*16+16,:],sg[c%2][:,:].rearrange("p (a l) -> p a l",l=K),ACT.Exp).then_inc(exs.sem,1)
                scn.of(act,i)
                yy1.before(act,i,2)
                A.activation(EA[:,q,:],ac[:,q,:],ACT.Exp).then_inc(eas.sem,1)
                xd.of(act,i)
                ys.before(act,i,2)
                for s in range(SP):
                    last=A.activation(XB[:,q,:,s,:],xdt[:,q,:].rearrange("p (a d) -> p a d",d=HD),ACT.Copy,scale=blk[:,s:s+1])
                last.then_inc(xbs.sem,1)
                ss.of(act,i)
                sts.before(act,i,1)
                A.copy(S1[:,:,:],SPs[:,:].rearrange("p (c x) -> p x c",x=32)).then_inc(scop.sem,1)
                sts.of(act,i)
                yos.before(act,i,2)
                for s in range(SP):
                    last=A.activation(PB[:,q,1:CH,:,s,:],ST[:,q,:].rearrange("p (h x c) -> p c h x",h=H,c=CH)[:,0:CH-1,:,:],ACT.Copy,scale=blk[:,s:s+1])
                last.then_inc(pbs.sem,1)
            images(act,[halves,middle,lambda i,q:None])
        @block.vector
        def _(dve):
            for f in (dtt,dat,rs,scn,sX,sB,sC,sZ,xtt,btt,xd,gm,dec,ms,d0,tm,pb0,s1,sts,car,yy1,yy2,yy3):
                f.start(dve)
            dve.wait_ge(w_in,16*14)
            dve.wait_ge(aexp,1)
            for k in range(3):
                dve.wait_ge(raw_in,16*(k+1))
                for q in range(2):
                    for tap in range(3):
                        last=V.tensor_tensor(wk[:,k,q,tap,:],raw[:,q,:],cws[:,k*3+tap,:],ALU.mult)
                last.then_inc(raw_used,1)
            V.tensor_scalar(arow[:,:],arow[:,:],-1.0,None,ALU.mult)
            V.tensor_scalar(acol[:,:],acol[:,:],-1.0,None,ALU.mult)
            V.tensor_scalar(hb[:,:],hb[:,:],0.5,None,ALU.mult)
            V.memset(D0[:,:,:],0.0)
            V.tensor_scalar(perm[:,:],perm[:,:],ds[:,0:1],None,ALU.mult).then_inc(w_ready,1)
            dve.wait_ge(w_ready,1)
            trib=lambda n: tri[:,:].unsqueeze(1).broadcast_to([P,n,K])
            def ahead(i,q):
                pT.of(dve,i)
                xd.before(dve,i,2)
                V.transpose(dtT[:,q,:],pj[0][:,:]).then_inc(dtt.sem,1)
                dtt.of(dve,i)
                cds.before(dve,i,2)
                d=dtT[:,q,:].rearrange("p (c x) -> p c x",x=32)[:,:,0:H]
                V.tensor_tensor(dAT[:,q,:].rearrange("p (c h) -> p c h",h=H),d,arow[:,:].unsqueeze(1).broadcast_to([P,CH,H]),ALU.mult).then_inc(dat.sem,1)
                dat.of(dve,i)
                segs.of(dve,i*4-1)
                V.tensor_tensor(R[:,:,:],dAT[:,q,:].unsqueeze(2).broadcast_to([P,CH*H,K]),trib(CH*H),ALU.mult).then_inc(rs.sem,1)
                stepped.of(dve,i)
                eas.before(dve,i,2)
                V.tensor_tensor_scan(ac[:,q,:],keep[:,:],dA[:,q,:],0.0,ALU.mult,ALU.add).then_inc(scn.sem,1)
                for k,(h_,s_,o) in enumerate(((hX,sX,X),(hB,sB,Bc),(hC,sC,Cc),(hZ,sZ,Z))):
                    h_.of(dve,i)
                    if k==0: ys.before(dve,i,2)
                    if k==1: gs.before(dve,i,2)
                    if k==2: yos.before(dve,i,2)
                    if k==3: yy3.before(dve,i,2)
                    V.scalar_tensor_tensor(o[:,q,:],tan[:,k,:],1.0,half[:,k,:],ALU.add,ALU.mult).then_inc(s_.sem,1)
                sX.of(dve,i)
                xd.before(dve,i,1)
                V.transpose(XT[:,:],X[:,q,:]).then_inc(xtt.sem,1)
                sB.of(dve,i)
                ss.before(dve,i,2)
                V.transpose(BT[:,q,:],Bc[:,q,:]).then_inc(btt.sem,1)
                xtt.of(dve,i)
                xbs.before(dve,i,2)
                dec.before(dve,i,2)
                V.tensor_tensor(xdt[:,q,:].rearrange("p (c h d) -> p c h d",h=H,d=HD),XT[:,:].rearrange("p (c h d) -> p c h d",h=H,d=HD),d.unsqueeze(3).broadcast_to([P,CH,H,HD]),ALU.mult).then_inc(xd.sem,1)
            def middle(i,q):
                exs.of(dve,i*4+3)
                xd.of(dve,i)
                ss.before(dve,i,1)
                V.tensor_tensor(xdec[:,:].rearrange("p (a d) -> p a d",d=HD),xdt[:,q,:].rearrange("p (a d) -> p a d",d=HD),EX[:,:,K-1:K].broadcast_to([P,CH*H,HD]),ALU.mult).then_inc(dec.sem,1)
                gs.of(dve,i)
                ms.before(dve,i,1)
                V.tensor_tensor(Gm[:,:].rearrange("p (c l) -> p c l",l=K),GP[:,:].rearrange("p (c l) -> p c l",l=K),trib(CH),ALU.mult).then_inc(gm.sem,1)
                gm.of(dve,i)
                ys.before(dve,i,2)
                V.tensor_tensor(M[:,q,:,:].rearrange("p (c h) l -> p c h l",h=H),EX[:,:,:].rearrange("p (c h) l -> p c h l",h=H),Gm[:,:].rearrange("p (c l) -> p c l",l=K).unsqueeze(2).broadcast_to([P,CH,H,K]),ALU.mult).then_inc(ms.sem,1)
                cde.of(dve,i)
                sts.before(dve,i,1)
                cv=cd[:,:].rearrange("p (c h) -> p h c",h=H)
                V.tensor_copy(D0[:,:,1:CH].rearrange("p (h x) c -> p h x c",h=H),cv[:,:,1:CH].unsqueeze(2).broadcast_to([P,H,HD,CH-1])).then_inc(d0.sem,1)
                s1.before(dve,i,1)
                car.before(dve,i,1)
                V.tensor_tensor(tmp[:,:].rearrange("p (h x) -> p h x",h=H),carry[:,q,:].rearrange("p (h x) -> p h x",h=H),cv[:,:,0:1].broadcast_to([P,H,HD]),ALU.mult).then_inc(tm.sem,1)
                yos.before(dve,i,2)
                V.tensor_tensor(PB[:,q,0,:,:,:],carry[:,q,:].rearrange("p (h x) -> p h x",h=H).unsqueeze(2).broadcast_to([P,H,SP,HD]),blk[:,:].unsqueeze(1).unsqueeze(3).broadcast_to([P,H,SP,HD]),ALU.mult).then_inc(pb0.sem,1)
                scop.of(dve,i)
                tm.of(dve,i)
                V.tensor_tensor(S1[:,:,0],S1[:,:,0],tmp[:,:],ALU.add).then_inc(s1.sem,1)
                s1.of(dve,i)
                d0.of(dve,i)
                pbs.before(dve,i,2)
                V.tensor_tensor_scan(ST[:,q,:],D0[:,:,:].rearrange("p x c -> p (x c)"),S1[:,:,:].rearrange("p x c -> p (x c)"),0.0,ALU.mult,ALU.add).then_inc(sts.sem,1)
                sts.of(dve,i)
                pb0.of(dve,i)
                V.tensor_copy(carry[:,q,:],ST[:,q,:].rearrange("p (x c) -> p x c",c=CH)[:,:,CH-1]).then_inc(car.sem,1)
            def finish(i,q):
                yos.of(dve,i)
                eas.of(dve,i)
                yy2.before(dve,i,1)
                V.tensor_tensor(y1[:,:],YO[:,:],EA[:,q,:],ALU.mult).then_inc(yy1.sem,1)
                yy1.of(dve,i)
                ys.of(dve,i)
                yy3.before(dve,i,1)
                V.tensor_tensor(y2[:,:],YP[:,:],y1[:,:],ALU.add).then_inc(yy2.sem,1)
                yy2.of(dve,i)
                sZ.of(dve,i)
                stored.before(dve,i,2)
                V.tensor_tensor(y3[:,q,:],y2[:,:],Z[:,q,:],ALU.mult).then_inc(yy3.sem,1)
            def begin(b):
                car.of(dve,b*UNITS-1)
                V.memset(carry[:,:,:],0.0).then_inc(reset,1)
                dve.wait_ge(reset,b+1)
            images(dve,[ahead,middle,finish],begin)
        if placed is not None:
            scatter=Scatter(nc,r,placed,rec,0,COLS//(2*SHALF))
            block.gpsimd(scatter.pool)

def core_consts():
    p=np.arange(P)
    f=np.float32
    tri=(p[:,None]%K<=np.arange(K)[None]).astype(f)
    same=(p[:,None]//32==p[None]//32).astype(f)
    after=(same*(p[:,None]%32>p[None]%32)).astype(f)
    block=(p[:,None]//32==np.arange(4)[None]).astype(f)
    place=np.zeros((NDT,2,P),f)
    expand=np.zeros((NDT,2,P),f)
    perm=np.zeros((P,P),f)
    for q in range(2):
        for h in range(4):
            for s_ in range(4):
                place[q*16+h*4+s_,q,s_*32+h]=1
                expand[q*16+h*4+s_,q,h*32+s_*8:h*32+s_*8+8]=1
                for d in range(8): perm[s_*32+h*8+d,h*32+s_*8+d]=1
    keep=np.ones((P,T),f)
    keep[:,::K]=0
    return dict(tri=tri,after=after,same=same,block=block,place=place,expand=expand,keep=keep,perm=perm)
def core_weights(W_in,conv_w,conv_b,A_log,D):
    f=np.float32
    wx,wb,wc,wz=[np.zeros((P,2,P),f) for _ in range(4)]
    wdt=np.zeros((P,NDT),f)
    for q in range(2):
        for s_ in range(4):
            rows=slice((q*4+s_)*16,(q*4+s_)*16+16)
            for w,o in ((wx,32),(wb,64),(wc,96)): w[rows,q,s_*32:s_*32+32]=W_in[:,o:o+32]
            for h in range(4):
                wz[rows,q,h*32+s_*8:h*32+s_*8+8]=W_in[:,h*8:h*8+8]
                wdt[rows,q*16+h*4+s_]=W_in[:,128+h]
    cw=conv_w[:,0,:].reshape(3,32,3)
    cw=np.tile(cw.transpose(0,2,1),(1,1,4)).reshape(9,P)
    cb=np.tile(conv_b.reshape(3,1,32),(1,4,1)).reshape(3,P).T
    hsp=np.repeat(A_log,32)[:,None]
    dcol=np.tile(np.repeat(D,8),4)[:,None]
    return dict(wx=wx,wb=wb,wc=wc,wz=wz,cw=np.ascontiguousarray(cw),cb=np.ascontiguousarray(cb),alog_row=A_log,alog_col=np.ascontiguousarray(hsp),dcol=np.ascontiguousarray(dcol)),wdt


PADT=TOK+2
def mamba_out(nc, y, xs, x, wo, rms, skip, lnw, lnb, pw, pb, same_mean, ones, x_out, tag="m3"):
    with ExitStack() as ctx:
        ctx.enter_context(nc.cleanup_on_exit())
        r=Room(nc,ctx,tag)
        yt=r.sb("y",[P,2,2,T])
        xst=r.sb("xs",[P,2,T])
        xt=r.sb("x",[P,2,T])
        sq=r.sb("sq",[P,2,2,T])
        rs=r.sb("rs",[P,2,2,T])
        yn=r.sb("yn",[P,2,2,T])
        ym=r.sb("ym",[P,2,T])
        nn=r.sb("nn",[P,2,T])
        xo=r.sb("xo",[P,2,T])
        wos=r.sb("wo",[P,2,P])
        rm=r.sb("rms",[P,1])
        sk=r.sb("skip",[P,1])
        lw=r.sb("lw",[P,1])
        lb=r.sb("lb",[P,1])
        pws=r.sb("pw",[P,P])
        pbs=r.sb("pb",[P,1])
        sm=r.sb("sm",[P,P])
        mw=r.sb("mw",[P,P])
        eps=r.sb("eps",[P,1])
        rP=r.pb("rP",[P,2,T])
        oP=r.pb("oP",[P,T])
        qP=r.pb("qP",[P,T])
        w_in=r.sem("w_in")
        ready=r.sem("ready")
        y_in=r.pair("y_in")
        s_in=r.pair("s_in")
        x_in=r.pair("x_in")
        out=Stores(r,"out")
        squared,meaned,logged,rooted,scaled,mixed,skipped,affine,projected,added=r.flags("squared meaned logged rooted scaled mixed skipped affine projected added")
        nm=Norm(nc,r,"n",mw[:,:],eps[:,0:1],lambda i,par:ym[:,par,:],lambda e,i,par: skipped.of(e,i),lambda i,par:nn[:,par,:],lambda e,i,par: projected.before(e,i,2))
        block=ctx.enter_context(nc.Block())
        @block.sync
        def _(sp):
            for d,s in ((wos[:,:,:],wo),(rm[:,:],rms),(sk[:,:],skip.partition_broadcast(P)),(lw[:,:],lnw),(lb[:,:],lnb),(pws[:,:],pw),(pbs[:,:],pb),(sm[:,:],same_mean),(mw[:,:],ones)):
                sp.dma_start(d,s).then_inc(w_in,16)
            with sp.Fori(0,B) as b:
                with sp.Fori(0,TPI//2) as t:
                    for par in range(2):
                        i=b*TPI+t*2+par
                        scaled.before(sp,i,2)
                        sp.dma_start(yt[:,par,:,:],y.rearrange("q p n -> p q n")[:,:,bass.ds(i*T,T)]).then_inc(y_in[par],16)
                        skipped.before(sp,i,2)
                        sp.dma_start(xst[:,par,:],xs[:,bass.ds(b*PADT+(t*2+par)*T+2,T)]).then_inc(s_in[par],16)
        @block.tensor
        def _(pe):
            nm.pe_start(pe)
            for f in (meaned,mixed,projected): f.start(pe)
            pe.wait_ge(w_in,16*9)
            pe.wait_ge(ready,1)
            def mean_square(i,par):
                squared.of(pe,i)
                logged.before(pe,i,1)
                for q in range(2):
                    last=nc.tensor.matmul(rP[:,q,:],sm[:,:],sq[:,par,q,:],start=True,stop=True)
                last.then_inc(meaned.sem,1)
            def mix(i,par):
                scaled.of(pe,i)
                skipped.before(pe,i,1)
                for q in range(2):
                    last=nc.tensor.matmul(oP[:,:],wos[:,q,:],yn[:,par,q,:],start=(q==0),stop=(q==1))
                last.then_inc(mixed.sem,1)
            def project(i,par):
                affine.of(pe,i)
                added.before(pe,i,1)
                nc.tensor.matmul(qP[:,:],pws[:,:],nn[:,par,:],start=True,stop=True).then_inc(projected.sem,1)
            lagged(pe,TILES,[mean_square,mix,lambda i,p:nm.pe_mean(pe,i,p),lambda i,p:nm.pe_var(pe,i,p),project],last_first=True)
        @block.scalar
        def _(act):
            nc.scalar.preload_act_table_set("natural_log_exp_and_others")
            nm.act_start(act)
            for f in (squared,logged,rooted): f.start(act)
            act.wait_ge(ready,1)
            def square(i,par):
                landed(act,y_in,i,par)
                meaned.before(act,i,2)
                nc.scalar.activation(sq[:,par,:,:],yt[:,par,:,:],ACT.Square).then_inc(squared.sem,1)
            def root(i,par):
                meaned.of(act,i)
                rooted.before(act,i,1)
                scaled.before(act,i,2)
                for q in range(2):
                    last=nc.scalar.activation(rs[:,par,q,:],rP[:,q,:],ACT.Ln,bias=eps[:,0:1])
                last.then_inc(logged.sem,1)
                logged.of(act,i)
                nc.scalar.activation(rs[:,par,:,:],rs[:,par,:,:],ACT.Exp,scale=-0.5).then_inc(rooted.sem,1)
            lagged(act,TILES,[square,root,lambda i,p:None,lambda i,p:nm.act_square(act,i,p),lambda i,p:nm.act_root(act,i,p)],last_first=True)
        @block.vector
        def _(dve):
            nm.dve_start(dve)
            for f in (scaled,skipped,affine,added): f.start(dve)
            dve.wait_ge(w_in,16*9)
            nc.vector.memset(eps[:,:],1e-5)
            for q in range(2):
                last=nc.vector.tensor_scalar(wos[:,q,:],wos[:,q,:],rm[:,0:1],None,ALU.mult)
            last.then_inc(ready,1)
            def scale(i,par):
                rooted.of(dve,i)
                mixed.before(dve,i,2)
                nc.vector.tensor_tensor(yn[:,par,:,:],yt[:,par,:,:],rs[:,par,:,:],ALU.mult).then_inc(scaled.sem,1)
            def add_skip(i,par):
                mixed.of(dve,i)
                landed(dve,s_in,i,par)
                nm.centred.before(dve,i,2)
                nc.vector.scalar_tensor_tensor(ym[:,par,:],xst[:,par,:],sk[:,0:1],oP[:,:],ALU.mult,ALU.add).then_inc(skipped.sem,1)
            def norm(i,par):
                nm.dve_scale(dve,i,par)
                nm.normed.of(dve,i)
                nc.vector.tensor_scalar(nn[:,par,:],nn[:,par,:],lw[:,0:1],lb[:,0:1],ALU.mult,ALU.add).then_inc(affine.sem,1)
            def add_x(i,par):
                projected.of(dve,i)
                landed(dve,x_in,i,par)
                out.done.before(dve,i,2)
                nc.vector.scalar_tensor_tensor(xo[:,par,:],qP[:,:],pbs[:,0:1],xt[:,par,:],ALU.add,ALU.add).then_inc(added.sem,1)
            lagged(dve,TILES,[scale,add_skip,lambda i,p:nm.dve_centre(dve,i,p),norm,add_x],last_first=True)
        @block.gpsimd
        def _(pool):
            def load(i,par):
                pool.dma_start(xt[:,par,:],x[:,bass.ds(i*T,T)]).then_inc(x_in[par],16)
            def store(i,par):
                added.of(pool,i)
                pool.dma_start(x_out[:,bass.ds(i*T,T)],xo[:,par,:]).then_inc(out.sems[par],16)
            out.start(pool)
            load(0,0)
            load(1,1)
            with pool.Fori(0,TILES//2-1) as t:
                for par in range(2):
                    store(t*2+par,par)
                    load(t*2+par+2,par)
                    out.landed(pool,t*2+par,par)
            for par in range(2):
                store(TILES-2+par,par)
                out.landed(pool,TILES-2+par,par)
def out_weights(W_out,rms_w):
    wo=np.zeros((P,2,P),np.float32)
    rms=np.zeros((P,1),np.float32)
    for q in range(2):
        for h in range(4):
            for s in range(4):
                for d in range(8):
                    k=h*32+s*8+d
                    wo[k,q,(q*4+s)*16:(q*4+s)*16+16]=W_out[h*8+d]
                    rms[k]=rms_w[h*8+d]
    p=np.arange(P)
    sm=((p[:,None]//8%4)==(p[None]//8%4)).astype(np.float32)/32
    return wo,rms,sm


def build(nc, a, out):
    dram=lambda n,s,d=f32: nc.dram_tensor(n,s,d).ap()
    consts={k[2:]: v for k,v in a.items() if k.startswith("c_")}
    rec=[dram(f"rec{l}",[E,2],i32) for l in range(2)]
    start=[dram(f"start{l}",[P,HI]) for l in range(2)]
    deg=[dram(f"deg{l}",[P,HI]) for l in range(2)]
    placed=dram("placed",[P,COLS,3],i32)
    x1,x2,x3=dram("x1",[P,NODES]),dram("x2",[P,NODES]),dram("x3",[P,NODES])
    xn,table,gates=dram("xn",[P,NODES]),dram("table",[NODES,HW]),dram("gates",[EX,NODES])
    by_edge=edge_arrays(nc,"e")
    def project(l,x): heads(nc,x,a[f"wg{l}"],a[f"att{l}"],a["c_ones"],xn,table,tag=f"h{l}")
    def attend_and_feed(l,x,x_out):
        attention(nc,rec[l],start[l],deg[l],table,a[f"bgat{l}"],a[f"gamma{l}"],a[f"beta{l}"],a["c_eye"],gates,by_edge,tag=f"g{l}")
        experts(nc,x,xn,gates,a[f"w1_{l}"],a[f"b1_{l}"],a[f"w2_{l}"],a[f"b2_{l}"],x_out,tag=f"f{l}")
    def first_part(room,chunks):
        return None,Scatter(nc,room,placed,rec[0],0,FIRST_TURNS,chunks).pool
    sort_edges(nc,a["edges0"],placed,start[0],deg[0],first_part,tag="s0")
    def second_part(room): return Scatter(nc,room,placed,rec[0],FIRST_TURNS,COLS//(2*SHALF)).pool
    involution(nc,a["x"],a["cw1"],a["cb1"],a["cwd"],a["cw2"],a["cbd"],a["cb2"],a["c_pick"],a["c_ones"],x1,second_part)
    project(0,x1)
    def gather_beside(room,chunks):
        g=gather_of(nc,room,rec[0],table,by_edge)
        return g.sync,g.pool
    sort_edges(nc,a["edges1"],placed,start[1],deg[1],gather_beside,tag="s1")
    attend_and_feed(0,x1,x2)
    xs,dt,y=dram("xs",[P,B*PADT]),dram("dt",[NDT,NODES]),dram("y",[2,P,NODES])
    mamba_in(nc,x2,a["lnw"],a["lnb"],a["wdt"],a["dtb"],a["c_ones"],xs,dt)
    mamba_core(nc,xs,dt,a["wx"],a["wb"],a["wc"],a["wz"],a["cw"],a["cb"],a["alog_row"],a["alog_col"],a["dcol"],consts,y,placed,rec[1])
    mamba_out(nc,y,xs,x2,a["wo"],a["rms"],a["skip"],a["lnw"],a["lnb"],a["pw"],a["pb"],a["c_same_mean"],a["c_ones"],x3)
    project(1,x3)
    gather_alone(nc,rec[1],table,by_edge)
    attend_and_feed(1,x3,out)


def laid_out(i):
    tok=np.ascontiguousarray
    col=lambda v: tok(v.reshape(-1,1))
    a={}
    a["x"]=tok(i["x"].transpose(1,0,2,3).reshape(P,NODES))
    a["cw1"]=tok(np.tile(i["L0_conv_w1"].T,(1,3)))
    a["cb1"]=col(np.tile(i["L0_conv_b1"],3))
    a["cwd"]=tok(i["L0_conv_wd"][:,0].transpose(2,0,1).reshape(3*RED,3))
    a["cw2"]=tok(np.tile(i["L0_conv_w2"].T,(3,1)))
    a["cbd"]=col(i["L0_conv_bd"])
    a["cb2"]=col(i["L0_conv_b2"])
    for l in range(2):
        p=f"L{l}_ffn_"
        a[f"edges{l}"]=tok(i[p+"edge_index"])
        a[f"wg{l}"]=tok(i[p+"W_gat"])
        a[f"att{l}"]=tok(np.concatenate([i[p+"att_src"].ravel(),i[p+"att_dst"].ravel()]))
        a[f"bgat{l}"]=tok(i[p+"b_gat"])
        a[f"gamma{l}"]=tok(i[p+"ln_gamma"])
        a[f"beta{l}"]=tok(i[p+"ln_beta"])
        a[f"w1_{l}"]=tok(i[p+"W1"].transpose(1,0,2))
        a[f"b1_{l}"]=tok(i[p+"b1"].reshape(EX,2,P).transpose(2,0,1))
        a[f"w2_{l}"]=tok(i[p+"W2"].reshape(EX,2,P,P).transpose(2,0,1,3))
        a[f"b2_{l}"]=tok(i[p+"b2"].T)
    p="L1_conv_"
    ws,wdt=core_weights(i[p+"W_in"],i[p+"conv_w"],i[p+"conv_b"],i[p+"A_log"],i[p+"D"])
    a.update(ws)
    a["wdt"]=wdt
    a["dtb"]=col(np.tile(np.repeat(i[p+"dt_bias"],4),2))
    a["wo"],a["rms"],same_mean=out_weights(i[p+"W_out"],i[p+"rms_w"])
    a["skip"]=tok(i[p+"skip_scale"])
    a["lnw"]=col(i[p+"ln_w"])
    a["lnb"]=col(i[p+"ln_b"])
    a["pw"]=tok(i[p+"proj_w"])
    a["pb"]=col(i[p+"proj_b"])
    c=core_consts()
    c["same_mean"]=same_mean
    c["ones"]=np.full((P,P),1/P,np.float32)
    c["eye"]=np.eye(P,dtype=np.float32)
    pick=np.zeros((P,9,P),np.float32)
    for k in range(9):
        for ch in range(P): pick[(ch//16)*9+k,k,ch]=1
    c["pick"]=pick
    a.update({"c_"+k: v for k,v in c.items()})
    return a


def kernel(**inputs):
    import numpy as _np
    import concourse.bacc as _bacc
    from concourse import mybir as _mybir
    from concourse.bass_utils import run_bass_kernel_spmd as _run

    nc=_bacc.Bacc("TRN2", target_bir_lowering=False, num_devices=1)
    arrays,args={},{}
    for name,v in laid_out({k: _np.asarray(v) for k,v in inputs.items()}).items():
        arrays[f"in_{name}"]=v
        args[name]=nc.dram_tensor(f"in_{name}",v.shape,_mybir.dt.from_np(v.dtype),kind="ExternalInput").ap()
    out=nc.dram_tensor("out_x",(P,NODES),_mybir.dt.float32,kind="ExternalOutput").ap()
    build(nc,args,out)
    r=_run(nc,[arrays],core_ids=[0])
    got=r.results[0]["out_x"]
    return _np.ascontiguousarray(got.reshape(P,B,W,W).transpose(1,0,2,3))
```
